# Optimizing a Trainium2 kernel written in Bass

```python
import numpy as np
import jax
import jax.numpy as jnp

def _softmax(x, axis=-1):
    return jax.nn.softmax(x, axis=axis)

def _gelu(x):
    return jax.nn.gelu(x, approximate=True)

def _silu(x):
    return jax.nn.silu(x)

def _sigmoid(x):
    return jax.nn.sigmoid(x)

def _layernorm(x, axis=-1, eps=1e-05):
    m = jnp.mean(x, axis=axis, keepdims=True)
    v = jnp.var(x, axis=axis, keepdims=True)
    return (x - m) / jnp.sqrt(v + eps)

def _scatter_add(tgt, idx, src, axis=0):
    return tgt.at[idx].add(src)

def _segment_sum(src, seg, n):
    return jax.ops.segment_sum(src, seg, n)
kernel_name = 'mk_sandwich_d1_jaxref_r4_e6cff5'

def setup_inputs(seed: int=0):
    np.random.seed(seed)
    _w = jnp.asarray

    def _L0_attn_setup():
        import math
        import jax, jax.numpy as jnp
        import numpy as np
        A = 256
        H = 16
        HS = A // H
        M = 64
        ITERS = 6

        def split_heads(t):
            B, L, _ = t.shape
            return t.reshape(B, L, H, HS).transpose(0, 2, 1, 3)

        def moore_penrose_pinv(x, num_iter):
            abs_x = jnp.abs(x)
            col = abs_x.sum(axis=-1).max(axis=-1)
            row = abs_x.sum(axis=-2).max(axis=-1)
            z = jnp.swapaxes(x, -1, -2) / (col * row)[..., None, None]
            I = jnp.eye(x.shape[-1], dtype=x.dtype)
            for _ in range(num_iter):
                xz = x @ z
                z = 0.25 * z @ (13.0 * I - xz @ (15.0 * I - xz @ (7.0 * I - xz)))
            return z
        key = jax.random.key(seed)
        ks = jax.random.split(key, 6)
        x = jax.random.normal(ks[0], (4, 1024, A), dtype=jnp.float32)
        s = 1.0 / math.sqrt(A)
        Wk = jax.random.normal(ks[1], (A, A), dtype=jnp.float32) * s
        Wq = jax.random.normal(ks[2], (A, A), dtype=jnp.float32) * s
        Wv = jax.random.normal(ks[3], (A, A), dtype=jnp.float32) * s
        Wo = jax.random.normal(ks[4], (A, A), dtype=jnp.float32) * s
        bo = jnp.zeros((A,), dtype=jnp.float32)
        return {'x': x, 'Wk': Wk, 'Wq': Wq, 'Wv': Wv, 'Wo': Wo, 'bo': bo}
    _L0_attn_in = _L0_attn_setup()

    def _L0_ffn_setup():
        import jax, jax.numpy as jnp
        import numpy as np
        DIM = 256

        def _reference_tuple_inner(x, W_r, W_k, W_v, mu_r, mu_k):
            B, T, C = x.shape
            x_prev = jnp.concatenate([jnp.zeros((B, 1, C), x.dtype), x[:, :-1, :]], axis=1)
            xr = mu_r * x + (1.0 - mu_r) * x_prev
            xk = mu_k * x + (1.0 - mu_k) * x_prev
            r = jax.nn.sigmoid(jnp.einsum('btc,dc->btd', xr, W_r))
            k = jnp.einsum('btc,dc->btd', xk, W_k)
            k_act = jnp.square(jax.nn.relu(k))
            out = r * jnp.einsum('btc,dc->btd', k_act, W_v)
            new_state = x[:, -1, :]
            return (out, new_state)
        key = jax.random.key(seed)
        ks = jax.random.split(key, 6)
        B, T, C = (8, 512, DIM)
        x = jax.random.normal(ks[0], (B, T, C), dtype=jnp.float32)
        s = 1.0 / np.sqrt(C)
        W_r = jax.random.uniform(ks[1], (C, C), jnp.float32, -s, s)
        W_k = jax.random.uniform(ks[2], (C, C), jnp.float32, -s, s)
        W_v = jax.random.uniform(ks[3], (C, C), jnp.float32, -s, s)
        mu_r = jax.random.uniform(ks[4], (C,), jnp.float32)
        mu_k = jax.random.uniform(ks[5], (C,), jnp.float32)
        return {'x': x, 'W_r': W_r, 'W_k': W_k, 'W_v': W_v, 'mu_r': mu_r, 'mu_k': mu_k}
    _L0_ffn_in = _L0_ffn_setup()
    _d = {'L0_attn_x': _L0_attn_in['x'], 'L0_attn_Wk': _L0_attn_in['Wk'], 'L0_attn_Wq': _L0_attn_in['Wq'], 'L0_attn_Wv': _L0_attn_in['Wv'], 'L0_attn_Wo': _L0_attn_in['Wo'], 'L0_attn_bo': _L0_attn_in['bo'], 'L0_ffn_W_r': _L0_ffn_in['W_r'], 'L0_ffn_W_k': _L0_ffn_in['W_k'], 'L0_ffn_W_v': _L0_ffn_in['W_v'], 'L0_ffn_mu_r': _L0_ffn_in['mu_r'], 'L0_ffn_mu_k': _L0_ffn_in['mu_k']}
    _x0 = _d['L0_attn_x']
    _d['L0_attn_x'] = jax.random.normal(jax.random.fold_in(jax.random.key(seed), 1), (8, 2048, 256), dtype=_x0.dtype)
    del _x0
    return _d

def reference(L0_attn_x, L0_attn_Wk, L0_attn_Wq, L0_attn_Wv, L0_attn_Wo, L0_attn_bo, L0_ffn_W_r, L0_ffn_W_k, L0_ffn_W_v, L0_ffn_mu_r, L0_ffn_mu_k):

    def _L0_attn_ref(x, Wk, Wq, Wv, Wo, bo):
        import math
        import jax, jax.numpy as jnp
        import numpy as np
        A = 256
        H = 16
        HS = A // H
        M = 64
        ITERS = 6

        def split_heads(t):
            B, L, _ = t.shape
            return t.reshape(B, L, H, HS).transpose(0, 2, 1, 3)

        def moore_penrose_pinv(x, num_iter):
            abs_x = jnp.abs(x)
            col = abs_x.sum(axis=-1).max(axis=-1)
            row = abs_x.sum(axis=-2).max(axis=-1)
            z = jnp.swapaxes(x, -1, -2) / (col * row)[..., None, None]
            I = jnp.eye(x.shape[-1], dtype=x.dtype)
            for _ in range(num_iter):
                xz = x @ z
                z = 0.25 * z @ (13.0 * I - xz @ (15.0 * I - xz @ (7.0 * I - xz)))
            return z
        B, L, _ = x.shape
        k = split_heads(x @ Wk)
        q = split_heads(x @ Wq)
        v = split_heads(x @ Wv)
        q = q / math.sqrt(HS)
        denom = L // M
        q_l = q.reshape(B, H, M, denom, HS).sum(axis=-2) / denom
        k_l = k.reshape(B, H, M, denom, HS).sum(axis=-2) / denom
        s1 = jax.nn.softmax(jnp.einsum('bhld,bhmd->bhlm', q, k_l), axis=-1)
        s2 = jax.nn.softmax(jnp.einsum('bhmd,bhnd->bhmn', q_l, k_l), axis=-1)
        s3 = jax.nn.softmax(jnp.einsum('bhmd,bhld->bhml', q_l, k), axis=-1)
        z_star = moore_penrose_pinv(s2, ITERS)
        out = s1 @ (z_star @ (s3 @ v))
        out = out.transpose(0, 2, 1, 3).reshape(B, L, A)
        return out @ Wo + bo

    def _L0_ffn_ref(x, W_r, W_k, W_v, mu_r, mu_k):
        import jax, jax.numpy as jnp
        import numpy as np
        DIM = 256

        def _reference_tuple_inner(x, W_r, W_k, W_v, mu_r, mu_k):
            B, T, C = x.shape
            x_prev = jnp.concatenate([jnp.zeros((B, 1, C), x.dtype), x[:, :-1, :]], axis=1)
            xr = mu_r * x + (1.0 - mu_r) * x_prev
            xk = mu_k * x + (1.0 - mu_k) * x_prev
            r = jax.nn.sigmoid(jnp.einsum('btc,dc->btd', xr, W_r))
            k = jnp.einsum('btc,dc->btd', xk, W_k)
            k_act = jnp.square(jax.nn.relu(k))
            out = r * jnp.einsum('btc,dc->btd', k_act, W_v)
            new_state = x[:, -1, :]
            return (out, new_state)
        return _reference_tuple_inner(x, W_r, W_k, W_v, mu_r, mu_k)[0]
    x = L0_attn_x
    x = x + _layernorm(_L0_attn_ref(_layernorm(x, axis=-1), L0_attn_Wk, L0_attn_Wq, L0_attn_Wv, L0_attn_Wo, L0_attn_bo), axis=-1)
    x = x + _layernorm(_L0_ffn_ref(_layernorm(x, axis=-1), L0_ffn_W_r, L0_ffn_W_k, L0_ffn_W_v, L0_ffn_mu_r, L0_ffn_mu_k), axis=-1)
    return x

_drawn_inputs = setup_inputs


def setup_inputs(seed=0):
    import zlib

    import numpy as np

    out = dict(_drawn_inputs(seed))
    spreads = {'L0_attn_bo': (0.0, 0.1)}
    factors = {}
    for name, (base, spread) in spreads.items():
        noise = np.random.default_rng([zlib.crc32(name.encode()), seed]).standard_normal(out[name].shape)
        drawn = base * np.exp(spread * noise) if base else spread * noise
        out[name] = jnp.asarray(drawn.astype(out[name].dtype))
    for name, factor in factors.items():
        out[name] = (out[name] * factor).astype(out[name].dtype)
    return out
```

```python
from contextlib import ExitStack

import concourse.bass as bass
from concourse import mybir

F32 = mybir.dt.float32
F16 = mybir.dt.float16
ALU = mybir.AluOpType
ACT = mybir.ActivationFunctionType
AX = mybir.AxisListType

P = 128
HALF = P // 2


def sandwich(nc, x, Wk, Wq, Wv, Wo, bo, W_r, W_k, W_v, mu_r, mu_k, out):
    B, L, A = x.shape
    H, HS, M, ITERS = 16, 16, 64, 6
    KB = A // P
    HB = H // KB
    PAIRS, PB = H // 2, H // 2 // KB
    CH = 512
    NC, NT = L // CH, CH // P
    DEN = L // M
    TM = P // DEN
    EPS = 1e-5
    QSCALE = HS ** -0.5
    assert HS * HB == P and M == HALF and NC == 4 and NT == 4

    ctx = ExitStack()
    with ctx:
        def sb(name, shape, dt=F32, c=ctx):
            return c.enter_context(nc.sbuf_tensor(name, shape, dt))

        def sem(name):
            return ctx.enter_context(nc.semaphore(name))

        bank = [ctx.enter_context(nc.psum_tensor(f"bank{i}", [P, 512], F32)) for i in range(2)]
        wide = [ctx.enter_context(nc.psum_tensor(f"wide{i}", [P, 1024], F32)) for i in range(2)]
        acc = [ctx.enter_context(nc.psum_tensor(f"acc{i}", [P, 512], F32)) for i in range(2)]

        lm_dram = nc.dram_tensor("landmarks", [B, P, 4 * KB * M], F16).ap()
        zt_dram = nc.dram_tensor("inverse", [B, P, PAIRS * M], F32).ap()

        ident = sb("ident", [P, P])
        pool_w = sb("pool_w", [P, 2 * M - TM])
        head_mask = sb("head_mask", [P, HB])
        ones_pair = sb("ones_pair", [P, 2 * HS])
        ones32 = sb("ones32", [P, 32])
        ones4 = sb("ones4", [P, P], F16)
        neg_sel = sb("neg_sel", [P, PAIRS, P], F16)
        eye = sb("eye", [P, M])
        eye7 = sb("eye7", [P, M])
        eye15 = sb("eye15", [P, M])
        eye13 = sb("eye13", [P, M])
        wq = sb("wq", [P, KB, A])
        wk = sb("wk", [P, KB, A])
        wv = sb("wv", [P, KB, A])
        wo = sb("wo", [P, KB, A])
        wrT = sb("wrT", [P, KB, A])
        wkT = sb("wkT", [P, KB, A])
        wvT = sb("wvT", [P, KB, A])
        bo_all = sb("bo_all", [P, A])
        mu = sb("mu", [P, 2, KB])

        const_made = sem("const_made")
        weights_in = sem("weights_in")
        eyes_made = sem("eyes_made")
        wT_full = sem("wT_full")
        wT_drained = sem("wT_drained")
        NCONST = 17
        NW = 7 + 1 + 2

        part1 = ctx.enter_context(ExitStack())
        S2 = range(2)
        x1in = [sb(f"x1in{s}", [P, NC, NT, A], c=part1) for s in range(1)]
        wnat = sb("wnat", [P, 3, KB, A], c=part1)
        st1 = sb("st1", [P, NC, NT, 6], c=part1)
        mv1 = sb("mv1", [P, NC, NT, 2], c=part1)
        ln1 = sb("ln1", [P, NC, NT], c=part1)
        rstd1 = sb("rstd1", [P, NC, NT], c=part1)
        xl = [sb(f"xl{s}", [M, A], c=part1) for s in S2]
        xlT = [sb(f"xlT{s}", [P, KB, M], c=part1) for s in S2]
        qlT = [sb(f"qlT{s}", [P, 2, KB, M], c=part1) for s in S2]
        lm16 = [sb(f"lm16{s}", [P, 4, KB, M], F16, c=part1) for s in S2]
        qbd = [sb(f"qbd{s}", [P, KB, HB, M], c=part1) for s in S2]
        X = [sb(f"X{s}", [P, PAIRS, M], c=part1) for s in S2]
        XT = [sb(f"XT{s}", [P, PAIRS, M], c=part1) for s in S2]
        mx = [sb(f"mx{s}", [P, PAIRS], c=part1) for s in S2]
        rsum1 = [sb(f"rsum1{s}", [P, PAIRS], c=part1) for s in S2]
        rcp1 = [sb(f"rcp1{s}", [P, PAIRS], c=part1) for s in S2]
        rc1 = [sb(f"rc1{s}", [P, 2, PAIRS], c=part1) for s in S2]
        cm = [sb(f"cm{s}", [PAIRS, 2, 2], c=part1) for s in S2]
        cg = [sb(f"cg{s}", [PAIRS, 2, 2], c=part1) for s in S2]
        gb = [sb(f"gb{s}", [PAIRS, 2, M], c=part1) for s in S2]
        gcol = [sb(f"gcol{s}", [P, PAIRS], c=part1) for s in S2]
        Z = [sb(f"Z{s}", [P, PAIRS, M], c=part1) for s in S2]
        ZT = [sb(f"ZT{s}", [P, PAIRS, M], c=part1) for s in S2]
        SS = [sb(f"SS{s}", [P, PAIRS, M], c=part1) for s in S2]
        T1 = [sb(f"T1{s}", [P, PAIRS, M], c=part1) for s in S2]
        T2 = [sb(f"T2{s}", [P, PAIRS, M], c=part1) for s in S2]
        T3 = [sb(f"T3{s}", [P, PAIRS, M], c=part1) for s in S2]
        pb = [[bank[0], wide[0][:, 0:512], wide[0][:, 512:1024]],
              [bank[1], wide[1][:, 0:512], wide[1][:, 512:1024]]]
        pb = [[t[:, :] for t in row] for row in pb]

        p_in = [sem(f"p_in{c}") for c in range(NC)]
        p_stats = sem("p_stats")
        p_mv = sem("p_mv")
        p_ln = sem("p_ln")
        p_rstd = sem("p_rstd")
        p_hat = sem("p_hat")
        p_pe = sem("p_pe")
        p_pooled = sem("p_pooled")
        p_act = sem("p_act")
        p_dve = sem("p_dve")
        lm_out = sem("lm_out")
        zt_out = sem("zt_out")

        LIN = ["pooled", "lT", "qk", "logits", "XT", "sums", "g"]
        ITER = ["S", "ST1", "ST2", "Z", "ZT"]

        def order(first, each, last=()):
            return ([(n, s) for s in S2 for n in first]
                    + [(n, i, s) for i in range(ITERS) for s in S2 for n in each]
                    + [(n, s) for s in S2 for n in last])

        pe_steps = order(LIN, ITER)
        pe_steps = [k for k in pe_steps if k[0] != "Z" or k[1] < ITERS - 1]
        act_steps = order(["xl", "xlT", "ql", "kl", "lm", "exp", "XT"], ["S", "Z"])
        act_steps = [k for k in act_steps if k[0] != "Z" or k[1] < ITERS - 1]
        dve_steps = order(["lmlo", "qbd", "max", "shift", "sum", "rcp", "X", "rs", "cs", "cm", "cg", "cr",
                           "gb", "gcol", "ZT", "Z"], ["T1", "T2", "T3", "ZT"])

        def of(steps, i, *key):
            return i * len(steps) + steps.index(key) + 1

        part2 = ctx.enter_context(ExitStack())
        block = ctx.enter_context(nc.Block())

        part1.close()
        xin = [sb(f"xin{i}", [P, NT, A], c=part2) for i in range(2)]
        xhat = [sb(f"xhat{i}", [P, NT, A], c=part2) for i in range(2)]
        xT = sb("xT", [P, KB, CH], c=part2)
        qh = sb("qh", [P, KB, L], F16, c=part2)
        ql = sb("ql", [P, KB, L], F16, c=part2)
        kh = sb("kh", [P, KB, L], F16, c=part2)
        kl = sb("kl", [P, KB, L], F16, c=part2)
        vv = sb("vv", [P, L // P, A], c=part2)
        m3 = sb("m3", [P, PAIRS, NC], c=part2)
        m3m = sb("m3m", [P, PAIRS], c=part2)
        nmax = sb("nmax", [P, KB, PB, P], F16, c=part2)
        m1 = sb("m1", [P, L // P, H], c=part2)
        m1T = sb("m1T", [P, CH], F16, c=part2)
        q_bd = sb("q_bd", [P, 2, KB, HB, M], F16, c=part2)
        kA_bd = sb("kA_bd", [P, 1, KB, HB, M], F16, c=part2)
        kE_bd = sb("kE_bd", [P, 2, KB, HB, M], F16, c=part2)
        e3 = [sb(f"e3{i}", [P, 2 * 512], c=part2) for i in range(2)]
        uT = sb("uT", [P, KB * P], c=part2)
        rs3 = sb("rs3", [P, 256], c=part2)
        rr3 = sb("rr3", [P, PAIRS], c=part2)
        un = sb("un", [P, PAIRS, HS], c=part2)
        zt = sb("zt", [P, PAIRS, M], c=part2)
        wbd = sb("wbd", [P, PAIRS, 2, HS], c=part2)
        p1 = sb("p1", [P, PAIRS, CH], c=part2)
        rc = sb("rc", [P, KB, CH], c=part2)
        oT = sb("oT", [P, KB, CH], c=part2)
        yy = sb("yy", [P, NT, A], c=part2)
        xres = [sb(f"xres{i}", [P, NT, A], c=part2) for i in range(2)]
        xm = [sb(f"xm{i}", [P, NT, A], c=part2) for i in range(3)]
        x2h = sb("x2h", [P, NT, A], c=part2)
        x2T = [sb(f"x2T{i}", [P, KB, CH + 1], c=part2) for i in range(2)]
        dx = sb("dx", [P, KB, CH], c=part2)
        xrT = sb("xrT", [P, KB, CH], c=part2)
        xkT = sb("xkT", [P, KB, CH], c=part2)
        sg = sb("sg", [P, NT, A], c=part2)

        ka = sb("ka", [P, KB, CH], c=part2)
        ob = [sb(f"ob{i}", [P, NT, A], c=part2) for i in range(2)]

        held = {e: sem(f"held_{n}") for e, n in ((nc.sync.engine, "sp"), (nc.vector.engine, "dve"), (nc.gpsimd.engine, "pool"), (nc.tensor.engine, "pe"))}

        def hold(eng):
            eng.sem_inc(held[eng.engine], 1)

        class Norm:

            def __init__(self, name, copies=1):
                self.st = sb(name + "_st", [P, NT, 6], c=part2)
                self.mv = [sb(f"{name}_mv{i}", [P, NT, 2], c=part2) for i in range(copies)]
                self.ln = sb(name + "_ln", [P, NT], c=part2)
                self.rstd = [sb(f"{name}_rstd{i}", [P, NT], c=part2) for i in range(copies)]
                self.stats_made = sem(name + "_stats")
                self.mv_made = sem(name + "_mv")
                self.ln_made = sem(name + "_ln")
                self.rstd_made = sem(name + "_rstd")
                self.applied = sem(name + "_applied")
                self.copies = copies

            def stats(self, dve, src, g, c):
                dve.wait_ge(self.mv_made, g)
                for t in range(NT):
                    ins = nc.vector.bn_stats(self.st[:, t, :], src[:, t, :])
                ins.then_inc(self.stats_made, 1)
                dve.wait_ge(self.stats_made, g + 1)
                hold(dve)
                for t in range(NT):
                    ins = nc.vector.bn_aggr(self.mv[c % self.copies][:, t, :], self.st[:, t, :])
                ins.then_inc(self.mv_made, 1)

            def root(self, act, g, c):
                act.wait_ge(self.rstd_made, g)
                act.wait_ge(self.mv_made, g + 1)
                nc.scalar.activation(self.ln[:, :], self.mv[c % self.copies][:, :, 1], ACT.Ln,
                                     bias=EPS).then_inc(self.ln_made, 1)
                act.wait_ge(self.ln_made, g + 1)
                nc.scalar.activation(self.rstd[c % self.copies][:, :], self.ln[:, :], ACT.Exp,
                                     scale=-0.5).then_inc(self.rstd_made, 1)

            def apply(self, pool, dst, src, g, c):
                pool.wait_ge(self.rstd_made, g + 1)
                hold(pool)
                k = c % self.copies
                for t in range(NT):
                    ins = nc.gpsimd.tensor_scalar(dst[:, t, :], src[:, t, :], self.mv[k][:, t, 0:1],
                                                  self.rstd[k][:, t:t + 1], ALU.subtract, ALU.mult)
                ins.then_inc(self.applied, 1)

        norm_x = Norm("norm_x", 2)
        norm_y = Norm("norm_y")
        norm_m = Norm("norm_m")
        norm_f = Norm("norm_f")

        setup2 = sem("setup2")
        x_in = [sem(f"x_in{i}") for i in range(2)]
        xhat_read = sem("xhat_read")
        bank_full = [sem(f"bank{i}_full") for i in range(2)]
        bank_drained = [sem(f"bank{i}_drained") for i in range(2)]
        wide_full = [sem(f"wide{i}_full") for i in range(2)]
        wide_drained = [sem(f"wide{i}_drained") for i in range(2)]
        acc_full = [sem(f"acc{i}_full") for i in range(2)]
        acc_drained = [sem(f"acc{i}_drained") for i in range(2)]
        q_hi = sem("q_hi")
        k_hi = sem("k_hi")
        m3_max = sem("m3_max")
        q_bd_in = sem("q_bd_in")
        kA_bd_in = sem("kA_bd_in")
        kE_bd_in = sem("kE_bd_in")
        zt_in = sem("zt_in")
        q_bd_free = sem("q_bd_free")
        zt_free = sem("zt_free")
        k_bd_free = sem("k_bd_free")
        e3_made = sem("e3_made")
        e3_read = sem("e3_read")
        rr_made = sem("rr_made")
        un_made = sem("un_made")
        wbd_made = sem("wbd_made")
        rc_ln = sem("rc_ln")
        rc_made = sem("rc_made")
        oT_made = sem("oT_made")
        res_in = [sem(f"res_in{i}") for i in range(2)]
        xm_made = sem("xm_made")
        x2h_read = sem("x2h_read")
        carry = sem("carry")
        dx_made = sem("dx_made")
        xr_made = sem("xr_made")
        xk_scaled = sem("xk_scaled")
        xk_made = sem("xk_made")
        sg_ln = sem("sg_ln")
        sg_exp = sem("sg_exp")
        sg_made = sem("sg_made")
        kr_made = sem("kr_made")
        ka_made = sem("ka_made")
        fin_made = sem("fin_made")
        fin_out = [sem(f"fin_out{i}") for i in range(2)]

        PRO = [("X", 0), ("X", 1), ("A", 0), ("X", 2), ("A", 1), ("X", 3), ("A", 2), ("A", 3)]
        BODY = [("M", 0), ("F", 0), ("E", 0), ("X", 0), ("W", 0), ("X", 1), ("A", 0), ("H", 0), ("O", 0),
                ("E", 1), ("N", 0), ("X", 2), ("A", 1), ("T", 0), ("H", 1), ("O", 1), ("G1", 0),
                ("E", 2), ("N", 1), ("X", 3), ("A", 2), ("G2", 0), ("T", 1), ("H", 2), ("O", 2), ("G1", 1),
                ("E", 3), ("N", 2), ("A", 3), ("G2", 1), ("T", 2), ("H", 3), ("O", 3), ("G1", 2),
                ("N", 3), ("G2", 2), ("T", 3), ("G1", 3), ("G2", 3)]
        LAST = [k for k in BODY if k[0] not in "XA"]
        USES = {"X": (0, 0, 0), "N": (0, 0, 0), "A": (4, 4, 0), "M": (1, 0, 0), "F": (0, 8, 1), "W": (2, 0, 0),
                "E": (1, 2, 0), "H": (1, 0, 1), "O": (1, 0, 0), "T": (1, 0, 0), "G1": (2, 0, 0),
                "G2": (1, 0, 0)}

        class Use:

            def __init__(self, counts):
                self.bank, self.wide, self.acc = counts

        def uses(stages, start):
            at, n = {}, list(start)
            for key in stages:
                at[key] = Use(n)
                n = [a + b for a, b in zip(n, USES[key[0]])]
            return at, n

        _, pro_n = uses(PRO, (0, 0, 0))
        _, body_n = uses(BODY, (0, 0, 0))

        def part2_program(eng, stage):
            at, _ = uses(PRO, (0, 0, 0))
            for key in PRO:
                if key[0] in stage:
                    stage[key[0]](at, 0, key[1])
            with eng.Fori(0, B - 1) as b:
                base = [p + b * n for p, n in zip(pro_n, body_n)]
                at, _ = uses(BODY, base)
                for key in BODY:
                    if key[0] in stage:
                        stage[key[0]](at, b + 1 if key[0] in "XA" else b, key[1])
            base = [p + (B - 1) * n for p, n in zip(pro_n, body_n)]
            at, _ = uses(LAST, base)
            for key in LAST:
                if key[0] in stage:
                    stage[key[0]](at, B - 1, key[1])

        def older(b, c):
            return b * NC + max(c - 1, 0)

        @block.sync
        def _(sp):
            for w, (dst, src) in enumerate([(wq, Wq), (wk, Wk), (wv, Wv), (wo, Wo)]):
                sp.dma_start(dst[:, :, :], src.rearrange("(k p) n -> p k n", p=P)).then_inc(weights_in, 16)
            for w, src in enumerate([W_r, W_k, W_v]):
                sp.dma_start(wnat[:, w, :, :], src.rearrange("(k p) n -> p k n", p=P)).then_inc(weights_in, 16)
            sp.dma_start(bo_all[:, :], bo.rearrange("(a n) -> a n", a=1).to_broadcast([P, A])).then_inc(weights_in, 16)
            for w, src in enumerate([mu_r, mu_k]):
                sp.dma_start(mu[:, w, :], src.rearrange("(k p) -> p k", p=P),
                             allow_slow_non_contiguous=True).then_inc(weights_in, 16)

            with sp.Fori(0, B // 2) as i:
                for s in S2:
                    n = i * 2 + s
                    sp.wait_ge(p_hat, n * NC)
                    sp.wait_ge(p_pooled, n)
                    for c in range(NC):
                        src = x[bass.ds(n, 1), c * CH:(c + 1) * CH, :].rearrange("a (t p) n -> p (a t) n", p=P)
                        sp.dma_start(x1in[0][:, c, :, :], src).then_inc(p_in[c], 16)
                for s in S2:
                    n = i * 2 + s
                    sp.wait_ge(p_dve, of(dve_steps, i, "lmlo", s))
                    hold(sp)
                    sp.dma_start(lm_dram[bass.ds(n, 1)].rearrange("a p n -> p (a n)"),
                                 lm16[s][:, :, :, :].rearrange("p a k m -> p (a k m)")).then_inc(lm_out, 16)
                for s in S2:
                    n = i * 2 + s
                    sp.wait_ge(p_dve, of(dve_steps, i, "ZT", ITERS - 1, s))
                    hold(sp)
                    sp.dma_start(zt_dram[bass.ds(n, 1)].rearrange("a p n -> p (a n)"),
                                 ZT[s][:, :, :].rearrange("p a m -> p (a m)")).then_inc(zt_out, 16)
            sp.wait_ge(lm_out, 16 * B)
            sp.wait_ge(zt_out, 16 * B)
            sp.wait_ge(p_pe, len(pe_steps) * B // 2)
            sp.wait_ge(setup2, 6)

            def load_bd(dst, lo, key, b, done):
                n = 2 if lo else 1
                src = lm_dram[bass.ds(b, 1)].rearrange("a p (t w k m) -> p (a t) w k m", t=2, w=2, k=KB)
                for h in range(HB):
                    r = slice(h * HS, (h + 1) * HS)
                    for t in range(n):
                        sp.dma_start(dst[r, t, :, h, :], src[r, t, key, :, :]).then_inc(done, 16)

            def stage_X(at, b, c):
                if c == 0:
                    sp.wait_ge(k_bd_free, b - 1) if not isinstance(b, int) else None
                    if not isinstance(b, int):
                        sp.wait_ge(wide_full[1], pro_n[1])
                    load_bd(kA_bd, False, 1, b, kA_bd_in)
                    if isinstance(b, int):
                        load_bd(q_bd, True, 0, b, q_bd_in)
                if not (isinstance(b, int) and c < 2):
                    sp.wait_ge(norm_x.applied, b * NC + c - 1)
                    hold(sp)
                src = x[bass.ds(b, 1), c * CH:(c + 1) * CH, :].rearrange("a (t p) n -> p (a t) n", p=P)
                sp.dma_start(xin[c % 2][:, :, :], src).then_inc(x_in[c % 2], 16)

            def stage_F(at, b, c):
                sp.wait_ge(k_bd_free, b)
                hold(sp)
                load_bd(kE_bd, True, 1, b, kE_bd_in)
                sp.wait_ge(zt_free, b)
                hold(sp)
                sp.dma_start(zt[:, :, :].rearrange("p a m -> p (a m)"),
                             zt_dram[bass.ds(b, 1)].rearrange("a p n -> p (a n)")).then_inc(zt_in, 16)

            def stage_W(at, b, c):
                if not isinstance(b, int):
                    sp.wait_ge(q_bd_free, b + 1)
                    hold(sp)
                    load_bd(q_bd, True, 0, b + 1, q_bd_in)

            def stage_E(at, b, c):
                sp.wait_ge(xm_made, older(b, c))
                hold(sp)
                src = x[bass.ds(b, 1), c * CH:(c + 1) * CH, :].rearrange("a (t p) n -> p (a t) n", p=P)
                sp.dma_start(xres[c % 2][:, :, :], src).then_inc(res_in[c % 2], 16)

            def stage_G2(at, b, c):
                sp.wait_ge(fin_made, b * NC + c + 1)
                hold(sp)
                dst = out[bass.ds(b, 1), c * CH:(c + 1) * CH, :].rearrange("a (t p) n -> p (a t) n", p=P)
                sp.dma_start(dst, ob[c % 2][:, :, :]).then_inc(fin_out[c % 2], 16)

            part2_program(sp, {"X": stage_X, "F": stage_F, "W": stage_W, "E": stage_E, "G2": stage_G2})
            for i in range(2):
                sp.wait_ge(fin_out[i], 16 * B * NC // 2)

        @block.gpsimd
        def _(pool):
            g = nc.gpsimd
            g.memset(ident[:, :], 0.0).then_inc(const_made, 1)
            g.memset(pool_w[:, :], 1.0 / DEN).then_inc(const_made, 1)
            g.memset(head_mask[:, :], 1.0).then_inc(const_made, 1)
            g.memset(ones_pair[:, :], 1.0).then_inc(const_made, 1)
            g.memset(ones32[:, :], 1.0).then_inc(const_made, 1)
            g.memset(neg_sel[:, :, :], 0.0).then_inc(const_made, 1)
            pool.wait_ge(const_made, 6)
            g.affine_select(out=ident[:, :], in_=ident[:, :], compare_op=ALU.not_equal, fill=1.0, base=0,
                            pattern=[[-1, P]], channel_multiplier=1).then_inc(const_made, 1)
            o = M - TM
            g.affine_select(out=pool_w[:, :], in_=pool_w[:, :], compare_op=ALU.is_ge, fill=0.0, base=DEN * o,
                            pattern=[[-DEN, 2 * M - TM]], channel_multiplier=1).then_inc(const_made, 1)
            pool.wait_ge(const_made, 8)
            g.affine_select(out=pool_w[:, :], in_=pool_w[:, :], compare_op=ALU.is_ge, fill=0.0,
                            base=DEN - 1 - DEN * o, pattern=[[DEN, 2 * M - TM]],
                            channel_multiplier=-1).then_inc(const_made, 1)
            g.affine_select(out=head_mask[:, :], in_=head_mask[:, :], compare_op=ALU.is_ge, fill=0.0, base=0,
                            pattern=[[-HS, HB]], channel_multiplier=1).then_inc(const_made, 1)
            pool.wait_ge(const_made, 10)
            g.affine_select(out=head_mask[:, :], in_=head_mask[:, :], compare_op=ALU.is_ge, fill=0.0,
                            base=HS - 1, pattern=[[HS, HB]], channel_multiplier=-1).then_inc(const_made, 1)
            op = ones_pair[:, :].rearrange("p (h d) -> p h d", h=2)
            g.affine_select(out=op, in_=op, compare_op=ALU.is_ge, fill=0.0, base=0,
                            pattern=[[-M, 2], [0, HS]], channel_multiplier=1).then_inc(const_made, 1)
            pool.wait_ge(const_made, 12)
            g.affine_select(out=op, in_=op, compare_op=ALU.is_ge, fill=0.0, base=M - 1,
                            pattern=[[M, 2], [0, HS]], channel_multiplier=-1).then_inc(const_made, 1)
            ns = neg_sel[:, :, :].rearrange("k p (j m) -> k p j m", j=2)
            g.affine_select(out=ns, in_=ns, compare_op=ALU.not_equal, fill=-1.0, base=0,
                            pattern=[[-2, PAIRS], [-1, 2], [0, M]], channel_multiplier=1).then_inc(const_made, 1)
            g.memset(ones4[:, :], 0.0).then_inc(const_made, 1)
            pool.wait_ge(const_made, 15)
            g.memset(ones4[0:PB, :], 1.0).then_inc(const_made, 1)
            pool.wait_ge(const_made, 7)
            g.tensor_tensor(eye[:, :], ident[:, 0:M], ident[:, M:P], ALU.add).then_inc(const_made, 1)

            with pool.Fori(0, B // 2) as i:
                for s in S2:
                    n = i * 2 + s
                    for c in range(NC):
                        pool.wait_ge(p_rstd, n * NC + c + 1)
                        hold(pool)
                        for t in range(NT):
                            ins = g.tensor_scalar(x1in[0][:, c, t, :], x1in[0][:, c, t, :],
                                                  mv1[:, c, t, 0:1], rstd1[:, c, t:t + 1],
                                                  ALU.subtract, ALU.mult)
                        ins.then_inc(p_hat, 1)

            pool.wait_ge(p_pe, len(pe_steps) * B // 2)
            pool.wait_ge(p_dve, len(dve_steps) * B // 2)
            pool.wait_ge(lm_out, 16 * B)
            pool.wait_ge(zt_out, 16 * B)
            g.memset(q_bd[:, :, :, :, :], 0.0).then_inc(setup2, 1)
            g.memset(kA_bd[:, :, :, :, :], 0.0).then_inc(setup2, 1)
            g.memset(kE_bd[:, :, :, :, :], 0.0).then_inc(setup2, 1)
            g.memset(wbd[:, :, :, :], 0.0).then_inc(setup2, 1)
            g.memset(nmax[:, :, :, :], 0.0).then_inc(setup2, 1)
            g.memset(m1T[:, :], 0.0).then_inc(setup2, 1)

            def stage_X(at, b, c):
                if not (isinstance(b, int) and c < 2):
                    pool.wait_ge(xhat_read, b * NC + c - 1)
                norm_x.apply(pool, xhat[c % 2], xin[c % 2], b * NC + c, c)

            def stage_O(at, b, c):
                n = b * NC + c
                norm_y.apply(pool, yy, yy, n, c)
                pool.wait_ge(res_in[c % 2], 16 * (b * 2 + c // 2 + 1))
                pool.wait_ge(norm_y.applied, n + 1)
                if c:
                    pool.wait_ge(fin_made, b * NC + max(c - 2, 0))
                else:
                    pool.wait_ge(fin_made, b * NC)
                g.tensor_tensor(xm[c % 3][:, :, :], yy[:, :, :], xres[c % 2][:, :, :],
                                ALU.add).then_inc(xm_made, 1)

            def stage_N(at, b, c):
                n = b * NC + c
                pool.wait_ge(x2h_read, n)
                norm_m.apply(pool, x2h, xm[c % 3], n, c)

            def stage_T(at, b, c):
                n = b * NC + c
                pool.wait_ge(dx_made, n + 1)
                hold(pool)
                for k in range(KB):
                    ins = g.tensor_scalar(xkT[:, k, :], dx[:, k, :], mu[:, 1, k:k + 1], None, ALU.mult)
                ins.then_inc(xk_scaled, 1)
                pool.wait_ge(xk_scaled, n + 1)
                g.tensor_tensor(xkT[:, :, :], xkT[:, :, :], x2T[c % 2][:, :, 0:CH], ALU.add).then_inc(xk_made, 1)

            def stage_G2(at, b, c):
                n = b * NC + c
                norm_f.apply(pool, ob[c % 2], ob[c % 2], n, c)
                pool.wait_ge(norm_f.applied, n + 1)
                g.tensor_tensor(ob[c % 2][:, :, :], ob[c % 2][:, :, :], xm[c % 3][:, :, :],
                                ALU.add).then_inc(fin_made, 1)

            part2_program(pool, {"X": stage_X, "O": stage_O, "N": stage_N, "T": stage_T, "G2": stage_G2})

        @block.scalar
        def _(act):
            sc = nc.scalar
            nc.scalar.preload_act_table_set("natural_log_exp_and_others")
            for w, dst in enumerate([wrT, wkT, wvT]):
                act.wait_ge(wT_full, w + 1)
                sc.activation(dst[:, :, :], wide[w % 2][:, 0:KB * A].rearrange("p (k n) -> p k n", k=KB),
                              ACT.Copy).then_inc(wT_drained, 1)
            with act.Fori(0, B // 2) as i:
                for s in S2:
                    n = i * 2 + s
                    for c in range(NC):
                        act.wait_ge(p_mv, n * NC + c + 1)
                        sc.activation(ln1[:, c, :], mv1[:, c, :, 1], ACT.Ln, bias=EPS).then_inc(p_ln, 1)
                        act.wait_ge(p_ln, n * NC + c + 1)
                        sc.activation(rstd1[:, c, :], ln1[:, c, :], ACT.Exp, scale=-0.5).then_inc(p_rstd, 1)
                    act.wait_ge(p_pe, of(pe_steps, i, "pooled", s))
                    sc.activation(xl[s][:, :], pb[s][0][0:M, 0:A], ACT.Copy).then_inc(p_act, 1)
                    act.wait_ge(p_pe, of(pe_steps, i, "lT", s))
                    sc.activation(xlT[s][:, :, :], pb[s][1][:, 0:KB * M].rearrange("p (k m) -> p k m", k=KB),
                                  ACT.Copy).then_inc(p_act, 1)
                    act.wait_ge(p_pe, of(pe_steps, i, "qk", s))
                    qk = pb[s][2][:, 0:2 * KB * M].rearrange("p (a k m) -> p a k m", a=2, k=KB)
                    sc.activation(qlT[s][:, 0, :, :], qk[:, 0, :, :], ACT.Copy, scale=QSCALE).then_inc(p_act, 1)
                    sc.activation(qlT[s][:, 1, :, :], qk[:, 1, :, :], ACT.Copy).then_inc(p_act, 1)
                    act.wait_ge(p_act, of(act_steps, i, "kl", s))
                    act.wait_ge(lm_out, 32 * i)
                    sc.activation(lm16[s][:, 0:2, :, :], qlT[s][:, :, :, :], ACT.Copy).then_inc(p_act, 1)
                    act.wait_ge(p_dve, of(dve_steps, i, "shift", s))
                    sc.activation(X[s][:, :, :], X[s][:, :, :], ACT.Exp).then_inc(p_act, 1)
                    act.wait_ge(p_pe, of(pe_steps, i, "XT", s))
                    sc.activation(XT[s][:, :, :], pb[s][1].rearrange("p (a m) -> p a m", a=PAIRS),
                                  ACT.Copy).then_inc(p_act, 1)
                for it in range(ITERS):
                    for s in S2:
                        b0 = pb[s][0].rearrange("p (a m) -> p a m", a=PAIRS)
                        b1 = pb[s][1].rearrange("p (a m) -> p a m", a=PAIRS)
                        act.wait_ge(p_pe, of(pe_steps, i, "S", it, s))
                        sc.activation(SS[s][:, :, :], b0, ACT.Copy).then_inc(p_act, 1)
                        if it < ITERS - 1:
                            act.wait_ge(p_pe, of(pe_steps, i, "Z", it, s))
                            sc.activation(Z[s][:, :, :], b1, ACT.Copy, scale=0.25).then_inc(p_act, 1)

            act.wait_ge(p_pe, len(pe_steps) * B // 2)
            act.wait_ge(p_dve, len(dve_steps) * B // 2)
            act.wait_ge(p_hat, NC * B)
            act.wait_ge(lm_out, 16 * B)
            act.wait_ge(zt_out, 16 * B)

            def stage_X(at, b, c):
                if not (isinstance(b, int) and c < 2):
                    act.wait_ge(norm_x.applied, b * NC + c - 1)
                norm_x.root(act, b * NC + c, c)

            def stage_A(at, b, c):
                u = at["A", c].bank
                span = slice(c * CH, (c + 1) * CH)
                for k in range(KB):
                    act.wait_ge(bank_full[k], u + 1)
                    sc.activation(xT[:, k, :], bank[k][:, :], ACT.Copy).then_inc(bank_drained[k], 1)
                for k in range(KB):
                    act.wait_ge(bank_full[k], u + 2)
                    sc.activation(qh[:, k, span], bank[k][:, :], ACT.Copy, scale=QSCALE).then_inc(q_hi, 1)
                for k in range(KB):
                    act.wait_ge(bank_full[k], u + 3)
                    sc.activation(kh[:, k, span], bank[k][:, :], ACT.Copy).then_inc(k_hi, 1)

            def stage_F(at, b, c):
                u = at["F", 0].wide
                for t in range(NC * NT):
                    act.wait_ge(wide_full[t % 2], u + t // 2 + 1)
                    if t >= 2:
                        act.wait_ge(e3_read, b * (NC * NT - 1) + t - 1)
                    sc.activation(e3[t % 2][:, :], wide[t % 2][:, :], ACT.Exp).then_inc(wide_drained[t % 2], 1)

            def stage_W(at, b, c):
                u, a = at["W", 0].bank, at["F", 0].acc
                act.wait_ge(acc_full[0], a + 1)
                sc.activation(uT[:, :], acc[0][:, 0:KB * P], ACT.Copy).then_inc(acc_drained[0], 1)
                act.wait_ge(acc_full[1], a + 1)
                sc.activation(rs3[:, :], acc[1][:, 0:256], ACT.Copy).then_inc(acc_drained[1], 1)
                for j in range(2):
                    r = slice(j * HALF, (j + 1) * HALF)
                    act.wait_ge(bank_full[j], u + 2)
                    act.wait_ge(setup2, 6)
                    sc.activation(wbd[r, :, j, :], bank[j][r, 0:PAIRS * HS].rearrange("p (a d) -> p a d", a=PAIRS),
                                  ACT.Copy).then_inc(bank_drained[j], 1)

            def stage_E(at, b, c):
                u = at["E", c]
                for j in range(2):
                    act.wait_ge(bank_full[j], u.bank + 1)
                    sc.activation(m1T[0:H, j * 256:(j + 1) * 256], bank[j][0:H, 0:256],
                                  ACT.Copy).then_inc(bank_drained[j], 1)
                for j in range(PAIRS // 2):
                    act.wait_ge(wide_full[j % 2], u.wide + j // 2 + 1)
                    sc.activation(p1[:, 2 * j:2 * j + 2, :], wide[j % 2][:, :].rearrange("p (a n) -> p a n", a=2),
                                  ACT.Exp).then_inc(wide_drained[j % 2], 1)

            def stage_H(at, b, c):
                u, n = at["H", c].bank, b * NC + c
                for k in range(KB):
                    act.wait_ge(bank_full[k], u + 1)
                    act.wait_ge(acc_drained[k], at["H", c].acc)
                    sc.activation(rc[:, k, :], bank[k][:, :], ACT.Ln).then_inc(bank_drained[k], 1)
                    act.wait_ge(bank_drained[k], u + 1)
                    sc.activation(rc[:, k, :], rc[:, k, :], ACT.Exp, scale=-1.0).then_inc(rc_made, 1)

            def stage_O(at, b, c):
                u, n = at["O", c].bank, b * NC + c
                norm_y.root(act, n, c)

            def stage_N(at, b, c):
                norm_m.root(act, b * NC + c, c)

            def stage_T(at, b, c):
                u, n = at["T", c].bank, b * NC + c
                act.wait_ge(carry, n)
                act.wait_ge(xr_made, older(b, c))
                act.wait_ge(xk_made, older(b, c))
                for k in range(KB):
                    act.wait_ge(bank_full[k], u + 1)
                    sc.activation(x2T[c % 2][:, k, 1:CH + 1], bank[k][:, :], ACT.Copy).then_inc(bank_drained[k], 1)

            def stage_G1(at, b, c):
                u, n = at["G1", c].bank, b * NC + c
                act.wait_ge(norm_f.stats_made, n)
                for j in range(2):
                    act.wait_ge(bank_full[j], u + 1)
                    sc.activation(sg[:, 2 * j:2 * j + 2, :], bank[j][:, :].rearrange("p (t n) -> p t n", t=2),
                                  ACT.Exp, scale=-1.0).then_inc(bank_drained[j], 1)
                for k in range(KB):
                    act.wait_ge(bank_full[k], u + 2)
                    sc.activation(ka[:, k, :], bank[k][:, :], ACT.Relu).then_inc(bank_drained[k], 1)
                for k in range(KB):
                    act.wait_ge(bank_drained[k], u + 2)
                ins = sc.activation(ka[:, :, :], ka[:, :, :], ACT.Square)
                ins.then_inc(ka_made, 1)
                for j in range(2):
                    act.wait_ge(bank_drained[j], u + 1)
                sc.activation(sg[:, :, :], sg[:, :, :], ACT.Ln, bias=1.0).then_inc(sg_ln, 1)
                act.wait_ge(sg_ln, n + 1)
                sc.activation(sg[:, :, :], sg[:, :, :], ACT.Exp, scale=-1.0).then_inc(sg_made, 1)

            def stage_G2(at, b, c):
                n = b * NC + c
                act.wait_ge(norm_f.applied, n)
                norm_f.root(act, n, c)

            part2_program(act, {"X": stage_X, "A": stage_A, "F": stage_F, "W": stage_W, "E": stage_E, "H": stage_H, "O": stage_O, "N": stage_N, "T": stage_T, "G1": stage_G1,
                                "G2": stage_G2})

        @block.vector
        def _(dve):
            v = nc.vector
            dve.wait_ge(const_made, NCONST)
            for dst, scale in ((eye7, 7.0), (eye15, 15.0), (eye13, 13.0)):
                v.tensor_scalar(dst[:, :], eye[:, :], scale, None, ALU.mult).then_inc(eyes_made, 1)
            dve.wait_ge(eyes_made, 3)
            full = [P, PAIRS, M]

            def pm(t):
                return t.rearrange("p (a m) -> p a m", a=PAIRS)

            with dve.Fori(0, B // 2) as i:
                for s in S2:
                    n = i * 2 + s
                    for c in range(NC):
                        dve.wait_ge(p_in[c], 16 * (n + 1))
                        for t in range(NT):
                            ins = v.bn_stats(st1[:, c, t, :], x1in[0][:, c, t, :])
                        ins.then_inc(p_stats, 1)
                        dve.wait_ge(p_stats, n * NC + c + 1)
                        hold(dve)
                        for t in range(NT):
                            ins = v.bn_aggr(mv1[:, c, t, :], st1[:, c, t, :])
                        ins.then_inc(p_mv, 1)
                    done = lambda *k: dve.wait_ge(p_dve, of(dve_steps, i, *k))
                    dve.wait_ge(p_act, of(act_steps, i, "lm", s))
                    v.tensor_tensor(lm16[s][:, 2:4, :, :], qlT[s][:, :, :, :], lm16[s][:, 0:2, :, :],
                                    ALU.subtract).then_inc(p_dve, 1)
                    for k in range(KB):
                        ins = v.tensor_tensor(qbd[s][:, k, :, :],
                                              qlT[s][:, 0, k, :].unsqueeze(1).to_broadcast([P, HB, M]),
                                              head_mask[:, :].unsqueeze(2).to_broadcast([P, HB, M]), ALU.mult)
                    ins.then_inc(p_dve, 1)
                    dve.wait_ge(p_pe, of(pe_steps, i, "logits", s))
                    v.tensor_reduce(mx[s][:, :], pm(pb[s][0]), AX.X, ALU.max).then_inc(p_dve, 1)
                    done("max", s)
                    v.tensor_tensor(X[s][:, :, :], pm(pb[s][0]), mx[s][:, :].unsqueeze(2).to_broadcast(full),
                                    ALU.subtract).then_inc(p_dve, 1)
                    dve.wait_ge(p_act, of(act_steps, i, "exp", s))
                    v.tensor_reduce(rsum1[s][:, :], X[s][:, :, :], AX.X, ALU.add).then_inc(p_dve, 1)
                    done("sum", s)
                    v.reciprocal(rcp1[s][:, :], rsum1[s][:, :]).then_inc(p_dve, 1)
                    done("rcp", s)
                    v.tensor_tensor(X[s][:, :, :], X[s][:, :, :], rcp1[s][:, :].unsqueeze(2).to_broadcast(full),
                                    ALU.mult).then_inc(p_dve, 1)
                    done("X", s)
                    v.tensor_reduce(rc1[s][:, 0, :], X[s][:, :, :], AX.X, ALU.add).then_inc(p_dve, 1)
                    dve.wait_ge(p_act, of(act_steps, i, "XT", s))
                    v.tensor_reduce(rc1[s][:, 1, :], XT[s][:, :, :], AX.X, ALU.add).then_inc(p_dve, 1)
                    dve.wait_ge(p_pe, of(pe_steps, i, "sums", s))
                    v.tensor_reduce(cm[s][:, :, :], pb[s][2][0:PAIRS, 0:2 * P]
                                    .rearrange("p (a h m) -> p a h m", a=2, h=2), AX.X, ALU.max).then_inc(p_dve, 1)
                    done("cm", s)
                    v.tensor_tensor(cg[s][:, 0, :], cm[s][:, 0, :], cm[s][:, 1, :], ALU.mult).then_inc(p_dve, 1)
                    done("cg", s)
                    v.reciprocal(cg[s][:, 1, :], cg[s][:, 0, :]).then_inc(p_dve, 1)
                    done("cr", s)
                    v.tensor_copy(gb[s][:, :, :], cg[s][:, 1, :].unsqueeze(2).to_broadcast([PAIRS, 2, M]))\
                        .then_inc(p_dve, 1)
                    dve.wait_ge(p_pe, of(pe_steps, i, "g", s))
                    v.tensor_copy(gcol[s][:, :], pb[s][2][:, 0:PAIRS]).then_inc(p_dve, 1)
                    done("gcol", s)
                    gc = gcol[s][:, :].unsqueeze(2).to_broadcast(full)
                    dve.wait_ge(zt_out, 32 * i)
                    v.tensor_tensor(ZT[s][:, :, :], X[s][:, :, :], gc, ALU.mult).then_inc(p_dve, 1)
                    v.tensor_tensor(Z[s][:, :, :], XT[s][:, :, :], gc, ALU.mult).then_inc(p_dve, 1)
                for it in range(ITERS):
                    for s in S2:
                        def eyeb(t):
                            return t[:, :].unsqueeze(1).to_broadcast(full)
                        dve.wait_ge(p_act, of(act_steps, i, "S", it, s))
                        v.scalar_tensor_tensor(out=T1[s][:, :, :], in0=SS[s][:, :, :], scalar=-1.0, in1=eyeb(eye7),
                                               op0=ALU.mult, op1=ALU.add).then_inc(p_dve, 1)
                        dve.wait_ge(p_pe, of(pe_steps, i, "ST1", it, s))
                        v.scalar_tensor_tensor(out=T2[s][:, :, :], in0=pm(pb[s][1]), scalar=-1.0, in1=eyeb(eye15),
                                               op0=ALU.mult, op1=ALU.add).then_inc(p_dve, 1)
                        dve.wait_ge(p_pe, of(pe_steps, i, "ST2", it, s))
                        v.scalar_tensor_tensor(out=T3[s][:, :, :], in0=pm(pb[s][0]), scalar=-1.0, in1=eyeb(eye13),
                                               op0=ALU.mult, op1=ALU.add).then_inc(p_dve, 1)
                        dve.wait_ge(p_pe, of(pe_steps, i, "ZT", it, s))
                        v.tensor_scalar(ZT[s][:, :, :], pm(pb[s][2]), 0.25, None, ALU.mult).then_inc(p_dve, 1)

            dve.wait_ge(p_act, len(act_steps) * B // 2)
            dve.wait_ge(p_pe, len(pe_steps) * B // 2)
            dve.wait_ge(p_hat, NC * B)
            dve.wait_ge(lm_out, 16 * B)
            dve.wait_ge(zt_out, 16 * B)

            def stage_X(at, b, c):
                dve.wait_ge(x_in[c % 2], 16 * (b * 2 + c // 2 + 1))
                norm_x.stats(dve, xin[c % 2], b * NC + c, c)

            def stage_A(at, b, c):
                u, n = at["A", c], b * NC + c
                span = slice(c * CH, (c + 1) * CH)
                for k in range(KB):
                    dve.wait_ge(q_hi, n * KB + k + 1)
                    v.scalar_tensor_tensor(out=ql[:, k, span], in0=bank[k][:, :], scalar=QSCALE, in1=qh[:, k, span],
                                           op0=ALU.mult, op1=ALU.subtract).then_inc(bank_drained[k], 1)
                for k in range(KB):
                    dve.wait_ge(k_hi, n * KB + k + 1)
                    v.tensor_tensor(kl[:, k, span], bank[k][:, :], kh[:, k, span],
                                    ALU.subtract).then_inc(bank_drained[k], 1)
                for j in range(2):
                    dve.wait_ge(bank_full[j], u.bank + 4)
                    v.tensor_copy(vv[:, c * NT + 2 * j:c * NT + 2 * j + 2, :],
                                  bank[j][:, :].rearrange("p (t n) -> p t n", t=2)).then_inc(bank_drained[j], 1)
                for j in range(PAIRS // 2):
                    dve.wait_ge(wide_full[j % 2], u.wide + j // 2 + 1)
                    v.tensor_reduce(m3[:, 2 * j:2 * j + 2, c], wide[j % 2][:, :].rearrange("p (a n) -> p a n", a=2),
                                    AX.X, ALU.max).then_inc(wide_drained[j % 2], 1)
                for t in range(NT):
                    dve.wait_ge(wide_full[t % 2], u.wide + 2 + t // 2 + 1)
                    v.tensor_reduce(m1[:, c * NT + t, :], wide[t % 2][:, :].rearrange("p (h m) -> p h m", h=H),
                                    AX.X, ALU.max).then_inc(wide_drained[t % 2], 1)

            def stage_M(at, b, c):
                u = at["M", 0]
                dve.wait_ge(wide_drained[1], u.wide)
                v.tensor_reduce(m3m[:, :], m3[:, :, :], AX.X, ALU.max).then_inc(m3_max, 1)
                for k in range(KB):
                    dve.wait_ge(bank_full[k], u.bank + 1)
                    v.scalar_tensor_tensor(out=nmax[0:PB, k, :, :],
                                           in0=bank[k][0:PB, 0:P].unsqueeze(1).to_broadcast([PB, PB, P]), scalar=-1.0,
                                           in1=ident[0:PB, 0:PB].unsqueeze(2).to_broadcast([PB, PB, P]),
                                           op0=ALU.mult, op1=ALU.mult).then_inc(bank_drained[k], 1)

            def stage_W(at, b, c):
                u = at["W", 0].bank
                dve.wait_ge(bank_full[1], u + 1)
                v.reciprocal(rr3[:, :], bank[1][:, 0:PAIRS]).then_inc(bank_drained[1], 1)
                dve.wait_ge(bank_full[0], u + 1)
                dve.wait_ge(bank_drained[1], u + 1)
                for j in range(2):
                    r = slice(j * HALF, (j + 1) * HALF)
                    ins = v.tensor_tensor(un[r, :, :],
                                          bank[0][r, 0:KB * P].rearrange("p (a h d) -> p a h d", h=2, d=HS)[:, :, j, :],
                                          rr3[r, :].unsqueeze(2).to_broadcast([HALF, PAIRS, HS]), ALU.mult)
                ins.then_inc(bank_drained[0], 1)

            def stage_H(at, b, c):
                a, n = at["H", c].acc, b * NC + c
                for k in range(KB):
                    dve.wait_ge(acc_full[k], a + 1)
                    dve.wait_ge(rc_made, n * KB + k + 1)
                    v.tensor_tensor(oT[:, k, :], acc[k][:, :], rc[:, k, :], ALU.mult).then_inc(acc_drained[k], 1)

            def stage_O(at, b, c):
                u, n = at["O", c].bank, b * NC + c
                dve.wait_ge(xm_made, n)
                for j in range(2):
                    dve.wait_ge(bank_full[j], u + 1)
                    v.tensor_tensor(yy[:, 2 * j:2 * j + 2, :], bank[j][:, :].rearrange("p (t n) -> p t n", t=2),
                                    bo_all[:, :].unsqueeze(1).to_broadcast([P, 2, A]),
                                    ALU.add).then_inc(bank_drained[j], 1)
                for j in range(2):
                    dve.wait_ge(bank_drained[j], u + 1)
                norm_y.stats(dve, yy, n, c)

            def stage_N(at, b, c):
                n = b * NC + c
                dve.wait_ge(xm_made, n + 1)
                dve.wait_ge(norm_m.applied, n)
                norm_m.stats(dve, xm[c % 3], n, c)

            def stage_T(at, b, c):
                u, n = at["T", c].bank, b * NC + c
                dve.wait_ge(xk_made, n)
                if c == 0:
                    v.memset(x2T[0][:, :, 0:1], 0.0).then_inc(carry, 1)
                else:
                    v.tensor_copy(x2T[c % 2][:, :, 0:1], x2T[(c + 1) % 2][:, :, CH:CH + 1]).then_inc(carry, 1)
                dve.wait_ge(carry, n + 1)
                for k in range(KB):
                    dve.wait_ge(bank_drained[k], u + 1)
                cur, prev = x2T[c % 2][:, :, 1:CH + 1], x2T[c % 2][:, :, 0:CH]
                v.tensor_tensor(dx[:, :, :], cur, prev, ALU.subtract).then_inc(dx_made, 1)
                dve.wait_ge(dx_made, n + 1)
                for k in range(KB):
                    ins = v.scalar_tensor_tensor(out=xrT[:, k, :], in0=dx[:, k, :], scalar=mu[:, 0, k:k + 1],
                                                 in1=x2T[c % 2][:, k, 0:CH], op0=ALU.mult, op1=ALU.add)
                ins.then_inc(xr_made, 1)

            def stage_G2(at, b, c):
                u, n = at["G2", c].bank, b * NC + c
                dve.wait_ge(sg_made, n + 1)
                dve.wait_ge(fin_out[c % 2], 16 * (b * 2 + c // 2))
                dve.wait_ge(norm_f.applied, n)
                for j in range(2):
                    dve.wait_ge(bank_full[j], u + 1)
                    v.tensor_tensor(ob[c % 2][:, 2 * j:2 * j + 2, :], bank[j][:, :].rearrange("p (t n) -> p t n", t=2),
                                    sg[:, 2 * j:2 * j + 2, :], ALU.mult).then_inc(bank_drained[j], 1)
                for j in range(2):
                    dve.wait_ge(bank_drained[j], u + 1)
                norm_f.stats(dve, ob[c % 2], n, c)

            part2_program(dve, {"X": stage_X, "A": stage_A, "M": stage_M, "W": stage_W, "H": stage_H, "O": stage_O, "N": stage_N, "T": stage_T, "G2": stage_G2})

        @block.tensor
        def _(pe):
            mm = nc.tensor.matmul
            tr = nc.tensor.transpose
            pe.wait_ge(const_made, NCONST)
            pe.wait_ge(weights_in, 16 * NW)
            for w in range(3):
                if w >= 2:
                    pe.wait_ge(wT_drained, w - 1)
                for k in range(KB):
                    for o in range(KB):
                        ins = tr(wide[w % 2][:, k * A + o * P:k * A + (o + 1) * P],
                                 wnat[:, w, o, k * P:(k + 1) * P], ident[:, :])
                ins.then_inc(wT_full, 1)
            pe.wait_ge(wT_drained, 3)

            def heads(dst, left, right, sem_value=None):
                for a in range(PAIRS):
                    for j in range(2):
                        r = slice(j * HALF, (j + 1) * HALF)
                        ins = mm(dst[r, a * M:(a + 1) * M], left[r, a, :], right(r, a), start=True, stop=True)
                return ins

            with pe.Fori(0, B // 2) as i:
                for s in S2:
                    n = i * 2 + s
                    for c in range(NC):
                        pe.wait_ge(p_hat, n * NC + c + 1)
                        if c == 0:
                            pe.wait_ge(p_dve, i * len(dve_steps))
                        for t in range(NT):
                            q = M - TM - TM * (c * NT + t)
                            ins = mm(pb[s][0][0:M, 0:A], pool_w[:, q:q + M], x1in[0][:, c, t, :],
                                     start=(c == 0 and t == 0), stop=(c == NC - 1 and t == NT - 1))
                    ins.then_inc(p_pe, 1)
                    pe.wait_ge(p_act, of(act_steps, i, "xl", s))
                    hold(pe)
                    for k in range(KB):
                        if k == 1:
                            ins.then_inc(p_pooled, 1)
                        ins = tr(pb[s][1][:, k * M:(k + 1) * M], xl[s][:, k * P:(k + 1) * P], ident[0:M, 0:M])
                    ins.then_inc(p_pe, 1)
                    pe.wait_ge(p_act, of(act_steps, i, "xlT", s))
                    for a, w in enumerate((wq, wk)):
                        for o in range(KB):
                            for k in range(KB):
                                ins = mm(pb[s][2][:, (a * KB + o) * M:(a * KB + o + 1) * M],
                                         w[:, k, o * P:(o + 1) * P], xlT[s][:, k, :], start=(k == 0), stop=(k == KB - 1))
                    ins.then_inc(p_pe, 1)
                    pe.wait_ge(p_dve, of(dve_steps, i, "qbd", s))
                    for a in range(PAIRS):
                        k, j = a // PB, a % PB
                        ins = mm(pb[s][0][:, a * M:(a + 1) * M],
                                 qbd[s][:, k, 2 * j:2 * j + 2, :].rearrange("p h m -> p (h m)"), qlT[s][:, 1, k, :],
                                 start=True, stop=True)
                    ins.then_inc(p_pe, 1)
                    pe.wait_ge(p_dve, of(dve_steps, i, "X", s))
                    hold(pe)
                    heads(pb[s][1], X[s], lambda r, a: ident[r, r]).then_inc(p_pe, 1)
                    pe.wait_ge(p_dve, of(dve_steps, i, "cs", s))
                    for a in range(2):
                        ins = tr(pb[s][2][0:PAIRS, a * P:(a + 1) * P], rc1[s][:, a, :], ident[:, :])
                    ins.then_inc(p_pe, 1)
                    pe.wait_ge(p_dve, of(dve_steps, i, "gb", s))
                    mm(pb[s][2][:, 0:PAIRS], gb[s][:, :, :].rearrange("p h m -> p (h m)"), ident[0:PAIRS, 0:PAIRS],
                       start=True, stop=True).then_inc(p_pe, 1)
                for it in range(ITERS):
                    for s in S2:
                        def rhs(t):
                            return lambda r, a: t[r, a, :]
                        if it == 0:
                            pe.wait_ge(p_dve, of(dve_steps, i, "Z", s))
                        else:
                            pe.wait_ge(p_act, of(act_steps, i, "Z", it - 1, s))
                            pe.wait_ge(p_dve, of(dve_steps, i, "ZT", it - 1, s))
                        hold(pe)
                        heads(pb[s][0], XT[s], rhs(Z[s])).then_inc(p_pe, 1)
                        pe.wait_ge(p_dve, of(dve_steps, i, "T1", it, s))
                        hold(pe)
                        heads(pb[s][1], SS[s], rhs(T1[s])).then_inc(p_pe, 1)
                        pe.wait_ge(p_dve, of(dve_steps, i, "T2", it, s))
                        hold(pe)
                        heads(pb[s][0], SS[s], rhs(T2[s])).then_inc(p_pe, 1)
                        pe.wait_ge(p_dve, of(dve_steps, i, "T3", it, s))
                        hold(pe)
                        if it < ITERS - 1:
                            heads(pb[s][1], ZT[s], rhs(T3[s])).then_inc(p_pe, 1)
                        heads(pb[s][2], T3[s], rhs(ZT[s])).then_inc(p_pe, 1)

            pe.wait_ge(p_act, len(act_steps) * B // 2)
            pe.wait_ge(p_dve, len(dve_steps) * B // 2)

            def stage_A(at, b, c):
                u, n = at["A", c], b * NC + c
                span = slice(c * CH, (c + 1) * CH)
                pe.wait_ge(norm_x.applied, n + 1)
                for k in range(KB):
                    pe.wait_ge(bank_drained[k], u.bank)
                    for t in range(NT):
                        ins = tr(bank[k][:, t * P:(t + 1) * P], xhat[c % 2][:, t, k * P:(k + 1) * P], ident[:, :])
                    ins.then_inc(bank_full[k], 1)
                for a, w in enumerate((wq, wk)):
                    for o in range(KB):
                        pe.wait_ge(bank_drained[o], u.bank + 1 + a)
                        if a == 0 and o == 0:
                            pe.wait_ge(bank_drained[1], u.bank + 1)
                        for k in range(KB):
                            ins = mm(bank[o][:, :], w[:, k, o * P:(o + 1) * P], xT[:, k, :], start=(k == 0),
                                     stop=(k == KB - 1))
                            if a == 0 and o == 0 and k == 0:
                                ins.then_inc(xhat_read, 1)
                        ins.then_inc(bank_full[o], 1)
                for j in range(2):
                    pe.wait_ge(bank_drained[j], u.bank + 3)
                    for t in range(2):
                        tok = slice((2 * j + t) * P, (2 * j + t + 1) * P)
                        for k in range(KB):
                            ins = mm(bank[j][:, t * A:(t + 1) * A], xT[:, k, tok], wv[:, k, :], start=(k == 0),
                                     stop=(k == KB - 1))
                    ins.then_inc(bank_full[j], 1)
                if c == 0:
                    pe.wait_ge(q_bd_in, 16 * 2 * HB * (b + 1))
                    pe.wait_ge(kA_bd_in, 16 * HB * (b + 1))
                for j in range(PAIRS // 2):
                    pe.wait_ge(wide_drained[j % 2], u.wide + j // 2)
                    for a in range(2):
                        k, q = (2 * j + a) // PB, (2 * j + a) % PB
                        ins = mm(wide[j % 2][:, a * CH:(a + 1) * CH],
                                 q_bd[:, 0, k, 2 * q:2 * q + 2, :].rearrange("p h m -> p (h m)"), kh[:, k, span],
                                 start=True, stop=True)
                    ins.then_inc(wide_full[j % 2], 1)
                for t in range(NT):
                    pe.wait_ge(wide_drained[t % 2], u.wide + 2 + t // 2)
                    tok = slice(c * CH + t * P, c * CH + (t + 1) * P)
                    for k in range(KB):
                        ins = mm(wide[t % 2][:, k * 512:(k + 1) * 512], qh[:, k, tok],
                                 kA_bd[:, 0, k, :, :].rearrange("p h m -> p (h m)"), start=True, stop=True)
                    ins.then_inc(wide_full[t % 2], 1)

            def stage_M(at, b, c):
                u = at["M", 0]
                for j in range(2):
                    pe.wait_ge(bank_drained[j], u.bank)
                    pe.wait_ge(wide_drained[j], u.wide)
                    pe.wait_ge(acc_drained[j], u.acc)
                pe.wait_ge(m3_max, b + 1)
                for k in range(KB):
                    tr(bank[k][0:PB, 0:P], m3m[:, k * PB:(k + 1) * PB], ident[:, :]).then_inc(bank_full[k], 1)

            def stage_F(at, b, c):
                u = at["F", 0]
                NTL = NC * NT

                def sums(t):
                    pe.wait_ge(wide_drained[t % 2], u.wide + t // 2 + 1)
                    if t == 0:
                        for j in range(2):
                            pe.wait_ge(acc_drained[j], u.acc)
                    first, last = t == 0, t == NTL - 1
                    for q in range(4):
                        ins = mm(acc[1][32 * q:32 * q + 32, 0:256], ones32[:, :], e3[t % 2][:, q * 256:(q + 1) * 256],
                                 start=first, stop=last, skip_group_check=True)
                    if last:
                        ins.then_inc(acc_full[1], 1)
                    for a in range(PAIRS):
                        k, q = a // PB, a % PB
                        ins = mm(acc[0][32 * q:32 * q + 32, k * P:(k + 1) * P], vv[:, t, 32 * a:32 * a + 32],
                                 e3[t % 2][:, a * P:(a + 1) * P], start=(first and k == 0), stop=last,
                                 skip_group_check=True)
                    ins.then_inc(acc_full[0] if last else e3_read, 1)

                for k in range(KB):
                    pe.wait_ge(bank_drained[k], u.bank)
                for t in range(NTL):
                    pe.wait_ge(wide_drained[t % 2], u.wide + t // 2)
                    tok = slice(t * P, (t + 1) * P)
                    for k in range(KB):
                        dst = wide[t % 2][:, k * 512:(k + 1) * 512]
                        qb = [q_bd[:, e, k, :, :].rearrange("p h m -> p (h m)") for e in range(2)]
                        mm(dst, ones4[:, :], nmax[:, k, :, :].rearrange("p a n -> p (a n)"), start=True, stop=False)
                        mm(dst, kh[:, k, tok], qb[0], start=False, stop=False)
                        mm(dst, kh[:, k, tok], qb[1], start=False, stop=False)
                        ins = mm(dst, kl[:, k, tok], qb[0], start=False, stop=True)
                    ins.then_inc(wide_full[t % 2], 1)
                    if t:
                        sums(t - 1)
                sums(NTL - 1)

            def stage_W(at, b, c):
                u, a0 = at["W", 0].bank, at["F", 0].acc
                pe.wait_ge(acc_drained[0], a0 + 1)
                pe.wait_ge(bank_drained[0], u)
                for k in range(KB):
                    ins = tr(bank[0][:, k * P:(k + 1) * P], uT[:, k * P:(k + 1) * P], ident[:, :])
                    if k == 0:
                        ins.then_inc(q_bd_free, 1)
                ins.then_inc(bank_full[0], 1)
                pe.wait_ge(acc_drained[1], a0 + 1)
                pe.wait_ge(bank_drained[1], u)
                for h in range(2):
                    ins = mm(bank[1][:, 0:PAIRS].rearrange("p (q h) -> p h q", h=2)[:, h, :],
                             rs3[:, h * P:(h + 1) * P], ident[:, 0:P:32], start=True, stop=True)
                ins.then_inc(bank_full[1], 1)
                pe.wait_ge(zt_in, 16 * (b + 1))
                pe.wait_ge(bank_drained[1], u + 1)
                pe.wait_ge(bank_drained[0], u + 1)
                hold(pe)
                for j in range(2):
                    r = slice(j * HALF, (j + 1) * HALF)
                    for a in range(PAIRS):
                        ins = mm(bank[j][r, a * HS:(a + 1) * HS], zt[r, a, :], un[r, a, :], start=True, stop=True)
                    ins.then_inc(bank_full[j], 1)

            def stage_E(at, b, c):
                u = at["E", c]
                if c == 0:
                    pe.wait_ge(kE_bd_in, 16 * 2 * HB * (b + 1))
                for j in range(2):
                    pe.wait_ge(bank_drained[j], u.bank)
                    for t in range(2):
                        ins = tr(bank[j][0:H, t * P:(t + 1) * P], m1[:, c * NT + 2 * j + t, :], ident[:, :])
                    ins.then_inc(bank_full[j], 1)
                for j in range(2):
                    pe.wait_ge(bank_drained[j], u.bank + 1)
                span = slice(c * CH, (c + 1) * CH)
                for j in range(PAIRS // 2):
                    pe.wait_ge(wide_drained[j % 2], u.wide + j // 2)
                    for i2 in range(2):
                        a = 2 * j + i2
                        k, q = a // PB, a % PB
                        dst = wide[j % 2][:, i2 * CH:(i2 + 1) * CH]
                        kb = [kE_bd[:, e, k, 2 * q:2 * q + 2, :].rearrange("p h m -> p (h m)") for e in range(2)]
                        mm(dst, neg_sel[:, a, :], m1T[:, :], start=True, stop=False)
                        mm(dst, kb[0], qh[:, k, span], start=False, stop=False)
                        mm(dst, kb[0], ql[:, k, span], start=False, stop=False)
                        ins = mm(dst, kb[1], qh[:, k, span], start=False, stop=True)
                    ins.then_inc(wide_full[j % 2], 1)

            def stage_H(at, b, c):
                u, e = at["H", c], at["E", c].wide
                if c == 0:
                    for j in range(2):
                        pe.wait_ge(bank_drained[j], at["W", 0].bank + 2)
                for j in range(PAIRS // 2):
                    pe.wait_ge(wide_drained[j % 2], e + j // 2 + 1)
                    k = 2 * j // PB
                    if j % 2 == 0:
                        pe.wait_ge(bank_drained[k], u.bank)
                        pe.wait_ge(acc_drained[k], u.acc)
                    for a in (2 * j, 2 * j + 1):
                        r = slice(32 * (a % PB), 32 * (a % PB) + 32)
                        s_ = mm(bank[k][r, :], ones_pair[:, :], p1[:, a, :], start=True, stop=True)
                        if a == 0 and c == 0:
                            s_.then_inc(zt_free, 1)
                        if a == 0 and c == NC - 1:
                            s_.then_inc(k_bd_free, 1)
                        o_ = mm(acc[k][r, :], wbd[:, a, :, :].rearrange("p h d -> p (h d)"), p1[:, a, :], start=True,
                                stop=True)
                    if j % 2 == 1:
                        s_.then_inc(bank_full[k], 1)
                        o_.then_inc(acc_full[k], 1)

            def stage_O(at, b, c):
                u, h = at["O", c].bank, at["H", c].acc
                for k in range(KB):
                    pe.wait_ge(acc_drained[k], h + 1)
                for j in range(2):
                    pe.wait_ge(bank_drained[j], u)
                    for t in range(2):
                        dst = bank[j][:, t * A:(t + 1) * A]
                        tok = slice((2 * j + t) * P, (2 * j + t + 1) * P)
                        for k in range(KB):
                            ins = mm(dst, oT[:, k, tok], wo[:, k, :], start=(k == 0), stop=(k == KB - 1))
                    ins.then_inc(bank_full[j], 1)

            def stage_T(at, b, c):
                u, n = at["T", c].bank, b * NC + c
                pe.wait_ge(norm_m.applied, n + 1)
                for k in range(KB):
                    pe.wait_ge(bank_drained[k], u)
                    for t in range(NT):
                        ins = tr(bank[k][:, t * P:(t + 1) * P], x2h[:, t, k * P:(k + 1) * P], ident[:, :])
                    ins.then_inc(bank_full[k], 1)

            def stage_G1(at, b, c):
                u, n = at["G1", c].bank, b * NC + c
                pe.wait_ge(xr_made, n + 1)
                for j in range(2):
                    pe.wait_ge(bank_drained[j], u)
                    for t in range(2):
                        tok = slice((2 * j + t) * P, (2 * j + t + 1) * P)
                        for k in range(KB):
                            ins = mm(bank[j][:, t * A:(t + 1) * A], xrT[:, k, tok], wrT[:, k, :], start=(k == 0),
                                     stop=(k == KB - 1))
                            if j == 0 and t == 0 and k == 0:
                                ins.then_inc(x2h_read, 1)
                    ins.then_inc(bank_full[j], 1)
                pe.wait_ge(xk_made, n + 1)
                for o in range(KB):
                    pe.wait_ge(bank_drained[o], u + 1)
                    for k in range(KB):
                        ins = mm(bank[o][:, :], wkT[:, k, o * P:(o + 1) * P], xkT[:, k, :], start=(k == 0),
                                 stop=(k == KB - 1))
                    ins.then_inc(bank_full[o], 1)

            def stage_G2(at, b, c):
                u, n = at["G2", c].bank, b * NC + c
                pe.wait_ge(ka_made, n + 1)
                for j in range(2):
                    pe.wait_ge(bank_drained[j], u)
                    for t in range(2):
                        tok = slice((2 * j + t) * P, (2 * j + t + 1) * P)
                        for k in range(KB):
                            ins = mm(bank[j][:, t * A:(t + 1) * A], ka[:, k, tok], wvT[:, k, :], start=(k == 0),
                                     stop=(k == KB - 1))
                    ins.then_inc(bank_full[j], 1)

            part2_program(pe, {"A": stage_A, "M": stage_M, "F": stage_F, "W": stage_W, "E": stage_E, "H": stage_H, "O": stage_O, "T": stage_T, "G1": stage_G1,
                               "G2": stage_G2})


_INS = ["L0_attn_x", "L0_attn_Wk", "L0_attn_Wq", "L0_attn_Wv", "L0_attn_Wo", "L0_attn_bo", "L0_ffn_W_r",
        "L0_ffn_W_k", "L0_ffn_W_v", "L0_ffn_mu_r", "L0_ffn_mu_k"]


def kernel(**inputs):
    import numpy as np
    import concourse.bacc as bacc
    from concourse.bass_utils import run_bass_kernel_spmd

    nc = bacc.Bacc("TRN2", target_bir_lowering=False, num_devices=1)
    arrays, args = {}, []
    for name in _INS:
        a = np.ascontiguousarray(inputs[name])
        arrays[f"in_{name}"] = a
        args.append(nc.dram_tensor(f"in_{name}", a.shape, mybir.dt.from_np(a.dtype), kind="ExternalInput").ap())
    shape = inputs["L0_attn_x"].shape
    args.append(nc.dram_tensor("out", shape, F32, kind="ExternalOutput").ap())
    sandwich(nc, *args)
    return run_bass_kernel_spmd(nc, [arrays], core_ids=[0]).results[0]["out"]
```

```python
from contextlib import ExitStack

import concourse.bass as bass
from concourse import mybir

F32 = mybir.dt.float32
F16 = mybir.dt.float16
ALU = mybir.AluOpType
ACT = mybir.ActivationFunctionType
AX = mybir.AxisListType

P = 128
HALF = P // 2


def sandwich(nc, x, Wk, Wq, Wv, Wo, bo, W_r, W_k, W_v, mu_r, mu_k, out):
    B, L, A = x.shape
    H, HS, M, ITERS = 16, 16, 64, 6
    KB = A // P
    HB = H // KB
    PAIRS, PB = H // 2, H // 2 // KB
    CH = 512
    NC, NT = L // CH, CH // P
    DEN = L // M
    TM = P // DEN
    EPS = 1e-5
    QSCALE = HS ** -0.5
    assert HS * HB == P and M == HALF and NC == 4 and NT == 4

    ctx = ExitStack()
    with ctx:
        def sb(name, shape, dt=F32, c=ctx):
            return c.enter_context(nc.sbuf_tensor(name, shape, dt))

        def sem(name):
            return ctx.enter_context(nc.semaphore(name))

        bank = [ctx.enter_context(nc.psum_tensor(f"bank{i}", [P, 512], F32)) for i in range(2)]
        wide = [ctx.enter_context(nc.psum_tensor(f"wide{i}", [P, 1024], F32)) for i in range(2)]
        acc = [ctx.enter_context(nc.psum_tensor(f"acc{i}", [P, 512], F32)) for i in range(2)]

        lm_dram = nc.dram_tensor("landmarks", [B, P, 4 * KB * M], F16).ap()
        zt_dram = nc.dram_tensor("inverse", [B, P, PAIRS * M], F32).ap()

        ident = sb("ident", [P, P])
        pool_w = sb("pool_w", [P, 2 * M - TM])
        head_mask = sb("head_mask", [P, HB])
        ones_pair = sb("ones_pair", [P, 2 * HS])
        ones32 = sb("ones32", [P, 32])
        ones4 = sb("ones4", [P, P], F16)
        neg_sel = sb("neg_sel", [P, PAIRS, P], F16)
        eye = sb("eye", [P, M])
        eye7 = sb("eye7", [P, M])
        eye15 = sb("eye15", [P, M])
        eye13 = sb("eye13", [P, M])
        wq = sb("wq", [P, KB, A])
        wk = sb("wk", [P, KB, A])
        wv = sb("wv", [P, KB, A])
        wo = sb("wo", [P, KB, A])
        wrT = sb("wrT", [P, KB, A])
        wkT = sb("wkT", [P, KB, A])
        wvT = sb("wvT", [P, KB, A])
        bo_all = sb("bo_all", [P, A])
        mu = sb("mu", [P, 2, KB])

        const_made = sem("const_made")
        weights_in = sem("weights_in")
        eyes_made = sem("eyes_made")
        wT_full = sem("wT_full")
        wT_drained = sem("wT_drained")
        NCONST = 17
        NW = 7 + 1 + 2

        part1 = ctx.enter_context(ExitStack())
        GR = 4
        ROWS = range(GR)
        NTL = NC * NT
        wnat = sb("wnat", [P, 3, KB, A], c=part1)
        x1in = [sb(f"x1in{s}", [P, NTL, A], c=part1) for s in ROWS]
        st1 = [sb(f"st1{s}", [P, NTL, 6], c=part1) for s in ROWS]
        mv1 = [sb(f"mv1{s}", [P, NTL, 2], c=part1) for s in ROWS]
        ln1 = [sb(f"ln1{s}", [P, NTL], c=part1) for s in ROWS]
        rstd1 = [sb(f"rstd1{s}", [P, NTL], c=part1) for s in ROWS]
        pw = [sb(f"pw{s}", [P, NTL * (M + TM)], c=part1) for s in ROWS]
        stl = [sb(f"stl{s}", [M, 6], c=part1) for s in ROWS]
        mvl = [sb(f"mvl{s}", [M, 2], c=part1) for s in ROWS]
        xl = [sb(f"xl{s}", [M, A], c=part1) for s in ROWS]
        xlT = [sb(f"xlT{s}", [P, KB, M], c=part1) for s in ROWS]
        qlT = [sb(f"qlT{s}", [P, 2, KB, M], c=part1) for s in ROWS]
        lm16 = [sb(f"lm16{s}", [P, 4, KB, M], F16, c=part1) for s in ROWS]
        qbd = [sb(f"qbd{s}", [P, KB, HB, M], c=part1) for s in ROWS]
        X = [sb(f"X{s}", [P, PAIRS, M], c=part1) for s in ROWS]
        XT = [sb(f"XT{s}", [P, PAIRS, M], c=part1) for s in ROWS]
        mx = [sb(f"mx{s}", [P, PAIRS], c=part1) for s in ROWS]
        rsum1 = [sb(f"rsum1{s}", [P, PAIRS], c=part1) for s in ROWS]
        rcp1 = [sb(f"rcp1{s}", [P, PAIRS], c=part1) for s in ROWS]
        rc1 = [sb(f"rc1{s}", [P, 2, PAIRS], c=part1) for s in ROWS]
        cm = [sb(f"cm{s}", [PAIRS, 2, 2], c=part1) for s in ROWS]
        cg = [sb(f"cg{s}", [PAIRS, 2, 2], c=part1) for s in ROWS]
        gb = [sb(f"gb{s}", [PAIRS, 2, M], c=part1) for s in ROWS]
        gcol = [sb(f"gcol{s}", [P, PAIRS], c=part1) for s in ROWS]
        Z = [sb(f"Z{s}", [P, PAIRS, M], c=part1) for s in ROWS]
        ZT = [sb(f"ZT{s}", [P, PAIRS, M], c=part1) for s in ROWS]
        SS = [sb(f"SS{s}", [P, PAIRS, M], c=part1) for s in ROWS]
        T1 = [sb(f"T1{s}", [P, PAIRS, M], c=part1) for s in ROWS]
        T2 = [sb(f"T2{s}", [P, PAIRS, M], c=part1) for s in ROWS]
        T3 = [sb(f"T3{s}", [P, PAIRS, M], c=part1) for s in ROWS]
        pb = [[bank[0][:, :], bank[1][:, :]], [wide[0][:, 0:512], wide[0][:, 512:1024]],
              [wide[1][:, 0:512], wide[1][:, 512:1024]], [acc[0][:, :], acc[1][:, :]]]

        p_in = [sem(f"p_in{s}") for s in ROWS]
        p_pe = sem("p_pe")
        p_act = sem("p_act")
        p_dve = sem("p_dve")
        lm_out = sem("lm_out")
        zt_out = sem("zt_out")

        pe_steps = ([(n, s) for n in ("pooled", "lT", "qk", "logits", "XT", "sums", "g") for s in ROWS]
                    + [(n, i, s) for i in range(ITERS) for names in (["S"], ["ST1"], ["ST2"], ["Z", "ZT"])
                       for s in ROWS for n in names if not (n == "Z" and i == ITERS - 1)])
        act_steps = ([(n, s) for names in (["ln", "rstd"], ["xlT"], ["ql", "kl", "lm"], ["exp"], ["XT"])
                      for s in ROWS for n in names]
                     + [(n, i, s) for i in range(ITERS) for n in ("S", "Z") for s in ROWS
                        if not (n == "Z" and i == ITERS - 1)])
        dve_steps = ([(n, s) for names in (["st", "mv"], ["pw"], ["stl", "mvl", "xl"], ["lmlo", "qbd"],
                                           ["max", "shift"], ["sum", "rcp", "X", "rs"], ["cs"],
                                           ["cm", "cg", "cr", "gb"], ["gcol", "ZT", "Z"])
                      for s in ROWS for n in names]
                     + [(n, i, s) for i in range(ITERS) for n in ("T1", "T2", "T3", "ZT") for s in ROWS])

        def of(steps, i, *key):
            return i * len(steps) + steps.index(key) + 1

        part2 = ctx.enter_context(ExitStack())
        block = ctx.enter_context(nc.Block())

        part1.close()
        xin = [sb(f"xin{i}", [P, NT, A], c=part2) for i in range(2)]
        xhat = [sb(f"xhat{i}", [P, NT, A], c=part2) for i in range(2)]
        xT = sb("xT", [P, KB, CH], c=part2)
        qh = sb("qh", [P, KB, L], F16, c=part2)
        ql = sb("ql", [P, KB, L], F16, c=part2)
        kh = sb("kh", [P, KB, L], F16, c=part2)
        kl = sb("kl", [P, KB, L], F16, c=part2)
        vv = sb("vv", [P, L // P, A], c=part2)
        m3 = sb("m3", [P, PAIRS, NC], c=part2)
        m3m = sb("m3m", [P, PAIRS], c=part2)
        nmax = sb("nmax", [P, KB, PB, P], F16, c=part2)
        m1 = sb("m1", [P, L // P, H], c=part2)
        m1T = sb("m1T", [P, CH], F16, c=part2)
        q_bd = sb("q_bd", [P, 2, KB, HB, M], F16, c=part2)
        kA_bd = sb("kA_bd", [P, 1, KB, HB, M], F16, c=part2)
        kE_bd = sb("kE_bd", [P, 2, KB, HB, M], F16, c=part2)
        e3 = [sb(f"e3{i}", [P, 2 * 512], c=part2) for i in range(2)]
        uT = sb("uT", [P, KB * P], c=part2)
        rs3 = sb("rs3", [P, 256], c=part2)
        rr3 = sb("rr3", [P, PAIRS], c=part2)
        un = sb("un", [P, PAIRS, HS], c=part2)
        zt = sb("zt", [P, PAIRS, M], c=part2)
        wbd = sb("wbd", [P, PAIRS, 2, HS], c=part2)
        p1 = sb("p1", [P, PAIRS, CH], c=part2)
        rc = sb("rc", [P, KB, CH], c=part2)
        oT = sb("oT", [P, KB, CH], c=part2)
        yy = sb("yy", [P, NT, A], c=part2)
        xres = [sb(f"xres{i}", [P, NT, A], c=part2) for i in range(2)]
        xm = [sb(f"xm{i}", [P, NT, A], c=part2) for i in range(3)]
        x2h = sb("x2h", [P, NT, A], c=part2)
        x2T = [sb(f"x2T{i}", [P, KB, CH + 1], c=part2) for i in range(2)]
        dx = sb("dx", [P, KB, CH], c=part2)
        xrT = sb("xrT", [P, KB, CH], c=part2)
        xkT = sb("xkT", [P, KB, CH], c=part2)
        sg = sb("sg", [P, NT, A], c=part2)

        ka = sb("ka", [P, KB, CH], c=part2)
        ob = [sb(f"ob{i}", [P, NT, A], c=part2) for i in range(2)]

        held = {e: sem(f"held_{n}") for e, n in ((nc.sync.engine, "sp"), (nc.vector.engine, "dve"), (nc.gpsimd.engine, "pool"), (nc.tensor.engine, "pe"))}

        def hold(eng):
            eng.sem_inc(held[eng.engine], 1)

        class Norm:

            def __init__(self, name, copies=1):
                self.st = sb(name + "_st", [P, NT, 6], c=part2)
                self.mv = [sb(f"{name}_mv{i}", [P, NT, 2], c=part2) for i in range(copies)]
                self.ln = sb(name + "_ln", [P, NT], c=part2)
                self.rstd = [sb(f"{name}_rstd{i}", [P, NT], c=part2) for i in range(copies)]
                self.stats_made = sem(name + "_stats")
                self.mv_made = sem(name + "_mv")
                self.ln_made = sem(name + "_ln")
                self.rstd_made = sem(name + "_rstd")
                self.applied = sem(name + "_applied")
                self.copies = copies

            def stats(self, dve, src, g, c):
                dve.wait_ge(self.mv_made, g)
                for t in range(NT):
                    ins = nc.vector.bn_stats(self.st[:, t, :], src[:, t, :])
                ins.then_inc(self.stats_made, 1)
                dve.wait_ge(self.stats_made, g + 1)
                if not (isinstance(g, int) and g < self.copies):
                    dve.wait_ge(self.applied, g + 1 - self.copies)
                hold(dve)
                for t in range(NT):
                    ins = nc.vector.bn_aggr(self.mv[c % self.copies][:, t, :], self.st[:, t, :])
                ins.then_inc(self.mv_made, 1)

            def root(self, act, g, c):
                act.wait_ge(self.rstd_made, g)
                act.wait_ge(self.mv_made, g + 1)
                nc.scalar.activation(self.ln[:, :], self.mv[c % self.copies][:, :, 1], ACT.Ln,
                                     bias=EPS).then_inc(self.ln_made, 1)
                act.wait_ge(self.ln_made, g + 1)
                nc.scalar.activation(self.rstd[c % self.copies][:, :], self.ln[:, :], ACT.Exp,
                                     scale=-0.5).then_inc(self.rstd_made, 1)

            def apply(self, dve, dst, src, g, c):
                dve.wait_ge(self.rstd_made, g + 1)
                k = c % self.copies
                for t in range(NT):
                    ins = nc.vector.tensor_scalar(dst[:, t, :], src[:, t, :], self.mv[k][:, t, 0:1],
                                                  self.rstd[k][:, t:t + 1], ALU.subtract, ALU.mult)
                ins.then_inc(self.applied, 1)

        norm_x = Norm("norm_x", 2)
        norm_y = Norm("norm_y")
        norm_m = Norm("norm_m")
        norm_f = Norm("norm_f")

        setup2 = sem("setup2")
        x_in = [sem(f"x_in{i}") for i in range(2)]
        xhat_read = sem("xhat_read")
        bank_full = [sem(f"bank{i}_full") for i in range(2)]
        bank_drained = [sem(f"bank{i}_drained") for i in range(2)]
        wide_full = [sem(f"wide{i}_full") for i in range(2)]
        wide_drained = [sem(f"wide{i}_drained") for i in range(2)]
        acc_full = [sem(f"acc{i}_full") for i in range(2)]
        acc_drained = [sem(f"acc{i}_drained") for i in range(2)]
        q_hi = sem("q_hi")
        k_hi = sem("k_hi")
        m3_max = sem("m3_max")
        q_bd_in = sem("q_bd_in")
        kA_bd_in = sem("kA_bd_in")
        kE_bd_in = sem("kE_bd_in")
        zt_in = sem("zt_in")
        q_bd_free = sem("q_bd_free")
        zt_free = sem("zt_free")
        k_bd_free = sem("k_bd_free")
        e3_made = sem("e3_made")
        e3_read = sem("e3_read")
        rr_made = sem("rr_made")
        un_made = sem("un_made")
        wbd_made = sem("wbd_made")
        rc_ln = sem("rc_ln")
        rc_made = sem("rc_made")
        oT_made = sem("oT_made")
        res_in = [sem(f"res_in{i}") for i in range(2)]
        xm_made = sem("xm_made")
        x2h_read = sem("x2h_read")
        carry = sem("carry")
        dx_made = sem("dx_made")
        xr_made = sem("xr_made")
        xk_scaled = sem("xk_scaled")
        xk_made = sem("xk_made")
        sg_ln = sem("sg_ln")
        sg_exp = sem("sg_exp")
        sg_made = sem("sg_made")
        kr_made = sem("kr_made")
        ka_made = sem("ka_made")
        fin_made = sem("fin_made")
        fin_out = [sem(f"fin_out{i}") for i in range(2)]

        NEXT = ("X", "XA", "R", "A", "B1", "B2", "C1", "C2", "M", "F")
        PRO = [("X", 0), ("X", 1), ("XA", 0), ("R", 0), ("XA", 1), ("A", 0), ("X", 2), ("B1", 0), ("R", 1),
               ("B2", 0), ("XA", 2), ("C1", 0), ("A", 1), ("C2", 0), ("X", 3), ("B1", 1), ("R", 2), ("B2", 1),
               ("XA", 3), ("C1", 1), ("A", 2), ("C2", 1), ("B1", 2), ("R", 3), ("B2", 2), ("C1", 2), ("A", 3),
               ("C2", 2), ("B1", 3), ("B2", 3), ("C1", 3), ("C2", 3), ("M", 0),
               ("F", 0), ("F", 1), ("F", 2), ("F", 3)]
        BODY = [("W", 0), ("D", 0), ("E", 0), ("V", 0), ("X", 0), ("H", 0), ("D", 1), ("O", 0), ("XA", 0), ("OA", 0),
                ("X", 1), ("R", 0),
                ("E", 1), ("N", 0), ("XA", 1), ("A", 0), ("NA", 0), ("B1", 0), ("H", 1), ("B2", 0), ("T", 0),
                ("D", 2), ("O", 1), ("C1", 0), ("OA", 1), ("R", 1), ("X", 2), ("G1", 0), ("C2", 0),
                ("E", 2), ("N", 1), ("XA", 2), ("A", 1), ("NA", 1), ("B1", 1), ("H", 2), ("B2", 1), ("G2", 0),
                ("T", 1), ("D", 3), ("C1", 1), ("O", 2), ("GA", 0), ("OA", 2), ("R", 2), ("X", 3), ("G1", 1),
                ("C2", 1),
                ("E", 3), ("N", 2), ("XA", 3), ("A", 2), ("NA", 2), ("B1", 2), ("H", 3), ("B2", 2), ("G2", 1),
                ("T", 2), ("C1", 2), ("O", 3), ("GA", 1), ("OA", 3), ("R", 3), ("G1", 2), ("C2", 2), ("N", 3),
                ("A", 3), ("NA", 3), ("B1", 3), ("G2", 2), ("B2", 3), ("T", 3), ("GA", 2), ("C1", 3),
                ("G1", 3), ("C2", 3), ("G2", 3), ("M", 0), ("F", 0), ("GA", 3), ("F", 1), ("F", 2), ("F", 3)]
        LAST = [k for k in BODY if k[0] not in NEXT]
        USES = {"X": (0, 0, 0), "R": (1, 0, 0), "A": (2, 0, 1), "B1": (0, 1, 0), "B2": (0, 1, 0), "C1": (0, 1, 0), "C2": (0, 1, 0), "M": (1, 0, 0),
                "F": (0, 2, 0), "W": (1, 0, 1), "V": (1, 0, 0), "D": (1, 0, 0), "E": (0, 2, 0), "H": (1, 0, 1),
                "O": (1, 0, 0), "N": (0, 0, 0), "XA": (0, 0, 0), "OA": (0, 0, 0), "NA": (0, 0, 0), "GA": (0, 0, 0),
                "T": (1, 0, 0), "G1": (2, 0, 0), "G2": (1, 0, 0)}

        class Use:

            def __init__(self, counts):
                self.bank, self.wide, self.acc = counts

        def uses(stages, start):
            at, n = {}, list(start)
            for key in stages:
                at[key] = Use(n)
                n = [a + b for a, b in zip(n, USES[key[0]])]
            return at, n

        _, pro_n = uses(PRO, (0, 0, 0))
        _, body_n = uses(BODY, (0, 0, 0))

        def part2_program(eng, stage):
            at, _ = uses(PRO, (0, 0, 0))
            for key in PRO:
                if key[0] in stage:
                    stage[key[0]](at, 0, key[1])
            with eng.Fori(0, B - 1) as b:
                base = [p + b * n for p, n in zip(pro_n, body_n)]
                at, _ = uses(BODY, base)
                for key in BODY:
                    if key[0] in stage:
                        stage[key[0]](at, b + 1 if key[0] in NEXT else b, key[1])
            base = [p + (B - 1) * n for p, n in zip(pro_n, body_n)]
            at, _ = uses(LAST, base)
            for key in LAST:
                if key[0] in stage:
                    stage[key[0]](at, B - 1, key[1])

        def older(b, c):
            return b * NC + max(c - 1, 0)

        @block.sync
        def _(sp):
            for w, (dst, src) in enumerate([(wq, Wq), (wk, Wk), (wv, Wv), (wo, Wo)]):
                sp.dma_start(dst[:, :, :], src.rearrange("(k p) n -> p k n", p=P)).then_inc(weights_in, 16)
            for w, src in enumerate([W_r, W_k, W_v]):
                sp.dma_start(wnat[:, w, :, :], src.rearrange("(k p) n -> p k n", p=P)).then_inc(weights_in, 16)
            sp.dma_start(bo_all[:, :], bo.rearrange("(a n) -> a n", a=1).to_broadcast([P, A])).then_inc(weights_in, 16)
            for w, src in enumerate([mu_r, mu_k]):
                sp.dma_start(mu[:, w, :], src.rearrange("(k p) -> p k", p=P),
                             allow_slow_non_contiguous=True).then_inc(weights_in, 16)

            with sp.Fori(0, B // GR) as i:
                for s in ROWS:
                    n = i * GR + s
                    sp.wait_ge(p_pe, of(pe_steps, i, "pooled", s) - of(pe_steps, 0, "pooled", s))
                    hold(sp)
                    sp.dma_start(x1in[s][:, :, :], x[bass.ds(n, 1)].rearrange("a (t p) n -> p (a t) n", p=P))\
                        .then_inc(p_in[s], 16)
                for s in ROWS:
                    n = i * GR + s
                    sp.wait_ge(p_dve, of(dve_steps, i, "lmlo", s))
                    hold(sp)
                    sp.dma_start(lm_dram[bass.ds(n, 1)].rearrange("a p n -> p (a n)"),
                                 lm16[s][:, :, :, :].rearrange("p a k m -> p (a k m)")).then_inc(lm_out, 16)
                for s in ROWS:
                    n = i * GR + s
                    sp.wait_ge(p_dve, of(dve_steps, i, "ZT", ITERS - 1, s))
                    hold(sp)
                    sp.dma_start(zt_dram[bass.ds(n, 1)].rearrange("a p n -> p (a n)"),
                                 ZT[s][:, :, :].rearrange("p a m -> p (a m)")).then_inc(zt_out, 16)
            sp.wait_ge(lm_out, 16 * B)
            sp.wait_ge(zt_out, 16 * B)
            sp.wait_ge(p_pe, len(pe_steps) * B // GR)
            sp.wait_ge(setup2, 6)

            def load_bd(dst, lo, key, b, done):
                n = 2 if lo else 1
                src = lm_dram[bass.ds(b, 1)].rearrange("a p (t w k m) -> p (a t) w k m", t=2, w=2, k=KB)
                for h in range(HB):
                    r = slice(h * HS, (h + 1) * HS)
                    for t in range(n):
                        sp.dma_start(dst[r, t, :, h, :], src[r, t, key, :, :]).then_inc(done, 16)

            def stage_X(at, b, c):
                if c == 0:
                    if not isinstance(b, int):
                        sp.wait_ge(m3_max, b)
                        hold(sp)
                    load_bd(kA_bd, False, 1, b, kA_bd_in)
                    if isinstance(b, int):
                        load_bd(q_bd, True, 0, b, q_bd_in)
                if not (isinstance(b, int) and c < 2):
                    sp.wait_ge(norm_x.applied, b * NC + c - 1)
                    hold(sp)
                src = x[bass.ds(b, 1), c * CH:(c + 1) * CH, :].rearrange("a (t p) n -> p (a t) n", p=P)
                sp.dma_start(xin[c % 2][:, :, :], src).then_inc(x_in[c % 2], 16)

            def stage_F(at, b, c):
                if c:
                    return
                if not isinstance(b, int):
                    sp.wait_ge(k_bd_free, b)
                    sp.wait_ge(zt_free, b)
                    hold(sp)
                load_bd(kE_bd, True, 1, b, kE_bd_in)
                sp.dma_start(zt[:, :, :].rearrange("p a m -> p (a m)"),
                             zt_dram[bass.ds(b, 1)].rearrange("a p n -> p (a n)")).then_inc(zt_in, 16)

            def stage_W(at, b, c):
                if not isinstance(b, int):
                    sp.wait_ge(q_bd_free, b + 1)
                    hold(sp)
                    load_bd(q_bd, True, 0, b + 1, q_bd_in)

            def stage_E(at, b, c):
                sp.wait_ge(xm_made, older(b, c))
                hold(sp)
                src = x[bass.ds(b, 1), c * CH:(c + 1) * CH, :].rearrange("a (t p) n -> p (a t) n", p=P)
                sp.dma_start(xres[c % 2][:, :, :], src).then_inc(res_in[c % 2], 16)

            def stage_GA(at, b, c):
                sp.wait_ge(fin_made, b * NC + c + 1)
                hold(sp)
                dst = out[bass.ds(b, 1), c * CH:(c + 1) * CH, :].rearrange("a (t p) n -> p (a t) n", p=P)
                sp.dma_start(dst, ob[c % 2][:, :, :]).then_inc(fin_out[c % 2], 16)

            part2_program(sp, {"X": stage_X, "F": stage_F, "W": stage_W, "E": stage_E, "GA": stage_GA})
            for i in range(2):
                sp.wait_ge(fin_out[i], 16 * B * NC // 2)

        @block.gpsimd
        def _(pool):
            g = nc.gpsimd
            g.memset(ident[:, :], 0.0).then_inc(const_made, 1)
            g.memset(pool_w[:, :], 1.0 / DEN).then_inc(const_made, 1)
            g.memset(head_mask[:, :], 1.0).then_inc(const_made, 1)
            g.memset(ones_pair[:, :], 1.0).then_inc(const_made, 1)
            g.memset(ones32[:, :], 1.0).then_inc(const_made, 1)
            g.memset(neg_sel[:, :, :], 0.0).then_inc(const_made, 1)
            pool.wait_ge(const_made, 6)
            g.affine_select(out=ident[:, :], in_=ident[:, :], compare_op=ALU.not_equal, fill=1.0, base=0,
                            pattern=[[-1, P]], channel_multiplier=1).then_inc(const_made, 1)
            o = M - TM
            g.affine_select(out=pool_w[:, :], in_=pool_w[:, :], compare_op=ALU.is_ge, fill=0.0, base=DEN * o,
                            pattern=[[-DEN, 2 * M - TM]], channel_multiplier=1).then_inc(const_made, 1)
            pool.wait_ge(const_made, 8)
            g.affine_select(out=pool_w[:, :], in_=pool_w[:, :], compare_op=ALU.is_ge, fill=0.0,
                            base=DEN - 1 - DEN * o, pattern=[[DEN, 2 * M - TM]],
                            channel_multiplier=-1).then_inc(const_made, 1)
            g.affine_select(out=head_mask[:, :], in_=head_mask[:, :], compare_op=ALU.is_ge, fill=0.0, base=0,
                            pattern=[[-HS, HB]], channel_multiplier=1).then_inc(const_made, 1)
            pool.wait_ge(const_made, 10)
            g.affine_select(out=head_mask[:, :], in_=head_mask[:, :], compare_op=ALU.is_ge, fill=0.0,
                            base=HS - 1, pattern=[[HS, HB]], channel_multiplier=-1).then_inc(const_made, 1)
            op = ones_pair[:, :].rearrange("p (h d) -> p h d", h=2)
            g.affine_select(out=op, in_=op, compare_op=ALU.is_ge, fill=0.0, base=0,
                            pattern=[[-M, 2], [0, HS]], channel_multiplier=1).then_inc(const_made, 1)
            pool.wait_ge(const_made, 12)
            g.affine_select(out=op, in_=op, compare_op=ALU.is_ge, fill=0.0, base=M - 1,
                            pattern=[[M, 2], [0, HS]], channel_multiplier=-1).then_inc(const_made, 1)
            ns = neg_sel[:, :, :].rearrange("k p (j m) -> k p j m", j=2)
            g.affine_select(out=ns, in_=ns, compare_op=ALU.not_equal, fill=-1.0, base=0,
                            pattern=[[-2, PAIRS], [-1, 2], [0, M]], channel_multiplier=1).then_inc(const_made, 1)
            g.memset(ones4[:, :], 0.0).then_inc(const_made, 1)
            pool.wait_ge(const_made, 15)
            g.memset(ones4[0:PB, :], 1.0).then_inc(const_made, 1)
            pool.wait_ge(const_made, 7)
            g.tensor_tensor(eye[:, :], ident[:, 0:M], ident[:, M:P], ALU.add).then_inc(const_made, 1)

            pool.wait_ge(p_pe, len(pe_steps) * B // GR)
            pool.wait_ge(p_dve, len(dve_steps) * B // GR)
            pool.wait_ge(lm_out, 16 * B)
            pool.wait_ge(zt_out, 16 * B)
            g.memset(q_bd[:, :, :, :, :], 0.0).then_inc(setup2, 1)
            g.memset(kA_bd[:, :, :, :, :], 0.0).then_inc(setup2, 1)
            g.memset(kE_bd[:, :, :, :, :], 0.0).then_inc(setup2, 1)
            g.memset(wbd[:, :, :, :], 0.0).then_inc(setup2, 1)
            g.memset(nmax[:, :, :, :], 0.0).then_inc(setup2, 1)
            g.memset(m1T[:, :], 0.0).then_inc(setup2, 1)

            def stage_OA(at, b, c):
                n = b * NC + c
                pool.wait_ge(res_in[c % 2], 16 * (b * 2 + c // 2 + 1))
                pool.wait_ge(norm_y.applied, n + 1)
                pool.wait_ge(fin_made, b * NC + max(c - 2, 0))
                g.tensor_tensor(xm[c % 3][:, :, :], yy[:, :, :], xres[c % 2][:, :, :],
                                ALU.add).then_inc(xm_made, 1)

            def stage_GA(at, b, c):
                pool.wait_ge(norm_f.applied, b * NC + c + 1)
                g.tensor_tensor(ob[c % 2][:, :, :], ob[c % 2][:, :, :], xm[c % 3][:, :, :],
                                ALU.add).then_inc(fin_made, 1)

            part2_program(pool, {"OA": stage_OA, "GA": stage_GA})

        @block.scalar
        def _(act):
            sc = nc.scalar
            nc.scalar.preload_act_table_set("natural_log_exp_and_others")
            for w, dst in enumerate([wrT, wkT, wvT]):
                act.wait_ge(wT_full, w + 1)
                sc.activation(dst[:, :, :], wide[w % 2][:, 0:KB * A].rearrange("p (k n) -> p k n", k=KB),
                              ACT.Copy).then_inc(wT_drained, 1)
            with act.Fori(0, B // GR) as i:
                for s in ROWS:
                    act.wait_ge(p_dve, of(dve_steps, i, "mv", s))
                    sc.activation(ln1[s][:, :], mv1[s][:, :, 1], ACT.Ln, bias=EPS).then_inc(p_act, 1)
                    act.wait_ge(p_act, of(act_steps, i, "ln", s))
                    sc.activation(rstd1[s][:, :], ln1[s][:, :], ACT.Exp, scale=-0.5).then_inc(p_act, 1)
                for s in ROWS:
                    act.wait_ge(p_pe, of(pe_steps, i, "lT", s))
                    sc.activation(xlT[s][:, :, :], pb[s][1][:, 0:KB * M].rearrange("p (k m) -> p k m", k=KB),
                                  ACT.Copy).then_inc(p_act, 1)
                for s in ROWS:
                    act.wait_ge(p_pe, of(pe_steps, i, "qk", s))
                    qk = pb[s][0][:, 0:2 * KB * M].rearrange("p (a k m) -> p a k m", a=2, k=KB)
                    sc.activation(qlT[s][:, 0, :, :], qk[:, 0, :, :], ACT.Copy, scale=QSCALE).then_inc(p_act, 1)
                    sc.activation(qlT[s][:, 1, :, :], qk[:, 1, :, :], ACT.Copy).then_inc(p_act, 1)
                    act.wait_ge(p_act, of(act_steps, i, "kl", s))
                    act.wait_ge(lm_out, 16 * GR * i)
                    sc.activation(lm16[s][:, 0:2, :, :], qlT[s][:, :, :, :], ACT.Copy).then_inc(p_act, 1)
                for s in ROWS:
                    act.wait_ge(p_dve, of(dve_steps, i, "shift", s))
                    sc.activation(X[s][:, :, :], X[s][:, :, :], ACT.Exp).then_inc(p_act, 1)
                for s in ROWS:
                    act.wait_ge(p_pe, of(pe_steps, i, "XT", s))
                    sc.activation(XT[s][:, :, :], pb[s][0].rearrange("p (a m) -> p a m", a=PAIRS),
                                  ACT.Copy).then_inc(p_act, 1)
                for it in range(ITERS):
                    for s in ROWS:
                        act.wait_ge(p_pe, of(pe_steps, i, "S", it, s))
                        sc.activation(SS[s][:, :, :], pb[s][0].rearrange("p (a m) -> p a m", a=PAIRS),
                                      ACT.Copy).then_inc(p_act, 1)
                    if it < ITERS - 1:
                        for s in ROWS:
                            act.wait_ge(p_pe, of(pe_steps, i, "Z", it, s))
                            sc.activation(Z[s][:, :, :], pb[s][1].rearrange("p (a m) -> p a m", a=PAIRS),
                                          ACT.Copy, scale=0.25).then_inc(p_act, 1)

            act.wait_ge(p_pe, len(pe_steps) * B // GR)
            act.wait_ge(p_dve, len(dve_steps) * B // GR)
            act.wait_ge(lm_out, 16 * B)
            act.wait_ge(zt_out, 16 * B)

            def stage_X(at, b, c):
                if not (isinstance(b, int) and c < 2):
                    act.wait_ge(norm_x.applied, b * NC + c - 1)
                norm_x.root(act, b * NC + c, c)

            def stage_R(at, b, c):
                u, a = at["R", c].bank, at["R", c].acc
                for k in range(KB):
                    act.wait_ge(bank_full[k], u + 1)
                    sc.activation(xT[:, k, :], bank[k][:, :], ACT.Copy).then_inc(bank_drained[k], 1)

            def stage_A(at, b, c):
                u, a = at["A", c].bank, at["A", c].acc
                span = slice(c * CH, (c + 1) * CH)
                for k in range(KB):
                    act.wait_ge(bank_full[k], u + 1)
                    sc.activation(qh[:, k, span], bank[k][:, :], ACT.Copy, scale=QSCALE).then_inc(q_hi, 1)
                for k in range(KB):
                    act.wait_ge(acc_full[k], a + 1)
                    sc.activation(kh[:, k, span], acc[k][:, :], ACT.Copy).then_inc(k_hi, 1)

            def stage_F(at, b, c):
                u = at["F", 0].wide
                for t in range(c * NT, (c + 1) * NT):
                    act.wait_ge(wide_full[t % 2], u + t // 2 + 1)
                    if t >= 2:
                        act.wait_ge(e3_read, b * (NC * NT - 1) + t - 1)
                    sc.activation(e3[t % 2][:, :], wide[t % 2][:, :], ACT.Exp).then_inc(wide_drained[t % 2], 1)

            def stage_W(at, b, c):
                a = at["W", 0].acc
                act.wait_ge(acc_full[0], a + 1)
                sc.activation(uT[:, :], acc[0][:, 0:KB * P], ACT.Copy).then_inc(acc_drained[0], 1)
                act.wait_ge(acc_full[1], a + 1)
                sc.activation(rs3[:, :], acc[1][:, 0:256], ACT.Copy).then_inc(acc_drained[1], 1)
            def stage_V(at, b, c):
                u = at["V", 0].bank
                for j in range(2):
                    r = slice(j * HALF, (j + 1) * HALF)
                    act.wait_ge(bank_full[j], u + 1)
                    act.wait_ge(setup2, 6)
                    sc.activation(wbd[r, :, j, :], bank[j][r, 0:PAIRS * HS].rearrange("p (a d) -> p a d", a=PAIRS),
                                  ACT.Copy).then_inc(bank_drained[j], 1)

            def stage_D(at, b, c):
                u = at["D", c]
                for j in range(2):
                    act.wait_ge(bank_full[j], u.bank + 1)
                    sc.activation(m1T[0:H, j * 256:(j + 1) * 256], bank[j][0:H, 0:256],
                                  ACT.Copy).then_inc(bank_drained[j], 1)

            def stage_E(at, b, c):
                u = at["E", c]
                for j in range(PAIRS // 2):
                    act.wait_ge(wide_full[j % 2], u.wide + j // 2 + 1)
                    sc.activation(p1[:, 2 * j:2 * j + 2, :], wide[j % 2][:, :].rearrange("p (a n) -> p a n", a=2),
                                  ACT.Exp).then_inc(wide_drained[j % 2], 1)

            def stage_H(at, b, c):
                u, n = at["H", c].bank, b * NC + c
                for k in range(KB):
                    act.wait_ge(bank_full[k], u + 1)
                    act.wait_ge(acc_drained[k], at["H", c].acc)
                    sc.activation(rc[:, k, :], bank[k][:, :], ACT.Ln).then_inc(bank_drained[k], 1)
                    act.wait_ge(bank_drained[k], u + 1)
                    sc.activation(rc[:, k, :], rc[:, k, :], ACT.Exp, scale=-1.0).then_inc(rc_made, 1)

            def stage_O(at, b, c):
                u, n = at["O", c].bank, b * NC + c
                norm_y.root(act, n, c)

            def stage_N(at, b, c):
                norm_m.root(act, b * NC + c, c)

            def stage_T(at, b, c):
                u, n = at["T", c].bank, b * NC + c
                act.wait_ge(carry, n)
                act.wait_ge(xk_made, older(b, c))
                for k in range(KB):
                    act.wait_ge(bank_full[k], u + 1)
                    sc.activation(x2T[c % 2][:, k, 1:CH + 1], bank[k][:, :], ACT.Copy).then_inc(bank_drained[k], 1)

            def stage_G1(at, b, c):
                u, n = at["G1", c].bank, b * NC + c
                act.wait_ge(norm_f.stats_made, n)
                for j in range(2):
                    act.wait_ge(bank_full[j], u + 1)
                    sc.activation(sg[:, 2 * j:2 * j + 2, :], bank[j][:, :].rearrange("p (t n) -> p t n", t=2),
                                  ACT.Exp, scale=-1.0).then_inc(bank_drained[j], 1)
                for k in range(KB):
                    act.wait_ge(bank_full[k], u + 2)
                    sc.activation(ka[:, k, :], bank[k][:, :], ACT.Relu).then_inc(bank_drained[k], 1)
                for k in range(KB):
                    act.wait_ge(bank_drained[k], u + 2)
                ins = sc.activation(ka[:, :, :], ka[:, :, :], ACT.Square)
                ins.then_inc(ka_made, 1)
                for j in range(2):
                    act.wait_ge(bank_drained[j], u + 1)
                sc.activation(sg[:, :, :], sg[:, :, :], ACT.Ln, bias=1.0).then_inc(sg_ln, 1)
                act.wait_ge(sg_ln, n + 1)
                sc.activation(sg[:, :, :], sg[:, :, :], ACT.Exp, scale=-1.0).then_inc(sg_made, 1)

            def stage_G2(at, b, c):
                n = b * NC + c
                act.wait_ge(norm_f.applied, n)
                norm_f.root(act, n, c)

            part2_program(act, {"X": stage_X, "R": stage_R, "A": stage_A, "V": stage_V, "D": stage_D, "F": stage_F, "W": stage_W, "E": stage_E, "H": stage_H, "O": stage_O, "N": stage_N, "T": stage_T, "G1": stage_G1,
                                "G2": stage_G2})

        @block.vector
        def _(dve):
            v = nc.vector
            dve.wait_ge(const_made, NCONST)
            for dst, scale in ((eye7, 7.0), (eye15, 15.0), (eye13, 13.0)):
                v.tensor_scalar(dst[:, :], eye[:, :], scale, None, ALU.mult).then_inc(eyes_made, 1)
            dve.wait_ge(eyes_made, 3)
            full = [P, PAIRS, M]

            def pm(t):
                return t.rearrange("p (a m) -> p a m", a=PAIRS)

            for s in ROWS:
                v.memset(pw[s][:, :], 0.0).then_inc(eyes_made, 1)
            dve.wait_ge(eyes_made, 3 + GR)
            with dve.Fori(0, B // GR) as i:
                def done(*k):
                    dve.wait_ge(p_dve, of(dve_steps, i, *k))

                for s in ROWS:
                    dve.wait_ge(p_in[s], 16 * (i + 1))
                    for t in range(NTL):
                        ins = v.bn_stats(st1[s][:, t, :], x1in[s][:, t, :])
                    ins.then_inc(p_dve, 1)
                    done("st", s)
                    hold(dve)
                    for t in range(NTL):
                        ins = v.bn_aggr(mv1[s][:, t, :], st1[s][:, t, :])
                    ins.then_inc(p_dve, 1)
                for s in ROWS:
                    dve.wait_ge(p_act, of(act_steps, i, "rstd", s))
                    v.tensor_tensor(pw[s][:, :].rearrange("p (t c) -> p t c", t=NTL)[:, :, 0:TM],
                                    pool_w[:, M - TM:M].unsqueeze(1).to_broadcast([P, NTL, TM]),
                                    rstd1[s][:, :].unsqueeze(2).to_broadcast([P, NTL, TM]),
                                    ALU.mult).then_inc(p_dve, 1)
                for s in ROWS:
                    dve.wait_ge(p_pe, of(pe_steps, i, "pooled", s))
                    v.bn_stats(stl[s][:, :], pb[s][0][0:M, 0:A]).then_inc(p_dve, 1)
                    done("stl", s)
                    hold(dve)
                    v.bn_aggr(mvl[s][:, :], stl[s][:, :]).then_inc(p_dve, 1)
                    done("mvl", s)
                    v.tensor_scalar(xl[s][:, :], pb[s][0][0:M, 0:A], mvl[s][:, 0:1], None,
                                    ALU.subtract).then_inc(p_dve, 1)
                for s in ROWS:
                    dve.wait_ge(p_act, of(act_steps, i, "lm", s))
                    v.tensor_tensor(lm16[s][:, 2:4, :, :], qlT[s][:, :, :, :], lm16[s][:, 0:2, :, :],
                                    ALU.subtract).then_inc(p_dve, 1)
                    for k in range(KB):
                        ins = v.tensor_tensor(qbd[s][:, k, :, :],
                                              qlT[s][:, 0, k, :].unsqueeze(1).to_broadcast([P, HB, M]),
                                              head_mask[:, :].unsqueeze(2).to_broadcast([P, HB, M]), ALU.mult)
                    ins.then_inc(p_dve, 1)
                for s in ROWS:
                    dve.wait_ge(p_pe, of(pe_steps, i, "logits", s))
                    v.tensor_reduce(mx[s][:, :], pm(pb[s][1]), AX.X, ALU.max).then_inc(p_dve, 1)
                    done("max", s)
                    v.tensor_tensor(X[s][:, :, :], pm(pb[s][1]), mx[s][:, :].unsqueeze(2).to_broadcast(full),
                                    ALU.subtract).then_inc(p_dve, 1)
                for s in ROWS:
                    dve.wait_ge(p_act, of(act_steps, i, "exp", s))
                    v.tensor_reduce(rsum1[s][:, :], X[s][:, :, :], AX.X, ALU.add).then_inc(p_dve, 1)
                    done("sum", s)
                    v.reciprocal(rcp1[s][:, :], rsum1[s][:, :]).then_inc(p_dve, 1)
                    done("rcp", s)
                    v.tensor_tensor(X[s][:, :, :], X[s][:, :, :], rcp1[s][:, :].unsqueeze(2).to_broadcast(full),
                                    ALU.mult).then_inc(p_dve, 1)
                    done("X", s)
                    v.tensor_reduce(rc1[s][:, 0, :], X[s][:, :, :], AX.X, ALU.add).then_inc(p_dve, 1)
                for s in ROWS:
                    dve.wait_ge(p_act, of(act_steps, i, "XT", s))
                    v.tensor_reduce(rc1[s][:, 1, :], XT[s][:, :, :], AX.X, ALU.add).then_inc(p_dve, 1)
                for s in ROWS:
                    dve.wait_ge(p_pe, of(pe_steps, i, "sums", s))
                    v.tensor_reduce(cm[s][:, :, :], pb[s][1][0:PAIRS, 0:2 * P]
                                    .rearrange("p (a h m) -> p a h m", a=2, h=2), AX.X, ALU.max).then_inc(p_dve, 1)
                    done("cm", s)
                    v.tensor_tensor(cg[s][:, 0, :], cm[s][:, 0, :], cm[s][:, 1, :], ALU.mult).then_inc(p_dve, 1)
                    done("cg", s)
                    v.reciprocal(cg[s][:, 1, :], cg[s][:, 0, :]).then_inc(p_dve, 1)
                    done("cr", s)
                    v.tensor_copy(gb[s][:, :, :], cg[s][:, 1, :].unsqueeze(2).to_broadcast([PAIRS, 2, M]))\
                        .then_inc(p_dve, 1)
                for s in ROWS:
                    dve.wait_ge(p_pe, of(pe_steps, i, "g", s))
                    v.tensor_copy(gcol[s][:, :], pb[s][1][:, 0:PAIRS]).then_inc(p_dve, 1)
                    done("gcol", s)
                    gc = gcol[s][:, :].unsqueeze(2).to_broadcast(full)
                    dve.wait_ge(zt_out, 16 * GR * i)
                    v.tensor_tensor(ZT[s][:, :, :], X[s][:, :, :], gc, ALU.mult).then_inc(p_dve, 1)
                    v.tensor_tensor(Z[s][:, :, :], XT[s][:, :, :], gc, ALU.mult).then_inc(p_dve, 1)

                def eyeb(t):
                    return t[:, :].unsqueeze(1).to_broadcast(full)

                for it in range(ITERS):
                    for s in ROWS:
                        dve.wait_ge(p_act, of(act_steps, i, "S", it, s))
                        v.scalar_tensor_tensor(out=T1[s][:, :, :], in0=SS[s][:, :, :], scalar=-1.0, in1=eyeb(eye7),
                                               op0=ALU.mult, op1=ALU.add).then_inc(p_dve, 1)
                    for s in ROWS:
                        dve.wait_ge(p_pe, of(pe_steps, i, "ST1", it, s))
                        v.scalar_tensor_tensor(out=T2[s][:, :, :], in0=pm(pb[s][1]), scalar=-1.0, in1=eyeb(eye15),
                                               op0=ALU.mult, op1=ALU.add).then_inc(p_dve, 1)
                    for s in ROWS:
                        dve.wait_ge(p_pe, of(pe_steps, i, "ST2", it, s))
                        v.scalar_tensor_tensor(out=T3[s][:, :, :], in0=pm(pb[s][0]), scalar=-1.0, in1=eyeb(eye13),
                                               op0=ALU.mult, op1=ALU.add).then_inc(p_dve, 1)
                    for s in ROWS:
                        dve.wait_ge(p_pe, of(pe_steps, i, "ZT", it, s))
                        v.tensor_scalar(ZT[s][:, :, :], pm(pb[s][0]), 0.25, None, ALU.mult).then_inc(p_dve, 1)

            dve.wait_ge(p_act, len(act_steps) * B // GR)
            dve.wait_ge(p_pe, len(pe_steps) * B // GR)
            dve.wait_ge(lm_out, 16 * B)
            dve.wait_ge(zt_out, 16 * B)

            def stage_X(at, b, c):
                dve.wait_ge(x_in[c % 2], 16 * (b * 2 + c // 2 + 1))
                norm_x.stats(dve, xin[c % 2], b * NC + c, c)

            def stage_XA(at, b, c):
                if not (isinstance(b, int) and c < 2):
                    dve.wait_ge(xhat_read, b * NC + c - 1)
                norm_x.apply(dve, xhat[c % 2], xin[c % 2], b * NC + c, c)

            def stage_A(at, b, c):
                u, n = at["A", c], b * NC + c
                span = slice(c * CH, (c + 1) * CH)
                for k in range(KB):
                    dve.wait_ge(q_hi, n * KB + k + 1)
                    v.scalar_tensor_tensor(out=ql[:, k, span], in0=bank[k][:, :], scalar=QSCALE, in1=qh[:, k, span],
                                           op0=ALU.mult, op1=ALU.subtract).then_inc(bank_drained[k], 1)
                for k in range(KB):
                    dve.wait_ge(k_hi, n * KB + k + 1)
                    v.tensor_tensor(kl[:, k, span], acc[k][:, :], kh[:, k, span],
                                    ALU.subtract).then_inc(acc_drained[k], 1)
                for j in range(2):
                    dve.wait_ge(bank_full[j], u.bank + 2)
                    v.tensor_copy(vv[:, c * NT + 2 * j:c * NT + 2 * j + 2, :],
                                  bank[j][:, :].rearrange("p (t n) -> p t n", t=2)).then_inc(bank_drained[j], 1)

            def row_maxima(at, b, c, half):
                u = at[f"B{half + 1}", c]
                for j in (2 * half, 2 * half + 1):
                    dve.wait_ge(wide_full[j % 2], u.wide + 1)
                    v.tensor_reduce(m3[:, 2 * j:2 * j + 2, c], wide[j % 2][:, :].rearrange("p (a n) -> p a n", a=2),
                                    AX.X, ALU.max).then_inc(wide_drained[j % 2], 1)

            def token_maxima(at, b, c, half):
                u = at[f"C{half + 1}", c]
                for t in (2 * half, 2 * half + 1):
                    dve.wait_ge(wide_full[t % 2], u.wide + 1)
                    v.tensor_reduce(m1[:, c * NT + t, :], wide[t % 2][:, :].rearrange("p (h m) -> p h m", h=H),
                                    AX.X, ALU.max).then_inc(wide_drained[t % 2], 1)

            def stage_M(at, b, c):
                u = at["M", 0]
                dve.wait_ge(wide_drained[1], u.wide)
                v.tensor_reduce(m3m[:, :], m3[:, :, :], AX.X, ALU.max).then_inc(m3_max, 1)
                for k in range(KB):
                    dve.wait_ge(bank_full[k], u.bank + 1)
                    v.scalar_tensor_tensor(out=nmax[0:PB, k, :, :],
                                           in0=bank[k][0:PB, 0:P].unsqueeze(1).to_broadcast([PB, PB, P]), scalar=-1.0,
                                           in1=ident[0:PB, 0:PB].unsqueeze(2).to_broadcast([PB, PB, P]),
                                           op0=ALU.mult, op1=ALU.mult).then_inc(bank_drained[k], 1)

            def stage_W(at, b, c):
                u = at["W", 0].bank
                dve.wait_ge(bank_full[1], u + 1)
                v.reciprocal(rr3[:, :], bank[1][:, 0:PAIRS]).then_inc(bank_drained[1], 1)
                dve.wait_ge(bank_full[0], u + 1)
                dve.wait_ge(bank_drained[1], u + 1)
                for j in range(2):
                    r = slice(j * HALF, (j + 1) * HALF)
                    ins = v.tensor_tensor(un[r, :, :],
                                          bank[0][r, 0:KB * P].rearrange("p (a h d) -> p a h d", h=2, d=HS)[:, :, j, :],
                                          rr3[r, :].unsqueeze(2).to_broadcast([HALF, PAIRS, HS]), ALU.mult)
                ins.then_inc(bank_drained[0], 1)

            def stage_H(at, b, c):
                a, n = at["H", c].acc, b * NC + c
                for k in range(KB):
                    dve.wait_ge(acc_full[k], a + 1)
                    dve.wait_ge(rc_made, n * KB + k + 1)
                    v.tensor_tensor(oT[:, k, :], acc[k][:, :], rc[:, k, :], ALU.mult).then_inc(acc_drained[k], 1)

            def stage_O(at, b, c):
                u, n = at["O", c].bank, b * NC + c
                dve.wait_ge(xm_made, n)
                for j in range(2):
                    dve.wait_ge(bank_full[j], u + 1)
                    v.tensor_tensor(yy[:, 2 * j:2 * j + 2, :], bank[j][:, :].rearrange("p (t n) -> p t n", t=2),
                                    bo_all[:, :].unsqueeze(1).to_broadcast([P, 2, A]),
                                    ALU.add).then_inc(bank_drained[j], 1)
                for j in range(2):
                    dve.wait_ge(bank_drained[j], u + 1)
                norm_y.stats(dve, yy, n, c)

            def stage_OA(at, b, c):
                norm_y.apply(dve, yy, yy, b * NC + c, c)

            def stage_N(at, b, c):
                n = b * NC + c
                dve.wait_ge(xm_made, n + 1)
                norm_m.stats(dve, xm[c % 3], n, c)

            def stage_NA(at, b, c):
                dve.wait_ge(x2h_read, b * NC + c)
                norm_m.apply(dve, x2h, xm[c % 3], b * NC + c, c)

            def stage_T(at, b, c):
                u, n = at["T", c].bank, b * NC + c
                dve.wait_ge(xk_made, n)
                if c == 0:
                    v.memset(x2T[0][:, :, 0:1], 0.0).then_inc(carry, 1)
                else:
                    v.tensor_copy(x2T[c % 2][:, :, 0:1], x2T[(c + 1) % 2][:, :, CH:CH + 1]).then_inc(carry, 1)
                dve.wait_ge(carry, n + 1)
                for k in range(KB):
                    dve.wait_ge(bank_drained[k], u + 1)
                cur, prev = x2T[c % 2][:, :, 1:CH + 1], x2T[c % 2][:, :, 0:CH]
                v.tensor_tensor(dx[:, :, :], cur, prev, ALU.subtract).then_inc(dx_made, 1)
                dve.wait_ge(dx_made, n + 1)
                for w, dst, made in ((0, xrT, xr_made), (1, xkT, xk_made)):
                    for k in range(KB):
                        ins = v.scalar_tensor_tensor(out=dst[:, k, :], in0=dx[:, k, :], scalar=mu[:, w, k:k + 1],
                                                     in1=x2T[c % 2][:, k, 0:CH], op0=ALU.mult, op1=ALU.add)
                    ins.then_inc(made, 1)

            def stage_G2(at, b, c):
                u, n = at["G2", c].bank, b * NC + c
                dve.wait_ge(sg_made, n + 1)
                dve.wait_ge(fin_out[c % 2], 16 * (b * 2 + c // 2))
                for j in range(2):
                    dve.wait_ge(bank_full[j], u + 1)
                    v.tensor_tensor(ob[c % 2][:, 2 * j:2 * j + 2, :], bank[j][:, :].rearrange("p (t n) -> p t n", t=2),
                                    sg[:, 2 * j:2 * j + 2, :], ALU.mult).then_inc(bank_drained[j], 1)
                for j in range(2):
                    dve.wait_ge(bank_drained[j], u + 1)
                norm_f.stats(dve, ob[c % 2], n, c)

            def stage_GA(at, b, c):
                norm_f.apply(dve, ob[c % 2], ob[c % 2], b * NC + c, c)

            part2_program(dve, {"X": stage_X, "XA": stage_XA, "OA": stage_OA, "NA": stage_NA, "GA": stage_GA, "A": stage_A, "B1": lambda at, b, c: row_maxima(at, b, c, 0),
                                "B2": lambda at, b, c: row_maxima(at, b, c, 1),
                                "C1": lambda at, b, c: token_maxima(at, b, c, 0),
                                "C2": lambda at, b, c: token_maxima(at, b, c, 1),
                                 "M": stage_M, "W": stage_W, "H": stage_H, "O": stage_O, "N": stage_N, "T": stage_T, "G2": stage_G2})

        @block.tensor
        def _(pe):
            mm = nc.tensor.matmul
            tr = nc.tensor.transpose
            pe.wait_ge(const_made, NCONST)
            pe.wait_ge(weights_in, 16 * NW)
            for w in range(3):
                if w >= 2:
                    pe.wait_ge(wT_drained, w - 1)
                for k in range(KB):
                    for o in range(KB):
                        ins = tr(wide[w % 2][:, k * A + o * P:k * A + (o + 1) * P],
                                 wnat[:, w, o, k * P:(k + 1) * P], ident[:, :])
                ins.then_inc(wT_full, 1)
            pe.wait_ge(wT_drained, 3)

            def heads(dst, left, right, sem_value=None):
                for a in range(PAIRS):
                    for j in range(2):
                        r = slice(j * HALF, (j + 1) * HALF)
                        ins = mm(dst[r, a * M:(a + 1) * M], left[r, a, :], right(r, a), start=True, stop=True)
                return ins

            with pe.Fori(0, B // GR) as i:
                for s in ROWS:
                    pe.wait_ge(p_dve, of(dve_steps, i, "pw", s))
                    for t in range(NTL):
                        ins = mm(pb[s][0][0:M, 0:A], pw[s][:, t * M:(t + 1) * M], x1in[s][:, t, :],
                                 start=(t == 0), stop=(t == NTL - 1))
                    ins.then_inc(p_pe, 1)
                for s in ROWS:
                    pe.wait_ge(p_dve, of(dve_steps, i, "xl", s))
                    hold(pe)
                    for k in range(KB):
                        ins = tr(pb[s][1][:, k * M:(k + 1) * M], xl[s][:, k * P:(k + 1) * P], ident[0:M, 0:M])
                    ins.then_inc(p_pe, 1)
                for s in ROWS:
                    pe.wait_ge(p_act, of(act_steps, i, "xlT", s))
                    for a, w in enumerate((wq, wk)):
                        for o in range(KB):
                            for k in range(KB):
                                ins = mm(pb[s][0][:, (a * KB + o) * M:(a * KB + o + 1) * M],
                                         w[:, k, o * P:(o + 1) * P], xlT[s][:, k, :], start=(k == 0), stop=(k == KB - 1))
                    ins.then_inc(p_pe, 1)
                for s in ROWS:
                    pe.wait_ge(p_dve, of(dve_steps, i, "qbd", s))
                    for a in range(PAIRS):
                        k, j = a // PB, a % PB
                        ins = mm(pb[s][1][:, a * M:(a + 1) * M],
                                 qbd[s][:, k, 2 * j:2 * j + 2, :].rearrange("p h m -> p (h m)"), qlT[s][:, 1, k, :],
                                 start=True, stop=True)
                    ins.then_inc(p_pe, 1)
                for s in ROWS:
                    pe.wait_ge(p_dve, of(dve_steps, i, "X", s))
                    hold(pe)
                    heads(pb[s][0], X[s], lambda r, a: ident[r, r]).then_inc(p_pe, 1)
                for s in ROWS:
                    pe.wait_ge(p_dve, of(dve_steps, i, "cs", s))
                    for a in range(2):
                        ins = tr(pb[s][1][0:PAIRS, a * P:(a + 1) * P], rc1[s][:, a, :], ident[:, :])
                    ins.then_inc(p_pe, 1)
                for s in ROWS:
                    pe.wait_ge(p_dve, of(dve_steps, i, "gb", s))
                    mm(pb[s][1][:, 0:PAIRS], gb[s][:, :, :].rearrange("p h m -> p (h m)"), ident[0:PAIRS, 0:PAIRS],
                       start=True, stop=True).then_inc(p_pe, 1)

                def rhs(t):
                    return lambda r, a: t[r, a, :]

                for it in range(ITERS):
                    for s in ROWS:
                        if it == 0:
                            pe.wait_ge(p_dve, of(dve_steps, i, "Z", s))
                        else:
                            pe.wait_ge(p_act, of(act_steps, i, "Z", it - 1, s))
                            pe.wait_ge(p_dve, of(dve_steps, i, "ZT", it - 1, s))
                        hold(pe)
                        heads(pb[s][0], XT[s], rhs(Z[s])).then_inc(p_pe, 1)
                    for s in ROWS:
                        pe.wait_ge(p_dve, of(dve_steps, i, "T1", it, s))
                        hold(pe)
                        heads(pb[s][1], SS[s], rhs(T1[s])).then_inc(p_pe, 1)
                    for s in ROWS:
                        pe.wait_ge(p_dve, of(dve_steps, i, "T2", it, s))
                        hold(pe)
                        heads(pb[s][0], SS[s], rhs(T2[s])).then_inc(p_pe, 1)
                    for s in ROWS:
                        pe.wait_ge(p_dve, of(dve_steps, i, "T3", it, s))
                        hold(pe)
                        if it < ITERS - 1:
                            heads(pb[s][1], ZT[s], rhs(T3[s])).then_inc(p_pe, 1)
                        heads(pb[s][0], T3[s], rhs(ZT[s])).then_inc(p_pe, 1)

            pe.wait_ge(p_act, len(act_steps) * B // GR)
            pe.wait_ge(p_dve, len(dve_steps) * B // GR)

            def stage_R(at, b, c):
                u, n = at["R", c], b * NC + c
                pe.wait_ge(norm_x.applied, n + 1)
                for k in range(KB):
                    pe.wait_ge(bank_drained[k], u.bank)
                    for t in range(NT):
                        ins = tr(bank[k][:, t * P:(t + 1) * P], xhat[c % 2][:, t, k * P:(k + 1) * P], ident[:, :])
                    ins.then_inc(bank_full[k], 1)

            def stage_A(at, b, c):
                u = at["A", c]
                for o in range(KB):
                    pe.wait_ge(bank_drained[o], u.bank)
                for w, dst, drained, n, full in ((wq, bank, bank_drained, u.bank, bank_full),
                                                 (wk, acc, acc_drained, u.acc, acc_full)):
                    for o in range(KB):
                        pe.wait_ge(drained[o], n)
                        for k in range(KB):
                            ins = mm(dst[o][:, :], w[:, k, o * P:(o + 1) * P], xT[:, k, :], start=(k == 0),
                                     stop=(k == KB - 1))
                            if w is wq and o == 0 and k == 0:
                                ins.then_inc(xhat_read, 1)
                        ins.then_inc(full[o], 1)
                for j in range(2):
                    pe.wait_ge(bank_drained[j], u.bank + 1)
                    for t in range(2):
                        tok = slice((2 * j + t) * P, (2 * j + t + 1) * P)
                        for k in range(KB):
                            ins = mm(bank[j][:, t * A:(t + 1) * A], xT[:, k, tok], wv[:, k, :], start=(k == 0),
                                     stop=(k == KB - 1))
                    ins.then_inc(bank_full[j], 1)

            def row_maxima(at, b, c, half):
                u, a0 = at[f"B{half + 1}", c], at["A", c]
                span = slice(c * CH, (c + 1) * CH)
                for k in range(KB):
                    pe.wait_ge(acc_drained[k], a0.acc + 1)
                if c == 0:
                    pe.wait_ge(q_bd_in, 16 * 2 * HB * (b + 1))
                for j in (2 * half, 2 * half + 1):
                    pe.wait_ge(wide_drained[j % 2], u.wide)
                    for a in range(2):
                        k, q = (2 * j + a) // PB, (2 * j + a) % PB
                        ins = mm(wide[j % 2][:, a * CH:(a + 1) * CH],
                                 q_bd[:, 0, k, 2 * q:2 * q + 2, :].rearrange("p h m -> p (h m)"), kh[:, k, span],
                                 start=True, stop=True)
                    ins.then_inc(wide_full[j % 2], 1)

            def token_maxima(at, b, c, half):
                u = at[f"C{half + 1}", c]
                for k in range(KB):
                    pe.wait_ge(bank_drained[k], at["A", c].bank + 1)
                if c == 0:
                    pe.wait_ge(kA_bd_in, 16 * HB * (b + 1))
                for t in (2 * half, 2 * half + 1):
                    pe.wait_ge(wide_drained[t % 2], u.wide)
                    tok = slice(c * CH + t * P, c * CH + (t + 1) * P)
                    for k in range(KB):
                        ins = mm(wide[t % 2][:, k * 512:(k + 1) * 512], qh[:, k, tok],
                                 kA_bd[:, 0, k, :, :].rearrange("p h m -> p (h m)"), start=True, stop=True)
                    ins.then_inc(wide_full[t % 2], 1)

            def stage_M(at, b, c):
                u = at["M", 0]
                for j in range(2):
                    pe.wait_ge(bank_drained[j], u.bank)
                    pe.wait_ge(wide_drained[j], u.wide)
                    pe.wait_ge(acc_drained[j], u.acc)
                pe.wait_ge(m3_max, b + 1)
                for k in range(KB):
                    tr(bank[k][0:PB, 0:P], m3m[:, k * PB:(k + 1) * PB], ident[:, :]).then_inc(bank_full[k], 1)

            def stage_F(at, b, c):
                u = at["F", 0]
                NTL = NC * NT

                def sums(t):
                    pe.wait_ge(wide_drained[t % 2], u.wide + t // 2 + 1)
                    if t == 0:
                        for j in range(2):
                            pe.wait_ge(acc_drained[j], at["F", 0].acc)
                    first, last = t == 0, t == NTL - 1
                    for q in range(4):
                        ins = mm(acc[1][32 * q:32 * q + 32, 0:256], ones32[:, :], e3[t % 2][:, q * 256:(q + 1) * 256],
                                 start=first, stop=last, skip_group_check=True)
                    if last:
                        ins.then_inc(acc_full[1], 1)
                    for a in range(PAIRS):
                        k, q = a // PB, a % PB
                        ins = mm(acc[0][32 * q:32 * q + 32, k * P:(k + 1) * P], vv[:, t, 32 * a:32 * a + 32],
                                 e3[t % 2][:, a * P:(a + 1) * P], start=(first and k == 0), stop=last,
                                 skip_group_check=True)
                    ins.then_inc(acc_full[0] if last else e3_read, 1)

                if c == 0:
                    for k in range(KB):
                        pe.wait_ge(bank_drained[k], at["M", 0].bank + 1)
                for t in range(c * NT, (c + 1) * NT):
                    pe.wait_ge(wide_drained[t % 2], u.wide + t // 2)
                    tok = slice(t * P, (t + 1) * P)
                    for k in range(KB):
                        dst = wide[t % 2][:, k * 512:(k + 1) * 512]
                        qb = [q_bd[:, e, k, :, :].rearrange("p h m -> p (h m)") for e in range(2)]
                        mm(dst, ones4[:, :], nmax[:, k, :, :].rearrange("p a n -> p (a n)"), start=True, stop=False)
                        mm(dst, kh[:, k, tok], qb[0], start=False, stop=False)
                        mm(dst, kh[:, k, tok], qb[1], start=False, stop=False)
                        ins = mm(dst, kl[:, k, tok], qb[0], start=False, stop=True)
                    ins.then_inc(wide_full[t % 2], 1)
                    if t:
                        sums(t - 1)
                if c == NC - 1:
                    sums(NTL - 1)

            def stage_W(at, b, c):
                u, a0 = at["W", 0].bank, at["W", 0].acc
                pe.wait_ge(acc_drained[0], a0 + 1)
                pe.wait_ge(bank_drained[0], u)
                for k in range(KB):
                    ins = tr(bank[0][:, k * P:(k + 1) * P], uT[:, k * P:(k + 1) * P], ident[:, :])
                    if k == 0:
                        ins.then_inc(q_bd_free, 1)
                ins.then_inc(bank_full[0], 1)
                pe.wait_ge(acc_drained[1], a0 + 1)
                pe.wait_ge(bank_drained[1], u)
                for h in range(2):
                    ins = mm(bank[1][:, 0:PAIRS].rearrange("p (q h) -> p h q", h=2)[:, h, :],
                             rs3[:, h * P:(h + 1) * P], ident[:, 0:P:32], start=True, stop=True)
                ins.then_inc(bank_full[1], 1)

            def stage_V(at, b, c):
                u, w = at["V", 0].bank, at["W", 0].bank + 1
                pe.wait_ge(zt_in, 16 * (b + 1))
                pe.wait_ge(bank_drained[0], w)
                for j in range(2):
                    pe.wait_ge(bank_drained[j], u)
                hold(pe)
                for j in range(2):
                    r = slice(j * HALF, (j + 1) * HALF)
                    for a in range(PAIRS):
                        ins = mm(bank[j][r, a * HS:(a + 1) * HS], zt[r, a, :], un[r, a, :], start=True, stop=True)
                    ins.then_inc(bank_full[j], 1)

            def stage_D(at, b, c):
                u = at["D", c]
                for j in range(2):
                    pe.wait_ge(bank_drained[j], u.bank)
                    for t in range(2):
                        ins = tr(bank[j][0:H, t * P:(t + 1) * P], m1[:, c * NT + 2 * j + t, :], ident[:, :])
                    ins.then_inc(bank_full[j], 1)

            def stage_E(at, b, c):
                u = at["E", c]
                if c == 0:
                    pe.wait_ge(kE_bd_in, 16 * 2 * HB * (b + 1))
                for j in range(2):
                    pe.wait_ge(bank_drained[j], at["D", c].bank + 1)
                span = slice(c * CH, (c + 1) * CH)
                for j in range(PAIRS // 2):
                    pe.wait_ge(wide_drained[j % 2], u.wide + j // 2)
                    for i2 in range(2):
                        a = 2 * j + i2
                        k, q = a // PB, a % PB
                        dst = wide[j % 2][:, i2 * CH:(i2 + 1) * CH]
                        kb = [kE_bd[:, e, k, 2 * q:2 * q + 2, :].rearrange("p h m -> p (h m)") for e in range(2)]
                        mm(dst, neg_sel[:, a, :], m1T[:, :], start=True, stop=False)
                        mm(dst, kb[0], qh[:, k, span], start=False, stop=False)
                        mm(dst, kb[0], ql[:, k, span], start=False, stop=False)
                        ins = mm(dst, kb[1], qh[:, k, span], start=False, stop=True)
                    ins.then_inc(wide_full[j % 2], 1)

            def stage_H(at, b, c):
                u, e = at["H", c], at["E", c].wide
                if c == 0:
                    for j in range(2):
                        pe.wait_ge(bank_drained[j], at["V", 0].bank + 1)
                for j in range(PAIRS // 2):
                    pe.wait_ge(wide_drained[j % 2], e + j // 2 + 1)
                    k = 2 * j // PB
                    if j % 2 == 0:
                        pe.wait_ge(bank_drained[k], u.bank)
                        pe.wait_ge(acc_drained[k], u.acc)
                    for a in (2 * j, 2 * j + 1):
                        r = slice(32 * (a % PB), 32 * (a % PB) + 32)
                        s_ = mm(bank[k][r, :], ones_pair[:, :], p1[:, a, :], start=True, stop=True)
                        if a == 0 and c == 0:
                            s_.then_inc(zt_free, 1)
                        if a == 0 and c == NC - 1:
                            s_.then_inc(k_bd_free, 1)
                        o_ = mm(acc[k][r, :], wbd[:, a, :, :].rearrange("p h d -> p (h d)"), p1[:, a, :], start=True,
                                stop=True)
                    if j % 2 == 1:
                        s_.then_inc(bank_full[k], 1)
                        o_.then_inc(acc_full[k], 1)

            def stage_O(at, b, c):
                u, h = at["O", c].bank, at["H", c].acc
                for k in range(KB):
                    pe.wait_ge(acc_drained[k], h + 1)
                for j in range(2):
                    pe.wait_ge(bank_drained[j], u)
                    for t in range(2):
                        dst = bank[j][:, t * A:(t + 1) * A]
                        tok = slice((2 * j + t) * P, (2 * j + t + 1) * P)
                        for k in range(KB):
                            ins = mm(dst, oT[:, k, tok], wo[:, k, :], start=(k == 0), stop=(k == KB - 1))
                    ins.then_inc(bank_full[j], 1)

            def stage_T(at, b, c):
                u, n = at["T", c].bank, b * NC + c
                pe.wait_ge(norm_m.applied, n + 1)
                for k in range(KB):
                    pe.wait_ge(bank_drained[k], u)
                    for t in range(NT):
                        ins = tr(bank[k][:, t * P:(t + 1) * P], x2h[:, t, k * P:(k + 1) * P], ident[:, :])
                    ins.then_inc(bank_full[k], 1)

            def stage_G1(at, b, c):
                u, n = at["G1", c].bank, b * NC + c
                pe.wait_ge(xr_made, n + 1)
                for j in range(2):
                    pe.wait_ge(bank_drained[j], u)
                    for t in range(2):
                        tok = slice((2 * j + t) * P, (2 * j + t + 1) * P)
                        for k in range(KB):
                            ins = mm(bank[j][:, t * A:(t + 1) * A], xrT[:, k, tok], wrT[:, k, :], start=(k == 0),
                                     stop=(k == KB - 1))
                            if j == 0 and t == 0 and k == 0:
                                ins.then_inc(x2h_read, 1)
                    ins.then_inc(bank_full[j], 1)
                pe.wait_ge(xk_made, n + 1)
                for o in range(KB):
                    pe.wait_ge(bank_drained[o], u + 1)
                    for k in range(KB):
                        ins = mm(bank[o][:, :], wkT[:, k, o * P:(o + 1) * P], xkT[:, k, :], start=(k == 0),
                                 stop=(k == KB - 1))
                    ins.then_inc(bank_full[o], 1)

            def stage_G2(at, b, c):
                u, n = at["G2", c].bank, b * NC + c
                pe.wait_ge(ka_made, n + 1)
                for j in range(2):
                    pe.wait_ge(bank_drained[j], u)
                    for t in range(2):
                        tok = slice((2 * j + t) * P, (2 * j + t + 1) * P)
                        for k in range(KB):
                            ins = mm(bank[j][:, t * A:(t + 1) * A], ka[:, k, tok], wvT[:, k, :], start=(k == 0),
                                     stop=(k == KB - 1))
                    ins.then_inc(bank_full[j], 1)

            part2_program(pe, {"R": stage_R, "A": stage_A, "B1": lambda at, b, c: row_maxima(at, b, c, 0),
                                "B2": lambda at, b, c: row_maxima(at, b, c, 1),
                                "C1": lambda at, b, c: token_maxima(at, b, c, 0),
                                "C2": lambda at, b, c: token_maxima(at, b, c, 1),
                                 "V": stage_V, "D": stage_D, "M": stage_M, "F": stage_F, "W": stage_W, "E": stage_E, "H": stage_H, "O": stage_O, "T": stage_T, "G1": stage_G1,
                               "G2": stage_G2})


_INS = ["L0_attn_x", "L0_attn_Wk", "L0_attn_Wq", "L0_attn_Wv", "L0_attn_Wo", "L0_attn_bo", "L0_ffn_W_r",
        "L0_ffn_W_k", "L0_ffn_W_v", "L0_ffn_mu_r", "L0_ffn_mu_k"]


def kernel(**inputs):
    import numpy as np
    import concourse.bacc as bacc
    from concourse.bass_utils import run_bass_kernel_spmd

    nc = bacc.Bacc("TRN2", target_bir_lowering=False, num_devices=1)
    arrays, args = {}, []
    for name in _INS:
        a = np.ascontiguousarray(inputs[name])
        arrays[f"in_{name}"] = a
        args.append(nc.dram_tensor(f"in_{name}", a.shape, mybir.dt.from_np(a.dtype), kind="ExternalInput").ap())
    shape = inputs["L0_attn_x"].shape
    args.append(nc.dram_tensor("out", shape, F32, kind="ExternalOutput").ap())
    sandwich(nc, *args)
    return run_bass_kernel_spmd(nc, [arrays], core_ids=[0]).results[0]["out"]
```

```python
from contextlib import ExitStack

import concourse.bass as bass
from concourse import mybir

F32 = mybir.dt.float32
F16 = mybir.dt.float16
ALU = mybir.AluOpType
ACT = mybir.ActivationFunctionType
AX = mybir.AxisListType

P = 128
HALF = P // 2


def sandwich(nc, x, Wk, Wq, Wv, Wo, bo, W_r, W_k, W_v, mu_r, mu_k, out):
    B, L, A = x.shape
    H, HS, M, ITERS = 16, 16, 64, 6
    KB = A // P
    HB = H // KB
    PAIRS, PB = H // 2, H // 2 // KB
    CH = 512
    NC, NT = L // CH, CH // P
    DEN = L // M
    TM = P // DEN
    EPS = 1e-5
    QSCALE = HS ** -0.5
    assert HS * HB == P and M == HALF and NC == 4 and NT == 4

    ctx = ExitStack()
    with ctx:
        def sb(name, shape, dt=F32, c=ctx):
            return c.enter_context(nc.sbuf_tensor(name, shape, dt))

        def sem(name):
            return ctx.enter_context(nc.semaphore(name))

        bank = [ctx.enter_context(nc.psum_tensor(f"bank{i}", [P, 512], F32)) for i in range(2)]
        wide = [ctx.enter_context(nc.psum_tensor(f"wide{i}", [P, 1024], F32)) for i in range(2)]
        acc = [ctx.enter_context(nc.psum_tensor(f"acc{i}", [P, 512], F32)) for i in range(2)]

        lm_dram = nc.dram_tensor("landmarks", [B, P, 4 * KB * M], F16).ap()
        zt_dram = nc.dram_tensor("inverse", [B, P, PAIRS * M], F32).ap()

        ident = sb("ident", [P, P])
        pool_w = sb("pool_w", [P, 2 * M - TM])
        head_mask = sb("head_mask", [P, HB])
        ones_pair = sb("ones_pair", [P, 2 * HS])
        ones32 = sb("ones32", [P, 32])
        neg_sel = sb("neg_sel", [P, PAIRS, P], F16)
        eye = sb("eye", [P, M])
        ident16 = sb("ident16", [P, P], F16)
        eye7 = sb("eye7", [P, M], F16)
        eye15 = sb("eye15", [P, M], F16)
        eye13 = sb("eye13", [P, M], F16)
        WS = 16.0
        w16 = sb("w16", [P, 3, 2, KB, A], F16)
        wo = sb("wo", [P, KB, A])
        wrT = sb("wrT", [P, KB, A])
        wkT = sb("wkT", [P, KB, A])
        wvT = sb("wvT", [P, KB, A])
        bo_all = sb("bo_all", [P, A])
        mu = sb("mu", [P, 2, KB])

        const_made = sem("const_made")
        weights_in = sem("weights_in")
        w16_hi = sem("w16_hi")
        w16_lo = sem("w16_lo")
        eyes_made = sem("eyes_made")
        wT_full = sem("wT_full")
        wT_drained = sem("wT_drained")
        NCONST = 15
        NW = 7 + 1 + 2

        part1 = ctx.enter_context(ExitStack())
        GR = 4
        ROWS = range(GR)
        NTL = NC * NT
        wq = sb("wq", [P, KB, A], c=part1)
        wk = sb("wk", [P, KB, A], c=part1)
        wv = sb("wv", [P, KB, A], c=part1)
        wnat = sb("wnat", [P, 3, KB, A], c=part1)
        NX1 = 3
        x1in = [sb(f"x1in{i}", [P, NTL, A], c=part1) for i in range(NX1)]
        st1 = [sb(f"st1{s}", [P, NTL, 6], c=part1) for s in ROWS]
        mv1 = [sb(f"mv1{s}", [P, NTL, 2], c=part1) for s in ROWS]
        ln1 = [sb(f"ln1{s}", [P, NTL], c=part1) for s in ROWS]
        rstd1 = [sb(f"rstd1{s}", [P, NTL], c=part1) for s in ROWS]
        pw = [sb(f"pw{i}", [P, NTL * (M + TM)], c=part1) for i in range(2)]
        stl = [sb(f"stl{s}", [M, 6], c=part1) for s in ROWS]
        mvl = [sb(f"mvl{s}", [M, 2], c=part1) for s in ROWS]
        xl = [sb(f"xl{s}", [M, A], c=part1) for s in ROWS]
        xlT = [sb(f"xlT{s}", [P, KB, M], c=part1) for s in ROWS]
        qlT = [sb(f"qlT{s}", [P, 2, KB, M], c=part1) for s in ROWS]
        lm16 = [sb(f"lm16{s}", [P, 4, KB, M], F16, c=part1) for s in ROWS]
        qbd = [sb(f"qbd{i}", [P, KB, HB, M], c=part1) for i in range(2)]
        X = [sb(f"X{s}", [P, PAIRS, M], c=part1) for s in ROWS]
        XT = [sb(f"XT{s}", [P, PAIRS, M], c=part1) for s in ROWS]
        mx = [sb(f"mx{s}", [P, PAIRS], c=part1) for s in ROWS]
        rsum1 = [sb(f"rsum1{s}", [P, PAIRS], c=part1) for s in ROWS]
        rcp1 = [sb(f"rcp1{s}", [P, PAIRS], c=part1) for s in ROWS]
        rc1 = [sb(f"rc1{s}", [P, 2, PAIRS], c=part1) for s in ROWS]
        cm = [sb(f"cm{s}", [PAIRS, 2, 2], c=part1) for s in ROWS]
        cg = [sb(f"cg{s}", [PAIRS, 2, 2], c=part1) for s in ROWS]
        gb = [sb(f"gb{s}", [PAIRS, 2, M], c=part1) for s in ROWS]
        gcol = [sb(f"gcol{s}", [P, PAIRS], c=part1) for s in ROWS]
        XS, ZS, SS = 64.0, 16.0, 16.0
        XT_bd = [sb(f"XT_bd{s}", [P, PAIRS, 2, P], F16, c=part1) for s in ROWS]
        ST_d = [sb(f"ST_d{s}", [P, PAIRS, 2, M], F16, c=part1) for s in ROWS]
        ST_bd = [sb(f"ST_bd{s}", [P, PAIRS, 2, P], F16, c=part1) for s in ROWS]
        Z_d = [sb(f"Z_d{s}", [P, PAIRS, 2, M], F16, c=part1) for s in ROWS]
        ZT_d = [sb(f"ZT_d{s}", [P, PAIRS, 2, M], F16, c=part1) for s in ROWS]
        ZT_bd = [sb(f"ZT_bd{s}", [P, PAIRS, 2, P], F16, c=part1) for s in ROWS]
        pb = [[bank[0][:, :], bank[1][:, :]], [wide[0][:, 0:512], wide[0][:, 512:1024]],
              [wide[1][:, 0:512], wide[1][:, 512:1024]], [acc[0][:, :], acc[1][:, :]]]

        p_in = [sem(f"p_in{s}") for s in ROWS]
        p_pooled = sem("p_pooled")
        p_zero = sem("p_zero")
        p_pe = sem("p_pe")
        p_act = sem("p_act")
        p_dve = sem("p_dve")
        lm_out = sem("lm_out")
        zt_out = sem("zt_out")

        pe_steps = ([(n, s) for n in ("lT", "qk", "logits", "XT", "sums", "g") for s in ROWS]
                    + [(n, i, s) for i in range(ITERS) for names in (["S"], ["T2"], ["T3"], ["Z", "ZT"])
                       for s in ROWS for n in names if not (n == "Z" and i == ITERS - 1)])
        act_steps = ([(n, s) for names in (["ln", "rstd"], ["xlT"], ["ql", "kl", "lm"], ["exp"], ["XT", "XThi"],
                                           ["Zhi", "ZThi"])
                      for s in ROWS for n in names]
                     + [(n, i, s) for i in range(ITERS) for names in (["S"], ["ZTbd"], ["T2"], ["T3"], ["Z", "ZT"])
                        for s in ROWS for n in names
                        if not (n in ("Z", "ZT", "ZTbd") and i == ITERS - 1)])
        STATS = ([("st", 0), ("st", 1)] + [k for s in range(2, GR) for k in (("pw", s - 2), ("st", s))]
                 + [("pw", GR - 2), ("pw", GR - 1)])
        dve_steps = ([(n, s) for name, s in STATS for n in (("st", "mv") if name == "st" else ("pw",))]
                     + [(n, s) for names in (["stl", "mvl", "xl"], ["lmlo", "qbd"],
                                           ["max", "shift"], ["sum", "rcp", "X", "rs"], ["cs", "XTlo", "XTbd"],
                                           ["cm", "cg", "cr", "gb"], ["gcol", "gX", "gXT"], ["Zlo", "ZTlo"])
                      for s in ROWS for n in names]
                     + [(n, i, s) for i in range(ITERS)
                        for names in (["Slo", "Sbd"], ["T2lo"], ["T3lo", "T3bd"], ["Zlo", "ZTlo"])
                        for s in ROWS for n in names if not (n == "Zlo" and i == ITERS - 1)])

        def pm(t):
            return t.rearrange("p (a m) -> p a m", a=PAIRS)

        def of(steps, i, *key):
            return i * len(steps) + steps.index(key) + 1

        part2 = ctx.enter_context(ExitStack())
        block = ctx.enter_context(nc.Block())

        part1.close()
        xin = [sb(f"xin{i}", [P, NT, A], c=part2) for i in range(2)]
        xhat = [sb(f"xhat{i}", [P, NT, A], c=part2) for i in range(2)]
        xT = sb("xT", [P, 2, KB, CH], F16, c=part2)
        qh = sb("qh", [P, KB, L], F16, c=part2)
        ql = sb("ql", [P, KB, L], F16, c=part2)
        kh = sb("kh", [P, KB, CH], F16, c=part2)
        kl = sb("kl", [P, KB, CH], F16, c=part2)
        k_stack = sb("k_stack", [P, PAIRS, L], F16, c=part2)
        q_stack = sb("q_stack", [P, PAIRS, P], F16, c=part2)
        vv = sb("vv", [P, L // P, A], c=part2)
        m3 = sb("m3", [P, PAIRS, NC], c=part2)
        m3m = sb("m3m", [P, PAIRS], c=part2)
        m1 = sb("m1", [P, L // P, H], c=part2)
        m1T = sb("m1T", [P, CH], F16, c=part2)
        q_bd = sb("q_bd", [P, 1, KB, HB, M], F16, c=part2)
        kA_bd = sb("kA_bd", [P, 1, KB, HB, M], F16, c=part2)
        kE_bd = sb("kE_bd", [P, 2, KB, HB, M], F16, c=part2)
        e3 = [sb(f"e3{i}", [P, 2 * 512], c=part2) for i in range(2)]
        uT = sb("uT", [P, KB * P], c=part2)
        rs3 = sb("rs3", [P, 256], c=part2)
        rr3 = sb("rr3", [P, PAIRS], c=part2)
        un = sb("un", [P, PAIRS, HS], c=part2)
        zt = sb("zt", [P, PAIRS, M], c=part2)
        wbd = sb("wbd", [P, PAIRS, 2, HS], c=part2)
        p1 = sb("p1", [P, PAIRS, CH], c=part2)
        oT = sb("oT", [P, KB, CH], c=part2)
        yy = sb("yy", [P, NT, A], c=part2)
        xres = sb("xres", [P, NT, A], c=part2)
        xm = [sb(f"xm{i}", [P, NT, A], c=part2) for i in range(3)]
        x2h = sb("x2h", [P, NT, A], c=part2)
        x2T = sb("x2T", [P, KB, CH + 1], c=part2)
        xkT = sb("xkT", [P, KB, CH], c=part2)
        xrT = sb("xrT", [P, KB, CH], c=part2)
        sg = sb("sg", [P, NT, A], c=part2)

        ka = sb("ka", [P, KB, CH], c=part2)
        ob = [sb(f"ob{i}", [P, NT, A], c=part2) for i in range(2)]

        held = {nc.sync.engine: sem("held_sp"), nc.scalar.engine: sem("held_act"), nc.vector.engine: sem("held_dve"),
                nc.gpsimd.engine: sem("held_pool"), nc.tensor.engine: sem("held_pe")}

        def hold(eng):
            eng.sem_inc(held[eng.engine], 1)

        class Norm:

            def __init__(self, name, copies=1):
                self.st = sb(name + "_st", [P, NT, 6], c=part2)
                self.mv = [sb(f"{name}_mv{i}", [P, NT, 2], c=part2) for i in range(copies)]
                self.ln = sb(name + "_ln", [P, NT], c=part2)
                self.rstd = [sb(f"{name}_rstd{i}", [P, NT], c=part2) for i in range(copies)]
                self.stats_made = sem(name + "_stats")
                self.mv_made = sem(name + "_mv")
                self.ln_made = sem(name + "_ln")
                self.rstd_made = sem(name + "_rstd")
                self.applied = sem(name + "_applied")
                self.copies = copies

            def stats(self, dve, src, g, c):
                dve.wait_ge(self.mv_made, g)
                for t in range(NT):
                    ins = nc.vector.bn_stats(self.st[:, t, :], src[:, t, :])
                ins.then_inc(self.stats_made, 1)
                dve.wait_ge(self.stats_made, g + 1)
                if not (isinstance(g, int) and g < self.copies):
                    dve.wait_ge(self.applied, g + 1 - self.copies)
                hold(dve)
                for t in range(NT):
                    ins = nc.vector.bn_aggr(self.mv[c % self.copies][:, t, :], self.st[:, t, :])
                ins.then_inc(self.mv_made, 1)

            def root(self, act, g, c):
                act.wait_ge(self.rstd_made, g)
                act.wait_ge(self.mv_made, g + 1)
                nc.scalar.activation(self.ln[:, :], self.mv[c % self.copies][:, :, 1], ACT.Ln,
                                     bias=EPS).then_inc(self.ln_made, 1)
                act.wait_ge(self.ln_made, g + 1)
                nc.scalar.activation(self.rstd[c % self.copies][:, :], self.ln[:, :], ACT.Exp,
                                     scale=-0.5).then_inc(self.rstd_made, 1)

            def apply(self, dve, dst, src, g, c):
                dve.wait_ge(self.rstd_made, g + 1)
                k = c % self.copies
                for t in range(NT):
                    ins = nc.vector.tensor_scalar(dst[:, t, :], src[:, t, :], self.mv[k][:, t, 0:1],
                                                  self.rstd[k][:, t:t + 1], ALU.subtract, ALU.mult)
                ins.then_inc(self.applied, 1)

        norm_x = Norm("norm_x", 2)
        norm_y = Norm("norm_y")
        norm_m = Norm("norm_m")
        norm_f = Norm("norm_f")

        setup2 = sem("setup2")
        x_in = [sem(f"x_in{i}") for i in range(2)]
        xhat_read = sem("xhat_read")
        bank_full = [sem(f"bank{i}_full") for i in range(2)]
        bank_drained = [sem(f"bank{i}_drained") for i in range(2)]
        wide_full = [sem(f"wide{i}_full") for i in range(2)]
        wide_drained = [sem(f"wide{i}_drained") for i in range(2)]
        acc_full = [sem(f"acc{i}_full") for i in range(2)]
        acc_drained = [sem(f"acc{i}_drained") for i in range(2)]
        x_hi = sem("x_hi")
        q_hi = sem("q_hi")
        k_hi = sem("k_hi")
        m3_max = sem("m3_max")
        q_bd_in = sem("q_bd_in")
        kA_bd_in = sem("kA_bd_in")
        kE_bd_in = sem("kE_bd_in")
        k_stack_in = sem("k_stack_in")
        q_stack_in = sem("q_stack_in")
        NKS = 3 * 4
        zt_in = sem("zt_in")
        q_bd_free = sem("q_bd_free")
        zt_free = sem("zt_free")
        k_bd_free = sem("k_bd_free")
        e3_read = sem("e3_read")
        rc_made = sem("rc_made")
        res_in = [sem(f"res_in{i}") for i in range(2)]
        xm_made = sem("xm_made")
        x2h_read = sem("x2h_read")
        carry = sem("carry")
        dx_made = sem("dx_made")
        xr_made = sem("xr_made")
        xk_made = sem("xk_made")
        sg_ln = sem("sg_ln")
        sg_made = sem("sg_made")
        ka_made = sem("ka_made")
        fin_made = sem("fin_made")
        fin_out = [sem(f"fin_out{i}") for i in range(2)]

        NEXT = ("X", "XA", "R", "A", "B1", "B2", "C1", "C2", "M", "F")
        PRO = [("X", 0), ("X", 1), ("XA", 0), ("R", 0), ("XA", 1), ("A", 0), ("X", 2), ("B1", 0), ("R", 1),
               ("B2", 0), ("XA", 2), ("C1", 0), ("A", 1), ("C2", 0), ("X", 3), ("B1", 1), ("R", 2), ("B2", 1),
               ("XA", 3), ("C1", 1), ("A", 2), ("C2", 1), ("B1", 2), ("R", 3), ("B2", 2), ("C1", 2), ("A", 3),
               ("C2", 2), ("B1", 3), ("B2", 3), ("C1", 3), ("C2", 3), ("M", 0),
               ("F", 0), ("F", 1), ("F", 2), ("F", 3)]
        BODY = [("W", 0), ("D", 0), ("E", 0), ("V", 0), ("X", 0), ("H", 0), ("D", 1), ("O", 0), ("XA", 0),
                ("E", 1), ("R", 0), ("OA", 0), ("N", 0), ("A", 0), ("X", 1), ("NA", 0), ("XA", 1), ("B1", 0),
                ("H", 1), ("B2", 0), ("T", 0), ("D", 2), ("TA", 0), ("O", 1), ("R", 1), ("C1", 0), ("OA", 1),
                ("G1", 0), ("C2", 0), ("E", 2), ("N", 1), ("X", 2), ("XA", 2), ("GB", 0), ("A", 1), ("NA", 1),
                ("B1", 1), ("H", 2), ("B2", 1), ("T", 1), ("G2", 0), ("D", 3), ("TA", 1), ("O", 2), ("R", 2),
                ("GS", 0), ("C1", 1), ("OA", 2), ("GA", 0), ("G1", 1), ("C2", 1), ("E", 3), ("N", 2), ("X", 3),
                ("XA", 3), ("GB", 1), ("A", 2), ("NA", 2), ("B1", 2), ("H", 3), ("B2", 2), ("T", 2), ("G2", 1),
                ("TA", 2), ("O", 3), ("R", 3), ("GS", 1), ("C1", 2), ("OA", 3), ("GA", 1), ("A", 3), ("C2", 2),
                ("B1", 3), ("G1", 2), ("B2", 3), ("C1", 3), ("C2", 3), ("M", 0), ("GB", 2), ("N", 3),
                ("NA", 3), ("F", 0), ("T", 3), ("G2", 2), ("GS", 2), ("F", 1), ("TA", 3), ("GA", 2), ("G1", 3),
                ("F", 2), ("GB", 3), ("G2", 3), ("GS", 3), ("GA", 3), ("F", 3)]
        LAST = [k for k in BODY if k[0] not in NEXT]
        USES = {"X": (0, 0, 0), "R": (1, 0, 0), "A": (2, 0, 1), "B1": (0, 1, 0), "B2": (0, 1, 0),
                "C1": (0, 1, 0), "C2": (0, 1, 0), "M": (1, 0, 0), "F": (0, 2, 0), "W": (1, 0, 1),
                "V": (1, 0, 0), "D": (1, 0, 0), "E": (0, 2, 0), "H": (1, 0, 1), "O": (1, 0, 0), "N": (0, 0, 0),
                "XA": (0, 0, 0), "OA": (0, 0, 0), "NA": (0, 0, 0), "TA": (0, 0, 0), "GA": (0, 0, 0),
                "GB": (0, 0, 0), "GS": (0, 0, 0), "T": (1, 0, 0), "G1": (1, 0, 1), "G2": (1, 0, 0),
                ("G1", NC - 1): (2, 0, 0)}

        def gate_key_banks(at, c):
            u = at["G1", c]
            if c < NC - 1:
                return acc, acc_full, acc_drained, u.acc
            return bank, bank_full, bank_drained, u.bank + 1

        class Use:

            def __init__(self, counts):
                self.bank, self.wide, self.acc = counts

        def uses(stages, start):
            at, n = {}, list(start)
            for key in stages:
                at[key] = Use(n)
                n = [a + b for a, b in zip(n, USES.get(key, USES.get(key[0])))]
            return at, n

        _, pro_n = uses(PRO, (0, 0, 0))
        _, body_n = uses(BODY, (0, 0, 0))

        def part2_program(eng, stage):
            at, _ = uses(PRO, (0, 0, 0))
            for key in PRO:
                if key[0] in stage:
                    stage[key[0]](at, 0, key[1])
            with eng.Fori(0, B - 1) as b:
                base = [p + b * n for p, n in zip(pro_n, body_n)]
                at, _ = uses(BODY, base)
                for key in BODY:
                    if key[0] in stage:
                        stage[key[0]](at, b + 1 if key[0] in NEXT else b, key[1])
            base = [p + (B - 1) * n for p, n in zip(pro_n, body_n)]
            at, _ = uses(LAST, base)
            for key in LAST:
                if key[0] in stage:
                    stage[key[0]](at, B - 1, key[1])

        @block.sync
        def _(sp):
            for w, (dst, src) in enumerate([(wq, Wq), (wk, Wk), (wv, Wv), (wo, Wo)]):
                sp.dma_start(dst[:, :, :], src.rearrange("(k p) n -> p k n", p=P)).then_inc(weights_in, 16)
            for w, src in enumerate([W_r, W_k, W_v]):
                sp.dma_start(wnat[:, w, :, :], src.rearrange("(k p) n -> p k n", p=P)).then_inc(weights_in, 16)
            sp.dma_start(bo_all[:, :], bo.rearrange("(a n) -> a n", a=1).to_broadcast([P, A])).then_inc(weights_in, 16)
            for w, src in enumerate([mu_r, mu_k]):
                sp.dma_start(mu[:, w, :], src.rearrange("(k p) -> p k", p=P),
                             allow_slow_non_contiguous=True).then_inc(weights_in, 16)

            with sp.Fori(0, B // GR) as i:
                for s in ROWS:
                    n = i * GR + s
                    sp.wait_ge(p_pooled, i * GR + max(s + 1 - NX1, 0))
                    hold(sp)
                    sp.dma_start(x1in[s % NX1][:, :, :], x[bass.ds(n, 1)].rearrange("a (t p) n -> p (a t) n", p=P))\
                        .then_inc(p_in[s], 16)
                for s in ROWS:
                    n = i * GR + s
                    sp.wait_ge(p_dve, of(dve_steps, i, "lmlo", s))
                    hold(sp)
                    sp.dma_start(lm_dram[bass.ds(n, 1)].rearrange("a p n -> p (a n)"),
                                 lm16[s][:, :, :, :].rearrange("p a k m -> p (a k m)")).then_inc(lm_out, 16)
            sp.wait_ge(lm_out, 16 * B)
            sp.wait_ge(zt_out, 16 * B)
            sp.wait_ge(p_pe, len(pe_steps) * B // GR)
            sp.wait_ge(setup2, 8)

            def load_q(b):
                load_bd(q_bd, False, 0, b, q_bd_in)
                src = lm_dram[bass.ds(b, 1)].rearrange("a p (t w k m) -> p (a t) w k m", t=2, w=2, k=KB)
                for slot, t in enumerate((0, 1, 0)):
                    for h in range(HB):
                        q, j = h // 2, h % 2
                        r = slice(32 * slot + HS * j, 32 * slot + HS * (j + 1))
                        sp.dma_start(q_stack[r, q::PB, j * M:(j + 1) * M],
                                     src[h * HS:(h + 1) * HS, t, 0, :, :]).then_inc(q_stack_in, 16)

            def load_bd(dst, lo, key, b, done):
                n = 2 if lo else 1
                src = lm_dram[bass.ds(b, 1)].rearrange("a p (t w k m) -> p (a t) w k m", t=2, w=2, k=KB)
                for h in range(HB):
                    r = slice(h * HS, (h + 1) * HS)
                    for t in range(n):
                        sp.dma_start(dst[r, t, :, h, :], src[r, t, key, :, :]).then_inc(done, 16)

            def load_x(b, c):
                if not (isinstance(b, int) and c < 2):
                    sp.wait_ge(norm_x.applied, b * NC + c - 1)
                    hold(sp)
                src = x[bass.ds(b, 1), c * CH:(c + 1) * CH, :].rearrange("a (t p) n -> p (a t) n", p=P)
                sp.dma_start(xin[c % 2][:, :, :], src).then_inc(x_in[c % 2], 16)

            def stage_X(at, b, c):
                if c == 0:
                    if not isinstance(b, int):
                        sp.wait_ge(m3_max, b)
                        hold(sp)
                    load_bd(kA_bd, False, 1, b, kA_bd_in)
                    if isinstance(b, int):
                        load_q(b)
                if isinstance(b, int):
                    load_x(b, c)

            def stage_XA(at, b, c):
                if not isinstance(b, int) and c < 2:
                    load_x(b, c + 2)

            def stage_B1(at, b, c):
                for k in range(KB):
                    sp.wait_ge(acc_drained[k], at["A", c].acc + 1)
                hold(sp)
                for slot, src in enumerate((kh, kh, kl)):
                    for q in range(PB):
                        sp.dma_start(k_stack[32 * slot:32 * slot + 32, q::PB, c * CH:(c + 1) * CH],
                                     src[32 * q:32 * q + 32, :, :]).then_inc(k_stack_in, 16)

            def stage_F(at, b, c):
                if c:
                    return
                if not isinstance(b, int):
                    sp.wait_ge(k_bd_free, b)
                    sp.wait_ge(zt_free, b)
                    hold(sp)
                load_bd(kE_bd, True, 1, b, kE_bd_in)
                sp.dma_start(zt[:, :, :].rearrange("p a m -> p (a m)"),
                             zt_dram[bass.ds(b, 1)].rearrange("a p n -> p (a n)")).then_inc(zt_in, 16)

            def stage_W(at, b, c):
                if not isinstance(b, int):
                    load_x(b + 1, 0)
                    load_x(b + 1, 1)
                    sp.wait_ge(q_bd_free, b + 1)
                    hold(sp)
                    load_q(b + 1)

            def stage_E(at, b, c):
                sp.wait_ge(xm_made, b * NC + c)
                hold(sp)
                src = x[bass.ds(b, 1), c * CH:(c + 1) * CH, :].rearrange("a (t p) n -> p (a t) n", p=P)
                sp.dma_start(xres[:, :, :], src).then_inc(res_in[c % 2], 16)

            def stage_GA(at, b, c):
                sp.wait_ge(fin_made, b * NC + c + 1)
                hold(sp)
                dst = out[bass.ds(b, 1), c * CH:(c + 1) * CH, :].rearrange("a (t p) n -> p (a t) n", p=P)
                sp.dma_start(dst, ob[c % 2][:, :, :]).then_inc(fin_out[c % 2], 16)

            part2_program(sp, {"X": stage_X, "B1": stage_B1, "XA": stage_XA, "F": stage_F, "W": stage_W,
                               "E": stage_E, "GA": stage_GA})
            for i in range(2):
                sp.wait_ge(fin_out[i], 16 * B * NC // 2)

        @block.gpsimd
        def _(pool):
            g = nc.gpsimd
            g.memset(ident[:, :], 0.0).then_inc(const_made, 1)
            g.memset(pool_w[:, :], 1.0 / DEN).then_inc(const_made, 1)
            g.memset(head_mask[:, :], 1.0).then_inc(const_made, 1)
            g.memset(ones_pair[:, :], 1.0).then_inc(const_made, 1)
            g.memset(ones32[:, :], 1.0).then_inc(const_made, 1)
            g.memset(neg_sel[:, :, :], 0.0).then_inc(const_made, 1)
            pool.wait_ge(const_made, 6)
            g.affine_select(out=ident[:, :], in_=ident[:, :], compare_op=ALU.not_equal, fill=1.0, base=0,
                            pattern=[[-1, P]], channel_multiplier=1).then_inc(const_made, 1)
            o = M - TM
            g.affine_select(out=pool_w[:, :], in_=pool_w[:, :], compare_op=ALU.is_ge, fill=0.0, base=DEN * o,
                            pattern=[[-DEN, 2 * M - TM]], channel_multiplier=1).then_inc(const_made, 1)
            pool.wait_ge(const_made, 8)
            g.affine_select(out=pool_w[:, :], in_=pool_w[:, :], compare_op=ALU.is_ge, fill=0.0,
                            base=DEN - 1 - DEN * o, pattern=[[DEN, 2 * M - TM]],
                            channel_multiplier=-1).then_inc(const_made, 1)
            g.affine_select(out=head_mask[:, :], in_=head_mask[:, :], compare_op=ALU.is_ge, fill=0.0, base=0,
                            pattern=[[-HS, HB]], channel_multiplier=1).then_inc(const_made, 1)
            pool.wait_ge(const_made, 10)
            g.affine_select(out=head_mask[:, :], in_=head_mask[:, :], compare_op=ALU.is_ge, fill=0.0,
                            base=HS - 1, pattern=[[HS, HB]], channel_multiplier=-1).then_inc(const_made, 1)
            op = ones_pair[:, :].rearrange("p (h d) -> p h d", h=2)
            g.affine_select(out=op, in_=op, compare_op=ALU.is_ge, fill=0.0, base=0,
                            pattern=[[-M, 2], [0, HS]], channel_multiplier=1).then_inc(const_made, 1)
            pool.wait_ge(const_made, 12)
            g.affine_select(out=op, in_=op, compare_op=ALU.is_ge, fill=0.0, base=M - 1,
                            pattern=[[M, 2], [0, HS]], channel_multiplier=-1).then_inc(const_made, 1)
            ns = neg_sel[:, :, :].rearrange("k p (j m) -> k p j m", j=2)
            g.affine_select(out=ns, in_=ns, compare_op=ALU.not_equal, fill=-1.0, base=0,
                            pattern=[[-2, PAIRS], [-1, 2], [0, M]], channel_multiplier=1).then_inc(const_made, 1)
            pool.wait_ge(const_made, 7)
            g.tensor_tensor(eye[:, :], ident[:, 0:M], ident[:, M:P], ALU.add).then_inc(const_made, 1)

            for s in ROWS:
                for t in (XT_bd, ST_bd, ZT_bd):
                    g.memset(t[s][:, :, :, :], 0.0).then_inc(p_zero, 1)

            pool.wait_ge(p_pe, len(pe_steps) * B // GR)
            pool.wait_ge(p_dve, len(dve_steps) * B // GR)
            pool.wait_ge(lm_out, 16 * B)
            pool.wait_ge(zt_out, 16 * B)
            g.memset(q_bd[:, :, :, :, :], 0.0).then_inc(setup2, 1)
            g.memset(kA_bd[:, :, :, :, :], 0.0).then_inc(setup2, 1)
            g.memset(kE_bd[:, :, :, :, :], 0.0).then_inc(setup2, 1)
            g.memset(wbd[:, :, :, :], 0.0).then_inc(setup2, 1)
            g.memset(q_stack[:, :, :], 0.0).then_inc(setup2, 1)
            pool.wait_ge(setup2, 5)
            g.memset(k_stack[3 * 32:P, :, :], 0.0).then_inc(setup2, 1)
            pool.wait_ge(setup2, 6)
            g.memset(k_stack[3 * 32:3 * 32 + 1, :, :], 1.0).then_inc(setup2, 1)
            pool.wait_ge(setup2, 7)
            g.memset(m1T[:, :], 0.0).then_inc(setup2, 1)

            def stage_OA(at, b, c):
                n = b * NC + c
                pool.wait_ge(res_in[c % 2], 16 * (b * 2 + c // 2 + 1))
                pool.wait_ge(norm_y.applied, n + 1)
                pool.wait_ge(fin_made, b * NC + max(c - 2, 0))
                g.tensor_tensor(xm[c % 3][:, :, :], yy[:, :, :], xres[:, :, :],
                                ALU.add).then_inc(xm_made, 1)

            def stage_T(at, b, c):
                u, n = at["T", c].bank, b * NC + c
                pool.wait_ge(xk_made, n)
                pool.wait_ge(carry, n + 1)
                for k in range(KB):
                    pool.wait_ge(bank_drained[k], u + 1)
                g.tensor_tensor(xkT[:, :, :], x2T[:, :, 1:CH + 1], x2T[:, :, 0:CH],
                                ALU.subtract).then_inc(dx_made, 1)

            def stage_GA(at, b, c):
                pool.wait_ge(norm_f.applied, b * NC + c + 1)
                g.tensor_tensor(ob[c % 2][:, :, :], ob[c % 2][:, :, :], xm[c % 3][:, :, :],
                                ALU.add).then_inc(fin_made, 1)

            part2_program(pool, {"OA": stage_OA, "T": stage_T, "GA": stage_GA})

        @block.scalar
        def _(act):
            sc = nc.scalar
            nc.scalar.preload_act_table_set("natural_log_exp_and_others")
            for w, dst in enumerate([wrT, wkT, wvT]):
                act.wait_ge(wT_full, w + 1)
                sc.activation(dst[:, :, :], wide[w % 2][:, 0:KB * A].rearrange("p (k n) -> p k n", k=KB),
                              ACT.Copy).then_inc(wT_drained, 1)
            act.wait_ge(weights_in, 16 * NW)
            for w, src in enumerate((wq, wk, wv)):
                sc.activation(w16[:, w, 0, :, :], src[:, :, :], ACT.Copy, scale=WS).then_inc(w16_hi, 1)
            with act.Fori(0, B // GR) as i:
                for s in ROWS:
                    act.wait_ge(p_dve, of(dve_steps, i, "mv", s))
                    sc.activation(ln1[s][:, :], mv1[s][:, :, 1], ACT.Ln, bias=EPS).then_inc(p_act, 1)
                    act.wait_ge(p_act, of(act_steps, i, "ln", s))
                    sc.activation(rstd1[s][:, :], ln1[s][:, :], ACT.Exp, scale=-0.5).then_inc(p_act, 1)
                for s in ROWS:
                    act.wait_ge(p_pe, of(pe_steps, i, "lT", s))
                    sc.activation(xlT[s][:, :, :], pb[s][1][:, 0:KB * M].rearrange("p (k m) -> p k m", k=KB),
                                  ACT.Copy).then_inc(p_act, 1)
                for s in ROWS:
                    act.wait_ge(p_pe, of(pe_steps, i, "qk", s))
                    qk = pb[s][0][:, 0:2 * KB * M].rearrange("p (a k m) -> p a k m", a=2, k=KB)
                    sc.activation(qlT[s][:, 0, :, :], qk[:, 0, :, :], ACT.Copy, scale=QSCALE).then_inc(p_act, 1)
                    sc.activation(qlT[s][:, 1, :, :], qk[:, 1, :, :], ACT.Copy).then_inc(p_act, 1)
                    act.wait_ge(p_act, of(act_steps, i, "kl", s))
                    act.wait_ge(lm_out, 16 * GR * i)
                    sc.activation(lm16[s][:, 0:2, :, :], qlT[s][:, :, :, :], ACT.Copy).then_inc(p_act, 1)
                for s in ROWS:
                    act.wait_ge(p_dve, of(dve_steps, i, "shift", s))
                    sc.activation(X[s][:, :, :], X[s][:, :, :], ACT.Exp).then_inc(p_act, 1)
                for s in ROWS:
                    act.wait_ge(p_pe, of(pe_steps, i, "XT", s))
                    sc.activation(XT[s][:, :, :], pm(pb[s][0]), ACT.Copy).then_inc(p_act, 1)
                    act.wait_ge(p_act, of(act_steps, i, "XT", s))
                    sc.activation(ST_d[s][:, :, 0, :], XT[s][:, :, :], ACT.Copy, scale=XS).then_inc(p_act, 1)
                for s in ROWS:
                    act.wait_ge(p_dve, of(dve_steps, i, "gXT", s))
                    sc.activation(Z_d[s][:, :, 0, :], XT[s][:, :, :], ACT.Copy, scale=ZS).then_inc(p_act, 1)
                    sc.activation(ZT_d[s][:, :, 0, :], X[s][:, :, :], ACT.Copy, scale=ZS).then_inc(p_act, 1)

                def high(name, it, s, dst, src, scale):
                    act.wait_ge(p_pe, of(pe_steps, i, name, it, s))
                    sc.activation(dst[s][:, :, 0, :], pm(src), ACT.Copy, scale=scale).then_inc(p_act, 1)

                for it in range(ITERS):
                    for s in ROWS:
                        high("S", it, s, ST_d, pb[s][0], SS / (XS * ZS))
                    if it < ITERS - 1:
                        for s in ROWS:
                            if it == 0:
                                act.wait_ge(p_dve, of(dve_steps, i, "ZTlo", s))
                            else:
                                act.wait_ge(p_dve, of(dve_steps, i, "ZTlo", it - 1, s))
                            act.wait_ge(p_zero, 3 * GR)
                            for j in range(2):
                                r = slice(j * HALF, (j + 1) * HALF)
                                ins = sc.activation(ZT_bd[s][r, :, :, j * M:(j + 1) * M], ZT_d[s][r, :, :, :], ACT.Copy)
                            ins.then_inc(p_act, 1)
                    for s in ROWS:
                        high("T2", it, s, ST_d, pb[s][1], -1.0 / SS)
                    for s in ROWS:
                        high("T3", it, s, ST_d, pb[s][0], 1.0 / SS)
                    if it < ITERS - 1:
                        for s in ROWS:
                            high("Z", it, s, Z_d, pb[s][1], 0.25 / SS)
                            high("ZT", it, s, ZT_d, pb[s][0], 0.25 / SS)
                for s in ROWS:
                    n = i * GR + s
                    act.wait_ge(p_dve, of(dve_steps, i, "ZTlo", ITERS - 1, s))
                    hold(act)
                    act.dma_start(zt_dram[bass.ds(n, 1)].rearrange("a p n -> p (a n)"),
                                  X[s][:, :, :].rearrange("p a m -> p (a m)")).then_inc(zt_out, 16)

            act.wait_ge(p_pe, len(pe_steps) * B // GR)
            act.wait_ge(p_dve, len(dve_steps) * B // GR)
            act.wait_ge(lm_out, 16 * B)
            act.wait_ge(zt_out, 16 * B)

            def stage_X(at, b, c):
                if not (isinstance(b, int) and c < 2):
                    act.wait_ge(norm_x.applied, b * NC + c - 1)
                norm_x.root(act, b * NC + c, c)

            def stage_R(at, b, c):
                u = at["R", c].bank
                for k in range(KB):
                    act.wait_ge(bank_full[k], u + 1)
                    sc.activation(xT[:, 0, k, :], bank[k][:, :], ACT.Copy).then_inc(x_hi, 1)

            def stage_A(at, b, c):
                u, a = at["A", c].bank, at["A", c].acc
                span = slice(c * CH, (c + 1) * CH)
                for k in range(KB):
                    act.wait_ge(bank_full[k], u + 1)
                    sc.activation(qh[:, k, span], bank[k][:, :], ACT.Copy, scale=QSCALE / WS).then_inc(q_hi, 1)
                act.wait_ge(k_stack_in, 16 * NKS * (b * NC + c))
                for k in range(KB):
                    act.wait_ge(acc_full[k], a + 1)
                    sc.activation(kh[:, k, :], acc[k][:, :], ACT.Copy, scale=1.0 / WS).then_inc(k_hi, 1)
                for j in range(2):
                    act.wait_ge(bank_full[j], u + 2)
                    sc.activation(vv[:, c * NT + 2 * j:c * NT + 2 * j + 2, :],
                                  bank[j][:, :].rearrange("p (t n) -> p t n", t=2), ACT.Copy, scale=1.0 / WS)\
                        .then_inc(bank_drained[j], 1)

            def stage_F(at, b, c):
                u = at["F", 0].wide
                for t in range(c * NT, (c + 1) * NT):
                    act.wait_ge(wide_full[t % 2], u + t // 2 + 1)
                    if t >= 2:
                        act.wait_ge(e3_read, b * (NC * NT - 1) + t - 1)
                    sc.activation(e3[t % 2][:, :], wide[t % 2][:, :], ACT.Exp).then_inc(wide_drained[t % 2], 1)

            def stage_W(at, b, c):
                a = at["W", 0].acc
                act.wait_ge(acc_full[0], a + 1)
                sc.activation(uT[:, :], acc[0][:, 0:KB * P], ACT.Copy).then_inc(acc_drained[0], 1)
                act.wait_ge(acc_full[1], a + 1)
                sc.activation(rs3[:, :], acc[1][:, 0:256], ACT.Copy).then_inc(acc_drained[1], 1)
            def stage_V(at, b, c):
                u = at["V", 0].bank
                for j in range(2):
                    r = slice(j * HALF, (j + 1) * HALF)
                    act.wait_ge(bank_full[j], u + 1)
                    act.wait_ge(setup2, 8)
                    sc.activation(wbd[r, :, j, :], bank[j][r, 0:PAIRS * HS].rearrange("p (a d) -> p a d", a=PAIRS),
                                  ACT.Copy).then_inc(bank_drained[j], 1)

            def stage_D(at, b, c):
                u = at["D", c]
                for j in range(2):
                    act.wait_ge(bank_full[j], u.bank + 1)
                    sc.activation(m1T[0:H, j * 256:(j + 1) * 256], bank[j][0:H, 0:256],
                                  ACT.Copy).then_inc(bank_drained[j], 1)

            def stage_E(at, b, c):
                u = at["E", c]
                for j in range(PAIRS // 2):
                    act.wait_ge(wide_full[j % 2], u.wide + j // 2 + 1)
                    sc.activation(p1[:, 2 * j:2 * j + 2, :], wide[j % 2][:, :].rearrange("p (a n) -> p a n", a=2),
                                  ACT.Exp).then_inc(wide_drained[j % 2], 1)

            def stage_H(at, b, c):
                u, n = at["H", c].bank, b * NC + c
                for k in range(KB):
                    act.wait_ge(bank_full[k], u + 1)
                    act.wait_ge(acc_drained[k], at["H", c].acc)
                    sc.activation(oT[:, k, :], bank[k][:, :], ACT.Ln).then_inc(bank_drained[k], 1)
                    act.wait_ge(bank_drained[k], u + 1)
                    sc.activation(oT[:, k, :], oT[:, k, :], ACT.Exp, scale=-1.0).then_inc(rc_made, 1)

            def stage_OA(at, b, c):
                norm_y.root(act, b * NC + c, c)

            def stage_NA(at, b, c):
                norm_m.root(act, b * NC + c, c)

            def stage_T(at, b, c):
                u, n = at["T", c].bank, b * NC + c
                act.wait_ge(carry, n + 1)
                for k in range(KB):
                    act.wait_ge(bank_full[k], u + 1)
                    sc.activation(x2T[:, k, 1:CH + 1], bank[k][:, :], ACT.Copy).then_inc(bank_drained[k], 1)

            def stage_G1(at, b, c):
                u, n = at["G1", c].bank, b * NC + c
                act.wait_ge(norm_f.stats_made, n)
                for j in range(2):
                    act.wait_ge(bank_full[j], u + 1)
                    sc.activation(sg[:, 2 * j:2 * j + 2, :], bank[j][:, :].rearrange("p (t n) -> p t n", t=2),
                                  ACT.Exp, scale=-1.0).then_inc(bank_drained[j], 1)
                src, full, drained, a = gate_key_banks(at, c)
                for k in range(KB):
                    act.wait_ge(full[k], a + 1)
                    sc.activation(ka[:, k, :], src[k][:, :], ACT.Relu).then_inc(drained[k], 1)

            def stage_GB(at, b, c):
                u, n = at["G1", c].bank, b * NC + c
                _, _, drained, a = gate_key_banks(at, c)
                for k in range(KB):
                    act.wait_ge(drained[k], a + 1)
                sc.activation(ka[:, :, :], ka[:, :, :], ACT.Square).then_inc(ka_made, 1)
                for j in range(2):
                    act.wait_ge(bank_drained[j], u + 1)
                sc.activation(sg[:, :, :], sg[:, :, :], ACT.Ln, bias=1.0).then_inc(sg_ln, 1)
                act.wait_ge(sg_ln, n + 1)
                sc.activation(sg[:, :, :], sg[:, :, :], ACT.Exp, scale=-1.0).then_inc(sg_made, 1)

            def stage_GA(at, b, c):
                n = b * NC + c
                act.wait_ge(norm_f.applied, n)
                norm_f.root(act, n, c)

            part2_program(act, {"X": stage_X, "GB": stage_GB, "R": stage_R, "A": stage_A, "V": stage_V,
                                "D": stage_D, "F": stage_F, "W": stage_W, "E": stage_E, "H": stage_H,
                                "OA": stage_OA, "NA": stage_NA, "T": stage_T, "G1": stage_G1, "GA": stage_GA})

        @block.vector
        def _(dve):
            v = nc.vector
            dve.wait_ge(const_made, NCONST)
            v.tensor_copy(ident16[:, :], ident[:, :]).then_inc(eyes_made, 1)
            for dst, scale in ((eye7, -7.0 * SS), (eye15, 15.0 * SS * SS), (eye13, 13.0 * SS * SS)):
                v.tensor_scalar(dst[:, :], eye[:, :], scale, None, ALU.mult).then_inc(eyes_made, 1)
            dve.wait_ge(eyes_made, 4)
            full = [P, PAIRS, M]

            for w, src in enumerate((wq, wk, wv)):
                dve.wait_ge(w16_hi, w + 1)
                v.scalar_tensor_tensor(out=w16[:, w, 1, :, :], in0=src[:, :, :], scalar=WS, in1=w16[:, w, 0, :, :],
                                       op0=ALU.mult, op1=ALU.subtract).then_inc(w16_lo, 1)
            for i in range(2):
                v.memset(pw[i][:, :], 0.0).then_inc(eyes_made, 1)
            dve.wait_ge(eyes_made, 4 + 2)
            with dve.Fori(0, B // GR) as i:
                def done(*k):
                    dve.wait_ge(p_dve, of(dve_steps, i, *k))

                for name, s in STATS:
                    if name == "pw":
                        dve.wait_ge(p_act, of(act_steps, i, "rstd", s))
                        if s >= 2:
                            dve.wait_ge(p_pooled, i * GR + s - 1)
                        v.tensor_tensor(pw[s % 2][:, :].rearrange("p (t c) -> p t c", t=NTL)[:, :, 0:TM],
                                        pool_w[:, M - TM:M].unsqueeze(1).to_broadcast([P, NTL, TM]),
                                        rstd1[s][:, :].unsqueeze(2).to_broadcast([P, NTL, TM]),
                                        ALU.mult).then_inc(p_dve, 1)
                        continue
                    dve.wait_ge(p_in[s], 16 * (i + 1))
                    for t in range(NTL):
                        ins = v.bn_stats(st1[s][:, t, :], x1in[s % NX1][:, t, :])
                    ins.then_inc(p_dve, 1)
                    done("st", s)
                    hold(dve)
                    for t in range(NTL):
                        ins = v.bn_aggr(mv1[s][:, t, :], st1[s][:, t, :])
                    ins.then_inc(p_dve, 1)
                for s in ROWS:
                    dve.wait_ge(p_pooled, i * GR + s + 1)
                    v.bn_stats(stl[s][:, :], pb[s][0][0:M, 0:A]).then_inc(p_dve, 1)
                    done("stl", s)
                    hold(dve)
                    v.bn_aggr(mvl[s][:, :], stl[s][:, :]).then_inc(p_dve, 1)
                    done("mvl", s)
                    v.tensor_scalar(xl[s][:, :], pb[s][0][0:M, 0:A], mvl[s][:, 0:1], None,
                                    ALU.subtract).then_inc(p_dve, 1)
                for s in ROWS:
                    dve.wait_ge(p_act, of(act_steps, i, "lm", s))
                    v.tensor_tensor(lm16[s][:, 2:4, :, :], qlT[s][:, :, :, :], lm16[s][:, 0:2, :, :],
                                    ALU.subtract).then_inc(p_dve, 1)
                    if s >= 2:
                        dve.wait_ge(p_pe, of(pe_steps, i, "logits", s - 2))
                    for k in range(KB):
                        ins = v.tensor_tensor(qbd[s % 2][:, k, :, :],
                                              qlT[s][:, 0, k, :].unsqueeze(1).to_broadcast([P, HB, M]),
                                              head_mask[:, :].unsqueeze(2).to_broadcast([P, HB, M]), ALU.mult)
                    ins.then_inc(p_dve, 1)
                for s in ROWS:
                    dve.wait_ge(p_pe, of(pe_steps, i, "logits", s))
                    dve.wait_ge(zt_out, 16 * GR * i)
                    v.tensor_reduce(mx[s][:, :], pm(pb[s][1]), AX.X, ALU.max).then_inc(p_dve, 1)
                    done("max", s)
                    v.tensor_tensor(X[s][:, :, :], pm(pb[s][1]), mx[s][:, :].unsqueeze(2).to_broadcast(full),
                                    ALU.subtract).then_inc(p_dve, 1)
                for s in ROWS:
                    dve.wait_ge(p_act, of(act_steps, i, "exp", s))
                    v.tensor_reduce(rsum1[s][:, :], X[s][:, :, :], AX.X, ALU.add).then_inc(p_dve, 1)
                    done("sum", s)
                    v.reciprocal(rcp1[s][:, :], rsum1[s][:, :]).then_inc(p_dve, 1)
                    done("rcp", s)
                    v.tensor_tensor(X[s][:, :, :], X[s][:, :, :], rcp1[s][:, :].unsqueeze(2).to_broadcast(full),
                                    ALU.mult).then_inc(p_dve, 1)
                    done("X", s)
                    v.tensor_reduce(rc1[s][:, 0, :], X[s][:, :, :], AX.X, ALU.add).then_inc(p_dve, 1)

                def low(hi_key, dst, src, scale):
                    dve.wait_ge(p_act, of(act_steps, i, *hi_key))
                    v.scalar_tensor_tensor(out=dst[:, :, 1, :], in0=src, scalar=scale, in1=dst[:, :, 0, :],
                                           op0=ALU.mult, op1=ALU.subtract).then_inc(p_dve, 1)

                def blocks(lo_key, dst, src):
                    dve.wait_ge(p_zero, 3 * GR)
                    done(*lo_key)
                    for j in range(2):
                        r = slice(j * HALF, (j + 1) * HALF)
                        ins = v.tensor_copy(dst[r, :, :, j * M:(j + 1) * M], src[r, :, :, :])
                    ins.then_inc(p_dve, 1)

                for s in ROWS:
                    dve.wait_ge(p_act, of(act_steps, i, "XT", s))
                    v.tensor_reduce(rc1[s][:, 1, :], XT[s][:, :, :], AX.X, ALU.add).then_inc(p_dve, 1)
                    low(("XThi", s), ST_d[s], XT[s][:, :, :], XS)
                    blocks(("XTlo", s), XT_bd[s], ST_d[s])
                for s in ROWS:
                    dve.wait_ge(p_pe, of(pe_steps, i, "sums", s))
                    v.tensor_reduce(cm[s][:, :, :], pb[s][1][0:PAIRS, 0:2 * P]
                                    .rearrange("p (a h m) -> p a h m", a=2, h=2), AX.X, ALU.max).then_inc(p_dve, 1)
                    done("cm", s)
                    v.tensor_tensor(cg[s][:, 0, :], cm[s][:, 0, :], cm[s][:, 1, :], ALU.mult).then_inc(p_dve, 1)
                    done("cg", s)
                    v.reciprocal(cg[s][:, 1, :], cg[s][:, 0, :]).then_inc(p_dve, 1)
                    done("cr", s)
                    v.tensor_copy(gb[s][:, :, :], cg[s][:, 1, :].unsqueeze(2).to_broadcast([PAIRS, 2, M]))\
                        .then_inc(p_dve, 1)
                for s in ROWS:
                    dve.wait_ge(p_pe, of(pe_steps, i, "g", s))
                    v.tensor_copy(gcol[s][:, :], pb[s][1][:, 0:PAIRS]).then_inc(p_dve, 1)
                    done("gcol", s)
                    gc = gcol[s][:, :].unsqueeze(2).to_broadcast(full)
                    v.tensor_tensor(X[s][:, :, :], X[s][:, :, :], gc, ALU.mult).then_inc(p_dve, 1)
                    v.tensor_tensor(XT[s][:, :, :], XT[s][:, :, :], gc, ALU.mult).then_inc(p_dve, 1)
                for s in ROWS:
                    low(("Zhi", s), Z_d[s], XT[s][:, :, :], ZS)
                    low(("ZThi", s), ZT_d[s], X[s][:, :, :], ZS)

                for it in range(ITERS):
                    for s in ROWS:
                        low(("S", it, s), ST_d[s], pm(pb[s][0]), SS / (XS * ZS))
                        blocks(("Slo", it, s), ST_bd[s], ST_d[s])
                    for s in ROWS:
                        low(("T2", it, s), ST_d[s], pm(pb[s][1]), -1.0 / SS)
                    for s in ROWS:
                        low(("T3", it, s), ST_d[s], pm(pb[s][0]), 1.0 / SS)
                        blocks(("T3lo", it, s), ST_bd[s], ST_d[s])
                    for s in ROWS:
                        if it < ITERS - 1:
                            low(("Z", it, s), Z_d[s], pm(pb[s][1]), 0.25 / SS)
                            low(("ZT", it, s), ZT_d[s], pm(pb[s][0]), 0.25 / SS)
                        else:
                            dve.wait_ge(p_pe, of(pe_steps, i, "ZT", it, s))
                            v.tensor_scalar(X[s][:, :, :], pm(pb[s][0]), 0.25 / (SS * ZS), None,
                                            ALU.mult).then_inc(p_dve, 1)

            dve.wait_ge(p_act, len(act_steps) * B // GR)
            dve.wait_ge(p_pe, len(pe_steps) * B // GR)
            dve.wait_ge(lm_out, 16 * B)
            dve.wait_ge(zt_out, 16 * B)

            def stage_X(at, b, c):
                dve.wait_ge(x_in[c % 2], 16 * (b * 2 + c // 2 + 1))
                norm_x.stats(dve, xin[c % 2], b * NC + c, c)

            def stage_XA(at, b, c):
                if not (isinstance(b, int) and c < 2):
                    dve.wait_ge(xhat_read, b * NC + c - 1)
                norm_x.apply(dve, xhat[c % 2], xin[c % 2], b * NC + c, c)

            def stage_R(at, b, c):
                for k in range(KB):
                    dve.wait_ge(x_hi, (b * NC + c) * KB + k + 1)
                    v.tensor_tensor(xT[:, 1, k, :], bank[k][:, :], xT[:, 0, k, :],
                                    ALU.subtract).then_inc(bank_drained[k], 1)

            def stage_A(at, b, c):
                u, n = at["A", c], b * NC + c
                span = slice(c * CH, (c + 1) * CH)
                for k in range(KB):
                    dve.wait_ge(q_hi, n * KB + k + 1)
                    v.scalar_tensor_tensor(out=ql[:, k, span], in0=bank[k][:, :], scalar=QSCALE / WS, in1=qh[:, k, span],
                                           op0=ALU.mult, op1=ALU.subtract).then_inc(bank_drained[k], 1)
                for k in range(KB):
                    dve.wait_ge(k_hi, n * KB + k + 1)
                    v.scalar_tensor_tensor(out=kl[:, k, :], in0=acc[k][:, :], scalar=1.0 / WS, in1=kh[:, k, :],
                                           op0=ALU.mult, op1=ALU.subtract).then_inc(acc_drained[k], 1)

            def row_maxima(at, b, c, half):
                u = at[f"B{half + 1}", c]
                for j in (2 * half, 2 * half + 1):
                    dve.wait_ge(wide_full[j % 2], u.wide + 1)
                    v.tensor_reduce(m3[:, 2 * j:2 * j + 2, c], wide[j % 2][:, :].rearrange("p (a n) -> p a n", a=2),
                                    AX.X, ALU.max).then_inc(wide_drained[j % 2], 1)

            def token_maxima(at, b, c, half):
                u = at[f"C{half + 1}", c]
                for t in (2 * half, 2 * half + 1):
                    dve.wait_ge(wide_full[t % 2], u.wide + 1)
                    v.tensor_reduce(m1[:, c * NT + t, :], wide[t % 2][:, :].rearrange("p (h m) -> p h m", h=H),
                                    AX.X, ALU.max).then_inc(wide_drained[t % 2], 1)

            def stage_M(at, b, c):
                u = at["M", 0]
                dve.wait_ge(wide_drained[1], u.wide)
                v.tensor_reduce(m3m[:, :], m3[:, :, :], AX.X, ALU.max).then_inc(m3_max, 1)
                dve.wait_ge(setup2, 8)
                for k in range(KB):
                    dve.wait_ge(bank_full[k], u.bank + 1)
                    v.tensor_scalar(q_stack[3 * 32:P, k * PB:(k + 1) * PB, :],
                                    bank[k][3 * 32:P, :].rearrange("p (a n) -> p a n", a=PB), -1.0, None,
                                    ALU.mult).then_inc(bank_drained[k], 1)

            def stage_W(at, b, c):
                u = at["W", 0].bank
                dve.wait_ge(bank_full[1], u + 1)
                v.reciprocal(rr3[:, :], bank[1][:, 0:PAIRS]).then_inc(bank_drained[1], 1)
                dve.wait_ge(bank_full[0], u + 1)
                dve.wait_ge(bank_drained[1], u + 1)
                for j in range(2):
                    r = slice(j * HALF, (j + 1) * HALF)
                    ins = v.tensor_tensor(un[r, :, :],
                                          bank[0][r, 0:KB * P].rearrange("p (a h d) -> p a h d", h=2, d=HS)[:, :, j, :],
                                          rr3[r, :].unsqueeze(2).to_broadcast([HALF, PAIRS, HS]), ALU.mult)
                ins.then_inc(bank_drained[0], 1)

            def stage_H(at, b, c):
                a, n = at["H", c].acc, b * NC + c
                for k in range(KB):
                    dve.wait_ge(acc_full[k], a + 1)
                    dve.wait_ge(rc_made, n * KB + k + 1)
                    v.tensor_tensor(oT[:, k, :], acc[k][:, :], oT[:, k, :], ALU.mult).then_inc(acc_drained[k], 1)

            def stage_O(at, b, c):
                u, n = at["O", c].bank, b * NC + c
                dve.wait_ge(xm_made, n)
                for j in range(2):
                    dve.wait_ge(bank_full[j], u + 1)
                    v.tensor_tensor(yy[:, 2 * j:2 * j + 2, :], bank[j][:, :].rearrange("p (t n) -> p t n", t=2),
                                    bo_all[:, :].unsqueeze(1).to_broadcast([P, 2, A]),
                                    ALU.add).then_inc(bank_drained[j], 1)
                for j in range(2):
                    dve.wait_ge(bank_drained[j], u + 1)
                norm_y.stats(dve, yy, n, c)

            def stage_OA(at, b, c):
                norm_y.apply(dve, yy, yy, b * NC + c, c)

            def stage_N(at, b, c):
                n = b * NC + c
                dve.wait_ge(xm_made, n + 1)
                norm_m.stats(dve, xm[c % 3], n, c)

            def stage_NA(at, b, c):
                dve.wait_ge(x2h_read, b * NC + c)
                norm_m.apply(dve, x2h, xm[c % 3], b * NC + c, c)

            def stage_TA(at, b, c):
                n = b * NC + c
                dve.wait_ge(dx_made, n + 1)
                for w, dst, made in ((0, xrT, xr_made), (1, xkT, xk_made)):
                    for k in range(KB):
                        ins = v.scalar_tensor_tensor(out=dst[:, k, :], in0=xkT[:, k, :], scalar=mu[:, w, k:k + 1],
                                                     in1=x2T[:, k, 0:CH], op0=ALU.mult, op1=ALU.add)
                    ins.then_inc(made, 1)
                dve.wait_ge(xk_made, n + 1)
                if c < NC - 1:
                    v.tensor_copy(x2T[:, :, 0:1], x2T[:, :, CH:CH + 1]).then_inc(carry, 1)
                else:
                    v.memset(x2T[:, :, 0:1], 0.0).then_inc(carry, 1)

            def stage_G2(at, b, c):
                u, n = at["G2", c].bank, b * NC + c
                dve.wait_ge(sg_made, n + 1)
                dve.wait_ge(fin_out[c % 2], 16 * (b * 2 + c // 2))
                for j in range(2):
                    dve.wait_ge(bank_full[j], u + 1)
                    v.tensor_tensor(ob[c % 2][:, 2 * j:2 * j + 2, :], bank[j][:, :].rearrange("p (t n) -> p t n", t=2),
                                    sg[:, 2 * j:2 * j + 2, :], ALU.mult).then_inc(bank_drained[j], 1)

            def stage_GS(at, b, c):
                for j in range(2):
                    dve.wait_ge(bank_drained[j], at["G2", c].bank + 1)
                norm_f.stats(dve, ob[c % 2], b * NC + c, c)

            def stage_GA(at, b, c):
                norm_f.apply(dve, ob[c % 2], ob[c % 2], b * NC + c, c)

            v.memset(x2T[:, :, 0:1], 0.0).then_inc(carry, 1)
            part2_program(dve, {"X": stage_X, "R": stage_R, "TA": stage_TA, "XA": stage_XA, "OA": stage_OA,
                                "NA": stage_NA, "GA": stage_GA, "A": stage_A,
                                "B1": lambda at, b, c: row_maxima(at, b, c, 0),
                                "B2": lambda at, b, c: row_maxima(at, b, c, 1),
                                "C1": lambda at, b, c: token_maxima(at, b, c, 0),
                                "C2": lambda at, b, c: token_maxima(at, b, c, 1), "M": stage_M, "W": stage_W,
                                "H": stage_H, "O": stage_O, "N": stage_N, "G2": stage_G2,
                                "GS": stage_GS})

        @block.tensor
        def _(pe):
            mm = nc.tensor.matmul
            tr = nc.tensor.transpose
            pe.wait_ge(const_made, NCONST)
            pe.wait_ge(weights_in, 16 * NW)
            for w in range(3):
                if w >= 2:
                    pe.wait_ge(wT_drained, w - 1)
                for k in range(KB):
                    for o in range(KB):
                        ins = tr(wide[w % 2][:, k * A + o * P:k * A + (o + 1) * P],
                                 wnat[:, w, o, k * P:(k + 1) * P], ident[:, :])
                ins.then_inc(wT_full, 1)
            pe.wait_ge(wT_drained, 3)

            def heads(dst, left, right, sem_value=None):
                for a in range(PAIRS):
                    for j in range(2):
                        r = slice(j * HALF, (j + 1) * HALF)
                        ins = mm(dst[r, a * M:(a + 1) * M], left[r, a, :], right(r, a), start=True, stop=True)
                return ins

            pe.wait_ge(eyes_made, 4)

            def product(dst, left, right, added=()):
                for a in range(PAIRS):
                    terms = [(scaled(a), identity) for scaled, identity in added]
                    terms += [(left[:, a, 0, :], right[:, a, 0, :]), (left[:, a, 0, :], right[:, a, 1, :]),
                              (left[:, a, 1, :], right[:, a, 0, :])]
                    for n, (l, r) in enumerate(terms):
                        ins = mm(dst[:, a * M:(a + 1) * M], l, r, start=(n == 0), stop=(n == len(terms) - 1))
                return ins

            with pe.Fori(0, B // GR) as i:
                for s in ROWS:
                    pe.wait_ge(p_dve, of(dve_steps, i, "pw", s))
                    for t in range(NTL):
                        ins = mm(pb[s][0][0:M, 0:A], pw[s % 2][:, t * M:(t + 1) * M], x1in[s % NX1][:, t, :],
                                 start=(t == 0), stop=(t == NTL - 1))
                    ins.then_inc(p_pooled, 1)
                for s in ROWS:
                    pe.wait_ge(p_dve, of(dve_steps, i, "xl", s))
                    hold(pe)
                    for k in range(KB):
                        ins = tr(pb[s][1][:, k * M:(k + 1) * M], xl[s][:, k * P:(k + 1) * P], ident[0:M, 0:M])
                    ins.then_inc(p_pe, 1)
                for s in ROWS:
                    pe.wait_ge(p_act, of(act_steps, i, "xlT", s))
                    for a, w in enumerate((wq, wk)):
                        for o in range(KB):
                            for k in range(KB):
                                ins = mm(pb[s][0][:, (a * KB + o) * M:(a * KB + o + 1) * M],
                                         w[:, k, o * P:(o + 1) * P], xlT[s][:, k, :], start=(k == 0), stop=(k == KB - 1))
                    ins.then_inc(p_pe, 1)
                for s in ROWS:
                    pe.wait_ge(p_dve, of(dve_steps, i, "qbd", s))
                    for a in range(PAIRS):
                        k, j = a // PB, a % PB
                        ins = mm(pb[s][1][:, a * M:(a + 1) * M],
                                 qbd[s % 2][:, k, 2 * j:2 * j + 2, :].rearrange("p h m -> p (h m)"), qlT[s][:, 1, k, :],
                                 start=True, stop=True)
                    ins.then_inc(p_pe, 1)
                for s in ROWS:
                    pe.wait_ge(p_dve, of(dve_steps, i, "X", s))
                    hold(pe)
                    heads(pb[s][0], X[s], lambda r, a: ident[r, r]).then_inc(p_pe, 1)
                for s in ROWS:
                    pe.wait_ge(p_dve, of(dve_steps, i, "cs", s))
                    for a in range(2):
                        ins = tr(pb[s][1][0:PAIRS, a * P:(a + 1) * P], rc1[s][:, a, :], ident[:, :])
                    ins.then_inc(p_pe, 1)
                for s in ROWS:
                    pe.wait_ge(p_dve, of(dve_steps, i, "gb", s))
                    mm(pb[s][1][:, 0:PAIRS], gb[s][:, :, :].rearrange("p h m -> p (h m)"), ident[0:PAIRS, 0:PAIRS],
                       start=True, stop=True).then_inc(p_pe, 1)

                for it in range(ITERS):
                    for s in ROWS:
                        key = ("ZTlo", s) if it == 0 else ("ZTlo", it - 1, s)
                        pe.wait_ge(p_dve, of(dve_steps, i, *key))
                        product(pb[s][0], XT_bd[s], Z_d[s]).then_inc(p_pe, 1)
                    for s in ROWS:
                        pe.wait_ge(p_dve, of(dve_steps, i, "Sbd", it, s))
                        product(pb[s][1], ST_bd[s], ST_d[s],
                                [(lambda a: ident16[:, :], eye15[:, :]),
                                 (lambda a: ST_bd[s][:, a, 0, :], eye7[:, :]),
                                 (lambda a: ST_bd[s][:, a, 1, :], eye7[:, :])]).then_inc(p_pe, 1)
                    for s in ROWS:
                        pe.wait_ge(p_dve, of(dve_steps, i, "T2lo", it, s))
                        product(pb[s][0], ST_bd[s], ST_d[s],
                                [(lambda a: ident16[:, :], eye13[:, :])]).then_inc(p_pe, 1)
                    for s in ROWS:
                        pe.wait_ge(p_dve, of(dve_steps, i, "T3bd", it, s))
                        if it < ITERS - 1:
                            pe.wait_ge(p_act, of(act_steps, i, "ZTbd", it, s))
                            product(pb[s][1], ZT_bd[s], ST_d[s]).then_inc(p_pe, 1)
                        product(pb[s][0], ST_bd[s], ZT_d[s]).then_inc(p_pe, 1)

            pe.wait_ge(p_act, len(act_steps) * B // GR)
            pe.wait_ge(p_dve, len(dve_steps) * B // GR)

            pe.wait_ge(w16_lo, 3)
            TERMS = [(k, wt, xt) for k in range(KB) for wt, xt in ((0, 0), (0, 1), (1, 0))]

            def stage_R(at, b, c):
                u, n = at["R", c], b * NC + c
                pe.wait_ge(norm_x.applied, n + 1)
                for k in range(KB):
                    pe.wait_ge(bank_drained[k], u.bank)
                    for t in range(NT):
                        ins = tr(bank[k][:, t * P:(t + 1) * P], xhat[c % 2][:, t, k * P:(k + 1) * P], ident[:, :])
                    ins.then_inc(bank_full[k], 1)

            def stage_A(at, b, c):
                u = at["A", c]
                for o in range(KB):
                    pe.wait_ge(bank_drained[o], u.bank)
                for w, dst, drained, n, full in ((0, bank, bank_drained, u.bank, bank_full),
                                                 (1, acc, acc_drained, u.acc, acc_full)):
                    for o in range(KB):
                        pe.wait_ge(drained[o], n)
                        for i, (k, wt, xt) in enumerate(TERMS):
                            ins = mm(dst[o][:, :], w16[:, w, wt, k, o * P:(o + 1) * P], xT[:, xt, k, :],
                                     start=(i == 0), stop=(i == len(TERMS) - 1))
                            if w == 0 and o == 0 and i == 0:
                                ins.then_inc(xhat_read, 1)
                        ins.then_inc(full[o], 1)
                for j in range(2):
                    pe.wait_ge(bank_drained[j], u.bank + 1)
                    for t in range(2):
                        tok = slice((2 * j + t) * P, (2 * j + t + 1) * P)
                        for i, (k, wt, xt) in enumerate(TERMS):
                            ins = mm(bank[j][:, t * A:(t + 1) * A], xT[:, xt, k, tok], w16[:, 2, wt, k, :],
                                     start=(i == 0), stop=(i == len(TERMS) - 1))
                    ins.then_inc(bank_full[j], 1)

            def row_maxima(at, b, c, half):
                u, a0 = at[f"B{half + 1}", c], at["A", c]
                span = slice(c * CH, (c + 1) * CH)
                for k in range(KB):
                    pe.wait_ge(acc_drained[k], a0.acc + 1)
                if c == 0:
                    pe.wait_ge(q_bd_in, 16 * HB * (b + 1))
                for j in (2 * half, 2 * half + 1):
                    pe.wait_ge(wide_drained[j % 2], u.wide)
                    for a in range(2):
                        k, q = (2 * j + a) // PB, (2 * j + a) % PB
                        ins = mm(wide[j % 2][:, a * CH:(a + 1) * CH],
                                 q_bd[:, 0, k, 2 * q:2 * q + 2, :].rearrange("p h m -> p (h m)"), kh[:, k, :],
                                 start=True, stop=True)
                    ins.then_inc(wide_full[j % 2], 1)

            def token_maxima(at, b, c, half):
                u = at[f"C{half + 1}", c]
                for k in range(KB):
                    pe.wait_ge(bank_drained[k], at["A", c].bank + 1)
                if c == 0:
                    pe.wait_ge(kA_bd_in, 16 * HB * (b + 1))
                for t in (2 * half, 2 * half + 1):
                    pe.wait_ge(wide_drained[t % 2], u.wide)
                    tok = slice(c * CH + t * P, c * CH + (t + 1) * P)
                    for k in range(KB):
                        ins = mm(wide[t % 2][:, k * 512:(k + 1) * 512], qh[:, k, tok],
                                 kA_bd[:, 0, k, :, :].rearrange("p h m -> p (h m)"), start=True, stop=True)
                    ins.then_inc(wide_full[t % 2], 1)

            def stage_M(at, b, c):
                u = at["M", 0]
                for j in range(2):
                    pe.wait_ge(bank_drained[j], u.bank)
                    pe.wait_ge(wide_drained[j], u.wide)
                    pe.wait_ge(acc_drained[j], u.acc)
                pe.wait_ge(m3_max, b + 1)
                for k in range(KB):
                    for q in range(PB):
                        a = k * PB + q
                        ins = mm(bank[k][3 * 32:P, q * P:(q + 1) * P], m3m[:, a:a + 1].to_broadcast([P, 32]),
                                 ident[:, :], start=True, stop=True)
                    ins.then_inc(bank_full[k], 1)

            def stage_F(at, b, c):
                u = at["F", 0]
                NTL = NC * NT

                def sums(t):
                    pe.wait_ge(wide_drained[t % 2], u.wide + t // 2 + 1)
                    if t == 0:
                        for j in range(2):
                            pe.wait_ge(acc_drained[j], at["F", 0].acc)
                    first, last = t == 0, t == NTL - 1
                    for q in range(4):
                        ins = mm(acc[1][32 * q:32 * q + 32, 0:256], ones32[:, :], e3[t % 2][:, q * 256:(q + 1) * 256],
                                 start=first, stop=last, skip_group_check=True)
                    if last:
                        ins.then_inc(acc_full[1], 1)
                    for a in range(PAIRS):
                        k, q = a // PB, a % PB
                        ins = mm(acc[0][32 * q:32 * q + 32, k * P:(k + 1) * P], vv[:, t, 32 * a:32 * a + 32],
                                 e3[t % 2][:, a * P:(a + 1) * P], start=(first and k == 0), stop=last,
                                 skip_group_check=True)
                    ins.then_inc(acc_full[0] if last else e3_read, 1)

                if c == 0:
                    for k in range(KB):
                        pe.wait_ge(bank_drained[k], at["M", 0].bank + 1)
                    pe.wait_ge(q_stack_in, 16 * 3 * HB * (b + 1))
                    pe.wait_ge(k_stack_in, 16 * NKS * NC * (b + 1))
                for t in range(c * NT, (c + 1) * NT):
                    pe.wait_ge(wide_drained[t % 2], u.wide + t // 2)
                    tok = slice(t * P, (t + 1) * P)
                    for a in range(PAIRS):
                        ins = mm(wide[t % 2][:, a * P:(a + 1) * P], k_stack[:, a, tok], q_stack[:, a, :],
                                 start=True, stop=True)
                    ins.then_inc(wide_full[t % 2], 1)
                    if t:
                        sums(t - 1)
                if c == NC - 1:
                    sums(NTL - 1)

            def stage_W(at, b, c):
                u, a0 = at["W", 0].bank, at["W", 0].acc
                pe.wait_ge(acc_drained[0], a0 + 1)
                pe.wait_ge(bank_drained[0], u)
                for k in range(KB):
                    ins = tr(bank[0][:, k * P:(k + 1) * P], uT[:, k * P:(k + 1) * P], ident[:, :])
                    if k == 0:
                        ins.then_inc(q_bd_free, 1)
                ins.then_inc(bank_full[0], 1)
                pe.wait_ge(acc_drained[1], a0 + 1)
                pe.wait_ge(bank_drained[1], u)
                for h in range(2):
                    ins = mm(bank[1][:, 0:PAIRS].rearrange("p (q h) -> p h q", h=2)[:, h, :],
                             rs3[:, h * P:(h + 1) * P], ident[:, 0:P:32], start=True, stop=True)
                ins.then_inc(bank_full[1], 1)

            def stage_V(at, b, c):
                u, w = at["V", 0].bank, at["W", 0].bank + 1
                pe.wait_ge(zt_in, 16 * (b + 1))
                pe.wait_ge(bank_drained[0], w)
                for j in range(2):
                    pe.wait_ge(bank_drained[j], u)
                hold(pe)
                for j in range(2):
                    r = slice(j * HALF, (j + 1) * HALF)
                    for a in range(PAIRS):
                        ins = mm(bank[j][r, a * HS:(a + 1) * HS], zt[r, a, :], un[r, a, :], start=True, stop=True)
                    ins.then_inc(bank_full[j], 1)

            def stage_D(at, b, c):
                u = at["D", c]
                for j in range(2):
                    pe.wait_ge(bank_drained[j], u.bank)
                    for t in range(2):
                        ins = tr(bank[j][0:H, t * P:(t + 1) * P], m1[:, c * NT + 2 * j + t, :], ident[:, :])
                    ins.then_inc(bank_full[j], 1)

            def stage_E(at, b, c):
                u = at["E", c]
                if c == 0:
                    pe.wait_ge(kE_bd_in, 16 * 2 * HB * (b + 1))
                for j in range(2):
                    pe.wait_ge(bank_drained[j], at["D", c].bank + 1)
                span = slice(c * CH, (c + 1) * CH)
                for j in range(PAIRS // 2):
                    pe.wait_ge(wide_drained[j % 2], u.wide + j // 2)
                    for i2 in range(2):
                        a = 2 * j + i2
                        k, q = a // PB, a % PB
                        dst = wide[j % 2][:, i2 * CH:(i2 + 1) * CH]
                        kb = [kE_bd[:, e, k, 2 * q:2 * q + 2, :].rearrange("p h m -> p (h m)") for e in range(2)]
                        mm(dst, neg_sel[:, a, :], m1T[:, :], start=True, stop=False)
                        mm(dst, kb[0], qh[:, k, span], start=False, stop=False)
                        mm(dst, kb[0], ql[:, k, span], start=False, stop=False)
                        ins = mm(dst, kb[1], qh[:, k, span], start=False, stop=True)
                    ins.then_inc(wide_full[j % 2], 1)

            def stage_H(at, b, c):
                u, e = at["H", c], at["E", c].wide
                if c == 0:
                    for j in range(2):
                        pe.wait_ge(bank_drained[j], at["V", 0].bank + 1)
                for j in range(PAIRS // 2):
                    pe.wait_ge(wide_drained[j % 2], e + j // 2 + 1)
                    k = 2 * j // PB
                    if j % 2 == 0:
                        pe.wait_ge(bank_drained[k], u.bank)
                        pe.wait_ge(acc_drained[k], u.acc)
                    for a in (2 * j, 2 * j + 1):
                        r = slice(32 * (a % PB), 32 * (a % PB) + 32)
                        s_ = mm(bank[k][r, :], ones_pair[:, :], p1[:, a, :], start=True, stop=True)
                        if a == 0 and c == 0:
                            s_.then_inc(zt_free, 1)
                        if a == 0 and c == NC - 1:
                            s_.then_inc(k_bd_free, 1)
                        o_ = mm(acc[k][r, :], wbd[:, a, :, :].rearrange("p h d -> p (h d)"), p1[:, a, :], start=True,
                                stop=True)
                    if j % 2 == 1:
                        s_.then_inc(bank_full[k], 1)
                        o_.then_inc(acc_full[k], 1)

            def stage_O(at, b, c):
                u, h = at["O", c].bank, at["H", c].acc
                for k in range(KB):
                    pe.wait_ge(acc_drained[k], h + 1)
                for j in range(2):
                    pe.wait_ge(bank_drained[j], u)
                    for t in range(2):
                        dst = bank[j][:, t * A:(t + 1) * A]
                        tok = slice((2 * j + t) * P, (2 * j + t + 1) * P)
                        for k in range(KB):
                            ins = mm(dst, oT[:, k, tok], wo[:, k, :], start=(k == 0), stop=(k == KB - 1))
                    ins.then_inc(bank_full[j], 1)

            def stage_T(at, b, c):
                u, n = at["T", c].bank, b * NC + c
                pe.wait_ge(norm_m.applied, n + 1)
                for k in range(KB):
                    pe.wait_ge(bank_drained[k], u)
                    for t in range(NT):
                        ins = tr(bank[k][:, t * P:(t + 1) * P], x2h[:, t, k * P:(k + 1) * P], ident[:, :])
                    ins.then_inc(bank_full[k], 1)

            def stage_G1(at, b, c):
                u, n = at["G1", c].bank, b * NC + c
                pe.wait_ge(xr_made, n + 1)
                for j in range(2):
                    pe.wait_ge(bank_drained[j], u)
                    for t in range(2):
                        tok = slice((2 * j + t) * P, (2 * j + t + 1) * P)
                        for k in range(KB):
                            ins = mm(bank[j][:, t * A:(t + 1) * A], xrT[:, k, tok], wrT[:, k, :], start=(k == 0),
                                     stop=(k == KB - 1))
                            if j == 0 and t == 0 and k == 0:
                                ins.then_inc(x2h_read, 1)
                    ins.then_inc(bank_full[j], 1)
                pe.wait_ge(xk_made, n + 1)
                dst, full, drained, a = gate_key_banks(at, c)
                for o in range(KB):
                    pe.wait_ge(drained[o], a)
                    for k in range(KB):
                        ins = mm(dst[o][:, :], wkT[:, k, o * P:(o + 1) * P], xkT[:, k, :], start=(k == 0),
                                 stop=(k == KB - 1))
                    ins.then_inc(full[o], 1)

            def stage_G2(at, b, c):
                u, n = at["G2", c].bank, b * NC + c
                pe.wait_ge(ka_made, n + 1)
                for j in range(2):
                    pe.wait_ge(bank_drained[j], u)
                    for t in range(2):
                        tok = slice((2 * j + t) * P, (2 * j + t + 1) * P)
                        for k in range(KB):
                            ins = mm(bank[j][:, t * A:(t + 1) * A], ka[:, k, tok], wvT[:, k, :], start=(k == 0),
                                     stop=(k == KB - 1))
                    ins.then_inc(bank_full[j], 1)

            part2_program(pe, {"R": stage_R, "A": stage_A, "B1": lambda at, b, c: row_maxima(at, b, c, 0),
                               "B2": lambda at, b, c: row_maxima(at, b, c, 1),
                               "C1": lambda at, b, c: token_maxima(at, b, c, 0),
                               "C2": lambda at, b, c: token_maxima(at, b, c, 1), "V": stage_V, "D": stage_D,
                               "M": stage_M, "F": stage_F, "W": stage_W, "E": stage_E, "H": stage_H, "O": stage_O,
                               "T": stage_T, "G1": stage_G1, "G2": stage_G2})


_INS = ["L0_attn_x", "L0_attn_Wk", "L0_attn_Wq", "L0_attn_Wv", "L0_attn_Wo", "L0_attn_bo", "L0_ffn_W_r",
        "L0_ffn_W_k", "L0_ffn_W_v", "L0_ffn_mu_r", "L0_ffn_mu_k"]


def kernel(**inputs):
    import numpy as np
    import concourse.bacc as bacc
    from concourse.bass_utils import run_bass_kernel_spmd

    nc = bacc.Bacc("TRN2", target_bir_lowering=False, num_devices=1)
    arrays, args = {}, []
    for name in _INS:
        a = np.ascontiguousarray(inputs[name])
        arrays[f"in_{name}"] = a
        args.append(nc.dram_tensor(f"in_{name}", a.shape, mybir.dt.from_np(a.dtype), kind="ExternalInput").ap())
    shape = inputs["L0_attn_x"].shape
    args.append(nc.dram_tensor("out", shape, F32, kind="ExternalOutput").ap())
    sandwich(nc, *args)
    return run_bass_kernel_spmd(nc, [arrays], core_ids=[0]).results[0]["out"]
```
